# Optimizing a Trainium2 kernel written in Bass

```python
import numpy as np
import jax
import jax.numpy as jnp

def _softmax(x, axis=-1):
    return jax.nn.softmax(x, axis=axis)

def _gelu(x):
    return jax.nn.gelu(x, approximate=True)

def _silu(x):
    return jax.nn.silu(x)

def _sigmoid(x):
    return jax.nn.sigmoid(x)

def _layernorm(x, axis=-1, eps=1e-05):
    m = jnp.mean(x, axis=axis, keepdims=True)
    v = jnp.var(x, axis=axis, keepdims=True)
    return (x - m) / jnp.sqrt(v + eps)

def _scatter_add(tgt, idx, src, axis=0):
    return tgt.at[idx].add(src)

def _segment_sum(src, seg, n):
    return jax.ops.segment_sum(src, seg, n)
kernel_name = 'mk_gnn_resnorm_d4_gnn_r32_e68bb9'

def setup_inputs(seed: int=0):
    np.random.seed(seed)
    _w = jnp.asarray

    def _rec_inputs():
        import jax
        import jax.numpy as jnp
        _gk = jax.random.key(seed)
        x = -0.000125 + 0.9999 * jax.random.normal(jax.random.fold_in(_gk, 1), (2048, 512), jnp.float32)
        _s = jax.random.randint(jax.random.fold_in(_gk, 2), (16384,), 0, 2048, jnp.int32)
        _d = jax.random.randint(jax.random.fold_in(_gk, 3), (16384,), 0, 2048, jnp.int32)
        _loop = jnp.arange(2048, dtype=jnp.int32)
        src = jnp.concatenate([_s, _d, _loop])
        dst = jnp.concatenate([_d, _s, _loop])
        _o = jnp.argsort(dst, stable=True)
        src = src[_o]
        dst = dst[_o]
        edge_attr_64 = 0.000189758 + 1.00013 * jax.random.normal(jax.random.fold_in(_gk, 13), (34816, 64), jnp.float32)
        edge_weight = jax.random.uniform(jax.random.fold_in(_gk, 15), (34816,), jnp.float32, 0.0, 0.999999)
        return (x, src, dst, edge_attr_64, edge_weight)
    x, src, dst, edge_attr_64, edge_weight = _rec_inputs()

    def _L0_gnn_setup():
        import jax, jax.numpy as jnp
        import numpy as np
        N = 2048
        D = 512
        E = 16384
        T = 5
        BETA = 0.5
        EPS_ORTHO = 1e-05
        EPS_BN = 1e-05

        def ortho_trans(we):
            Zc = we - jnp.mean(we, axis=-1, keepdims=True)
            S = Zc @ Zc.T + EPS_ORTHO * jnp.eye(D, dtype=we.dtype)
            norm_S = jnp.sqrt(jnp.sum(S * S))
            S = S / norm_S
            B = jnp.eye(D, dtype=we.dtype)
            for _ in range(T):
                B3 = B @ B @ B
                B = 1.5 * B - 0.5 * (B3 @ S)
            return B @ Zc / jnp.sqrt(norm_S)
        key = jax.random.key(seed)
        ks = jax.random.split(key, 6)
        stdv = 1.0 / np.sqrt(D)
        return {'x': jax.random.normal(ks[0], (N, D), dtype=jnp.float32), 'edge_src': jax.random.randint(ks[1], (E,), 0, N, dtype=jnp.int32), 'edge_dst': jax.random.randint(ks[2], (E,), 0, N, dtype=jnp.int32), 'edge_val': jax.random.uniform(ks[3], (E,), dtype=jnp.float32), 'weight': jax.random.uniform(ks[4], (D, D), dtype=jnp.float32, minval=-stdv, maxval=stdv), 'self_weight': jax.random.uniform(ks[5], (D, D), dtype=jnp.float32, minval=-stdv, maxval=stdv), 'bn_gamma': jnp.ones((D,), dtype=jnp.float32), 'bn_beta': jnp.zeros((D,), dtype=jnp.float32)}
    _L0_gnn_all = _L0_gnn_setup()
    _L0_gnn_in = {k: v for k, v in _L0_gnn_all.items() if k in ('weight', 'self_weight', 'bn_gamma', 'bn_beta')}
    del _L0_gnn_all

    def _L1_gnn_setup():
        import jax, jax.numpy as jnp
        import numpy as np
        N, D, E = (50000, 512, 12500)
        EPS = 1e-05
        SLOPE = 0.01
        key = jax.random.key(seed)
        k1, k2, k3, k4 = jax.random.split(key, 4)
        x = jax.random.normal(k1, (N, D), dtype=jnp.float32)
        edge_index = jax.random.randint(k2, (2, E), 0, N, dtype=jnp.int64)
        s = 1.0 / np.sqrt(D)
        W_l = jax.random.normal(k3, (D, D), dtype=jnp.float32) * s
        b_l = jnp.zeros((D,), dtype=jnp.float32)
        W_r = jax.random.normal(k4, (D, D), dtype=jnp.float32) * s
        gamma = jnp.ones((D,), dtype=jnp.float32)
        beta = jnp.zeros((D,), dtype=jnp.float32)
        return {'x': x, 'edge_index': edge_index, 'W_l': W_l, 'b_l': b_l, 'W_r': W_r, 'gamma': gamma, 'beta': beta}
    _L1_gnn_all = _L1_gnn_setup()
    _L1_gnn_in = {k: v for k, v in _L1_gnn_all.items() if k in ('W_l', 'b_l', 'W_r', 'gamma', 'beta')}
    del _L1_gnn_all

    def _L2_gnn_setup():
        import jax, jax.numpy as jnp
        import numpy as np
        N_NODES = 50000
        N_EDGES = 25000
        NODE_IN = 512
        EDGE_IN = 64
        HID = 1024
        key = jax.random.key(seed)
        ks = jax.random.split(key, 6)
        x = jax.random.normal(ks[0], (N_NODES, NODE_IN), dtype=jnp.float32)
        edge_index = jax.random.randint(ks[1], (2, N_EDGES), 0, N_NODES, dtype=jnp.int64)
        edge_attr = jax.random.normal(ks[2], (N_EDGES, EDGE_IN), dtype=jnp.float32)
        u = jnp.zeros((1, 16), dtype=jnp.float32)
        batch = jnp.zeros((N_NODES,), dtype=jnp.int64)
        s1 = 1.0 / np.sqrt(NODE_IN + EDGE_IN)
        s2 = 1.0 / np.sqrt(HID)
        W1 = jax.random.normal(ks[3], (NODE_IN + EDGE_IN, HID), dtype=jnp.float32) * s1
        b1 = jnp.zeros((HID,), dtype=jnp.float32)
        W2 = jax.random.normal(ks[4], (HID, NODE_IN), dtype=jnp.float32) * s2
        b2 = jnp.zeros((NODE_IN,), dtype=jnp.float32)
        return {'x': x, 'edge_index': edge_index, 'edge_attr': edge_attr, 'u': u, 'batch': batch, 'W1': W1, 'b1': b1, 'W2': W2, 'b2': b2}
    _L2_gnn_all = _L2_gnn_setup()
    _L2_gnn_in = {k: v for k, v in _L2_gnn_all.items() if k in ('u', 'W1', 'b1', 'W2', 'b2')}
    del _L2_gnn_all

    def _L3_gnn_setup():
        import jax, jax.numpy as jnp
        import numpy as np
        N = 50000
        E = 5000
        D = 512
        H = 512
        NEG_SLOPE = 0.01

        def _cheb_norm(src, dst, n):
            deg = jax.ops.segment_sum(jnp.ones((src.shape[0],), jnp.float32), src, num_segments=n)
            dinv = jnp.where(deg > 0, jax.lax.rsqrt(jnp.maximum(deg, 1.0)), 0.0)
            return -dinv[src] * dinv[dst]

        def _cheb_conv(x, src, dst, norm, W0, W1, b):

            def prop(h):
                return jax.ops.segment_sum(h[src] * norm[:, None], dst, num_segments=x.shape[0])
            out = x @ W0
            tx1 = prop(x)
            out = out + tx1 @ W1
            return out + b

        def _layer_norm(x, gamma, beta, eps=1e-05):
            mu = jnp.mean(x, axis=-1, keepdims=True)
            var = jnp.mean(jnp.square(x - mu), axis=-1, keepdims=True)
            return (x - mu) * jax.lax.rsqrt(var + eps) * gamma + beta
        key = jax.random.key(seed)
        ks = jax.random.split(key, 8)
        s_in = 1.0 / np.sqrt(D)
        s_h = 1.0 / np.sqrt(H)
        x = jax.random.normal(ks[0], (N, D), jnp.float32)
        edge_index = jax.random.randint(ks[1], (2, E), 0, N, dtype=jnp.int64)
        return {'x': x, 'W1_0': jax.random.normal(ks[2], (D, H), jnp.float32) * s_in, 'W1_1': jax.random.normal(ks[3], (D, H), jnp.float32) * s_in, 'b1': jnp.zeros((H,), jnp.float32), 'gamma': jnp.ones((H,), jnp.float32), 'beta': jnp.zeros((H,), jnp.float32), 'W2_0': jax.random.normal(ks[4], (H, H), jnp.float32) * s_h, 'W2_1': jax.random.normal(ks[5], (H, H), jnp.float32) * s_h, 'b2': jnp.zeros((H,), jnp.float32), 'edge_index': edge_index}
    _L3_gnn_all = _L3_gnn_setup()
    _L3_gnn_in = {k: v for k, v in _L3_gnn_all.items() if k in ('W1_0', 'W1_1', 'b1', 'gamma', 'beta', 'W2_0', 'W2_1', 'b2')}
    del _L3_gnn_all
    return {'x': x, 'src': src, 'dst': dst, 'edge_attr_64': edge_attr_64, 'edge_weight': edge_weight, 'L0_gnn_weight': _L0_gnn_in['weight'], 'L0_gnn_self_weight': _L0_gnn_in['self_weight'], 'L0_gnn_bn_gamma': _L0_gnn_in['bn_gamma'], 'L0_gnn_bn_beta': _L0_gnn_in['bn_beta'], 'L1_gnn_W_l': _L1_gnn_in['W_l'], 'L1_gnn_b_l': _L1_gnn_in['b_l'], 'L1_gnn_W_r': _L1_gnn_in['W_r'], 'L1_gnn_gamma': _L1_gnn_in['gamma'], 'L1_gnn_beta': _L1_gnn_in['beta'], 'L2_gnn_u': _L2_gnn_in['u'], 'L2_gnn_W1': _L2_gnn_in['W1'], 'L2_gnn_b1': _L2_gnn_in['b1'], 'L2_gnn_W2': _L2_gnn_in['W2'], 'L2_gnn_b2': _L2_gnn_in['b2'], 'L3_gnn_W1_0': _L3_gnn_in['W1_0'], 'L3_gnn_W1_1': _L3_gnn_in['W1_1'], 'L3_gnn_b1': _L3_gnn_in['b1'], 'L3_gnn_gamma': _L3_gnn_in['gamma'], 'L3_gnn_beta': _L3_gnn_in['beta'], 'L3_gnn_W2_0': _L3_gnn_in['W2_0'], 'L3_gnn_W2_1': _L3_gnn_in['W2_1'], 'L3_gnn_b2': _L3_gnn_in['b2']}

def reference(x, src, dst, edge_attr_64, edge_weight, L0_gnn_weight, L0_gnn_self_weight, L0_gnn_bn_gamma, L0_gnn_bn_beta, L1_gnn_W_l, L1_gnn_b_l, L1_gnn_W_r, L1_gnn_gamma, L1_gnn_beta, L2_gnn_u, L2_gnn_W1, L2_gnn_b1, L2_gnn_W2, L2_gnn_b2, L3_gnn_W1_0, L3_gnn_W1_1, L3_gnn_b1, L3_gnn_gamma, L3_gnn_beta, L3_gnn_W2_0, L3_gnn_W2_1, L3_gnn_b2):
    import jax
    import jax.numpy as jnp

    def _L0_gnn_ref(x, edge_src, edge_dst, edge_val, weight, self_weight, bn_gamma, bn_beta):
        import jax, jax.numpy as jnp
        import numpy as np
        N = 2048
        D = 512
        E = 16384
        T = 5
        BETA = 0.5
        EPS_ORTHO = 1e-05
        EPS_BN = 1e-05

        def ortho_trans(we):
            Zc = we - jnp.mean(we, axis=-1, keepdims=True)
            S = Zc @ Zc.T + EPS_ORTHO * jnp.eye(D, dtype=we.dtype)
            norm_S = jnp.sqrt(jnp.sum(S * S))
            S = S / norm_S
            B = jnp.eye(D, dtype=we.dtype)
            for _ in range(T):
                B3 = B @ B @ B
                B = 1.5 * B - 0.5 * (B3 @ S)
            return B @ Zc / jnp.sqrt(norm_S)
        we = BETA * weight + (1.0 - BETA) * jnp.eye(D, dtype=weight.dtype)
        t = ortho_trans(we)
        support = x @ t
        msgs = edge_val[:, None] * support[edge_src]
        output = jax.ops.segment_sum(msgs, edge_dst, num_segments=N)
        output = output + x @ self_weight
        mean = jnp.mean(output, axis=0)
        var = jnp.mean((output - mean) ** 2, axis=0)
        output = (output - mean) * jax.lax.rsqrt(var + EPS_BN) * bn_gamma + bn_beta
        return jax.nn.relu(output)

    def _L1_gnn_ref(x, edge_index, W_l, b_l, W_r, gamma, beta):
        import jax, jax.numpy as jnp
        import numpy as np
        N, D, E = (50000, 512, 12500)
        EPS = 1e-05
        SLOPE = 0.01
        src, dst = (edge_index[0], edge_index[1])
        n = x.shape[0]
        summed = jax.ops.segment_sum(x[src], dst, num_segments=n)
        deg = jax.ops.segment_sum(jnp.ones((src.shape[0],), x.dtype), dst, num_segments=n)
        agg = summed / jnp.maximum(deg, 1.0)[:, None]
        out = agg @ W_l + b_l + x @ W_r
        mean = out.mean(axis=0)
        var = out.var(axis=0)
        out = (out - mean) * jax.lax.rsqrt(var + EPS) * gamma + beta
        out = jnp.where(out >= 0, out, SLOPE * out)
        out = out + x
        return out

    def _L2_gnn_ref(x, edge_index, edge_attr, u, batch, W1, b1, W2, b2):
        import jax, jax.numpy as jnp
        import numpy as np
        N_NODES = 50000
        N_EDGES = 25000
        NODE_IN = 512
        EDGE_IN = 64
        HID = 1024
        col = edge_index[1]
        summed = jax.ops.segment_sum(edge_attr, col, num_segments=x.shape[0])
        count = jax.ops.segment_sum(jnp.ones((edge_attr.shape[0],), dtype=x.dtype), col, num_segments=x.shape[0])
        agg = summed / jnp.maximum(count, 1.0)[:, None]
        h = jnp.concatenate([x, agg], axis=-1)
        h = jax.nn.relu(h @ W1 + b1)
        return x + h @ W2 + b2

    def _L3_gnn_ref(x, W1_0, W1_1, b1, gamma, beta, W2_0, W2_1, b2, edge_index):
        import jax, jax.numpy as jnp
        import numpy as np
        N = 50000
        E = 5000
        D = 512
        H = 512
        NEG_SLOPE = 0.01

        def _cheb_norm(src, dst, n):
            deg = jax.ops.segment_sum(jnp.ones((src.shape[0],), jnp.float32), src, num_segments=n)
            dinv = jnp.where(deg > 0, jax.lax.rsqrt(jnp.maximum(deg, 1.0)), 0.0)
            return -dinv[src] * dinv[dst]

        def _cheb_conv(x, src, dst, norm, W0, W1, b):

            def prop(h):
                return jax.ops.segment_sum(h[src] * norm[:, None], dst, num_segments=x.shape[0])
            out = x @ W0
            tx1 = prop(x)
            out = out + tx1 @ W1
            return out + b

        def _layer_norm(x, gamma, beta, eps=1e-05):
            mu = jnp.mean(x, axis=-1, keepdims=True)
            var = jnp.mean(jnp.square(x - mu), axis=-1, keepdims=True)
            return (x - mu) * jax.lax.rsqrt(var + eps) * gamma + beta
        src, dst = (edge_index[0], edge_index[1])
        norm = _cheb_norm(src, dst, x.shape[0])
        h = _cheb_conv(x, src, dst, norm, W1_0, W1_1, b1)
        h = _layer_norm(h, gamma, beta)
        h = jnp.where(h >= 0, h, NEG_SLOPE * h)
        out = _cheb_conv(h, src, dst, norm, W2_0, W2_1, b2)
        return out
    edge_index = jnp.stack([src, dst])
    batch0 = jnp.zeros((2048,), jnp.int32)
    x = _layernorm(x + _L0_gnn_ref(x, src, dst, edge_weight, L0_gnn_weight, L0_gnn_self_weight, L0_gnn_bn_gamma, L0_gnn_bn_beta), axis=-1)
    x = _layernorm(x + _L1_gnn_ref(x, edge_index, L1_gnn_W_l, L1_gnn_b_l, L1_gnn_W_r, L1_gnn_gamma, L1_gnn_beta), axis=-1)
    x = _layernorm(x + _L2_gnn_ref(x, edge_index, edge_attr_64, L2_gnn_u, batch0, L2_gnn_W1, L2_gnn_b1, L2_gnn_W2, L2_gnn_b2), axis=-1)
    x = _layernorm(x + _L3_gnn_ref(x, L3_gnn_W1_0, L3_gnn_W1_1, L3_gnn_b1, L3_gnn_gamma, L3_gnn_beta, L3_gnn_W2_0, L3_gnn_W2_1, L3_gnn_b2, edge_index), axis=-1)
    return x

_drawn_inputs = setup_inputs


def setup_inputs(seed=0):
    import zlib

    import numpy as np

    out = dict(_drawn_inputs(seed))
    spreads = {'L0_gnn_bn_gamma': (1.0, 0.2),
     'L0_gnn_bn_beta': (0.0, 0.1),
     'L1_gnn_b_l': (0.0, 0.1),
     'L1_gnn_gamma': (1.0, 0.2),
     'L1_gnn_beta': (0.0, 0.1),
     'L2_gnn_u': (0.0, 0.1),
     'L2_gnn_b1': (0.0, 0.1),
     'L2_gnn_b2': (0.0, 0.1),
     'L3_gnn_b1': (0.0, 0.1),
     'L3_gnn_gamma': (1.0, 0.2),
     'L3_gnn_beta': (0.0, 0.1),
     'L3_gnn_b2': (0.0, 0.1)}
    factors = {}
    for name, (base, spread) in spreads.items():
        noise = np.random.default_rng([zlib.crc32(name.encode()), seed]).standard_normal(out[name].shape)
        drawn = base * np.exp(spread * noise) if base else spread * noise
        out[name] = jnp.asarray(drawn.astype(out[name].dtype))
    for name, factor in factors.items():
        out[name] = (out[name] * factor).astype(out[name].dtype)
    return out
```

```python
from contextlib import contextmanager

import concourse.bass as bass
from concourse import mybir

FP32 = mybir.dt.float32
FP16 = mybir.dt.float16
BF16 = mybir.dt.bfloat16
I32 = mybir.dt.int32
U32 = mybir.dt.uint32
ALU = mybir.AluOpType
ACT = mybir.ActivationFunctionType
AX = mybir.AxisListType

P = 128
N, D, E = 2048, 512, 34816
HID, EDGE_IN = 1024, 64
NT = N // P
FT = D // P
HT = HID // P
CW = 512
NCH = N // CW
TPC = CW // P
EDGE_TILES = E // P
LOT = 16
LOTS = EDGE_TILES // LOT
KEYS = NT * NT
ST = 2 * TPC + 1
STEPS = NCH * NT
SLOT_TILES = STEPS * ST
GROUP = 3
GROUPS = ST // GROUP
OH_RING = 4
REC = 6
AW_RING = 4
ZERO_COLS = 2048
ZERO_DMAS = SLOT_TILES * EDGE_IN // ZERO_COLS
NORM_AFTER_LOTS = 2
EPS = 1e-5
SLOPE = 0.01


class Chain:

    def __init__(self, engine, sem):
        self.engine, self.sem, self.base, self.n = engine, sem, 0, 0

    def link(self, instruction):
        instruction.then_inc(self.sem, 1)
        self.n += 1
        self.engine.wait_ge(self.sem, self.base + self.n)

    def settle(self):
        self.engine.wait_ge(self.sem, self.base + self.n)

    @contextmanager
    def loop(self, times, per):
        start = self.base + self.n
        with self.engine.Fori(0, times) as i:
            self.base, self.n = start + i * per, 0
            yield i
            assert self.n == per, (self.n, per)
        self.base, self.n = start + times * per, 0

    def mark(self, instruction):
        instruction.then_inc(self.sem, 1)
        self.n += 1


def gnn_kernel(nc, x, src, dst, edge_attr, edge_weight, w0, self_w, bn_g, bn_b, wl, bl, wr, g1, be1,
               w1, b1, w2, b2, c1a, c1b, c1bias, ln_g, ln_b, c2a, c2b, c2bias, out, dbg=()):
    rec_table = nc.dram_tensor("rec_table", (P * SLOT_TILES, REC), BF16, kind="Internal").ap()
    attr_table = nc.dram_tensor("attr_table", (P * SLOT_TILES, EDGE_IN), FP32, kind="Internal").ap()
    x_after = [nc.dram_tensor(f"x_after_{i}", (N, D), FP32, kind="ExternalOutput" if dbg else "Internal").ap() for i in range(3)]
    h_parts = nc.dram_tensor("h_parts", (NT, P, 2, D), FP16, kind="Internal").ap()

    KB = 1024
    at = [(nc.sbuf_base + 31) // 32 * 32]

    def region(kb):
        start = at[0]
        at[0] += int(kb * KB)
        assert at[0] <= nc.sbuf_top, at[0] - nc.sbuf_top
        return start

    def sb(name, shape, dt, offset):
        return nc.alloc_sbuf_tensor_at(name, shape, dt, offset=offset)

    r_feat, r_adj, r_node = region(32), region(64), region(32)
    r_wa, r_wb = region(20), region(16)
    r_agg, r_y, r_xr, r_e2, r_cs = region(8), region(8), region(8), region(8), region(8)

    def small(name, shape, dt):
        size = {FP32: 4, I32: 4, U32: 4, FP16: 2, BF16: 2}[dt]
        for n in shape[1:]:
            size *= n
        start = at[0]
        at[0] += (size + 31) // 32 * 32
        assert at[0] <= nc.sbuf_top, at[0] - nc.sbuf_top
        return sb(name, shape, dt, start)

    featT = sb("featT", [P, FT, N], FP32, r_feat)
    adj = sb("adj", [P, NT, N], FP16, r_adj)
    x0 = sb("x0", [P, NT, D], FP32, r_node)
    x_hi = sb("x_hi", [P, NT, D], FP16, r_node)
    x_lo = sb("x_lo", [P, NT, D], FP16, r_node + 16 * KB)
    aggT = sb("aggT", [P, FT, CW], FP32, r_agg)
    ybuf = sb("ybuf", [P, FT, CW], FP32, r_y)
    xr = sb("xr", [P, TPC, D], FP32, r_xr)
    colscale = sb("colscale", [P, N], FP32, r_cs)
    zc, zcT, s_n, b_ping, b_pong, b_sq, b_s, w0_sb = (
        sb(n, [P, 4, D], FP32, r_adj + 8 * KB * i)
        for i, n in enumerate(("zc", "zcT", "s_n", "b_ping", "b_pong", "b_sq", "b_s", "w0_sb")))
    col = EDGE_TILES * 4
    src_i, dst_i, sb_i, db_i, dbl_i, sbl_i = (
        sb(n, [P, EDGE_TILES], I32, r_wa + col * i)
        for i, n in enumerate(("src_i", "dst_i", "sb_i", "db_i", "dbl_i", "sbl_i")))
    key, base, top, third, w_e = (
        sb(n, [P, EDGE_TILES], FP32, r_wa + col * (6 + i))
        for i, n in enumerate(("key", "base", "top", "third", "w_e")))
    rec = sb("rec", [P, EDGE_TILES, REC], BF16, r_wa + col * 11)
    slot = sb("slot", [P, EDGE_TILES], U32, r_wa + 18560)
    tri, no_tri = (sb(n, [P, P], BF16, r_cs + 256 * i) for i, n in enumerate(("tri", "no_tri")))
    eps_i, mhalf_i, threehalf_i = (
        sb(n, [P, P], FP32, r_cs + 512 * (1 + i)) for i, n in enumerate(("eps_i", "mhalf_i", "threehalf_i")))
    ranked_junk = sb("ranked_junk", [P, 2, KEYS], BF16, r_cs + 2048)
    rank = sb("rank", [P, LOT], FP32, r_cs + 3072)
    past1 = sb("past1", [P, LOT], FP32, r_cs + 3072 + 64)
    past2 = sb("past2", [P, LOT], FP32, r_cs + 3072 + 128)
    row = sb("row", [P, LOT], FP32, r_cs + 3072 + 192)
    z_sum = sb("z_sum", [P, 4], FP32, r_cs + 3584)
    sq_sum = sb("sq_sum", [P, 4], FP32, r_cs + 3648)
    s_tot = sb("s_tot", [P, 1], FP32, r_cs + 3680)
    s_rn = sb("s_rn", [P, 1], FP32, r_cs + 3712)
    s_rrn = sb("s_rrn", [P, 1], FP32, r_cs + 3744)
    s_u = sb("s_u", [P, 1], FP32, r_cs + 3776)
    sq_junk = sb("sq_junk", [P, D], FP32, r_cs + 4096)
    key_oh = sb("key_oh", [P, OH_RING, KEYS], BF16, r_cs + 6144)
    pad = sb("pad", [P, SLOT_TILES, REC], BF16, r_e2)
    zeros = sb("zeros", [P, ZERO_COLS], FP32, r_xr)
    oh = sb("oh", [P, OH_RING, GROUP, 5, P], BF16, r_wa)
    recs = sb("recs", [P, SLOT_TILES, REC], BF16, r_xr)
    dst_keep = sb("dst_keep", [P, SLOT_TILES], BF16, r_wa + 17 * KB)
    aw = sb("aw", [P, AW_RING, CW], FP32, r_y)
    stage = sb("stage", [P, 2, LOT, EDGE_IN], FP32, r_e2)
    t_sb = sb("t_sb", [P, 4, D], FP32, r_wb)
    self_sb = sb("self_sb", [P, 4, D], FP32, r_wb + 8 * KB)
    wl_sb = sb("wl_sb", [P, 4, D], FP32, r_wa)
    wr_sb = sb("wr_sb", [P, 4, D], FP32, r_wb)
    at_oh = sb("at_oh", [P, 2, ST, P], FP16, r_wa + 8 * KB)
    at_parts = sb("at_parts", [P, 2, ST, 2, EDGE_IN], FP16, r_wa + 8 * KB + 4608)
    at_in = sb("at_in", [P, 2, ST, EDGE_IN], FP32, r_wb + 8 * KB)
    e2T = sb("e2T", [P, N], FP32, r_e2)
    diag = sb("diag", [P, NT, P], FP32, r_agg)
    w1_sb = sb("w1_sb", [P, 4, HID], FP32, r_wa)
    w1e_sb = sb("w1e_sb", [P, HID], FP32, r_wa + 16 * KB)
    w2_sb = sb("w2_sb", [P, HT, D], FP32, r_wb)
    h_ring = sb("h_ring", [P, 4, CW], FP32, r_agg)
    c1_sb = sb("c1_sb", [P, 2, 4, D], FP32, r_wa)
    lng_sb = sb("lng_sb", [P, D], FP32, r_wa + 16 * KB)
    lnb_sb = sb("lnb_sb", [P, D], FP32, r_wa + 18 * KB)
    c2_sb = sb("c2_sb", [P, 2, 4, D], FP32, r_wb)
    hl = sb("hl", [P, TPC, 2, D], FP16, r_e2)
    ident = small("ident", [P, P], FP32)
    iota = small("iota", [P, KEYS], BF16)
    ones16 = small("ones16", [P, P], FP16)
    ones32 = small("ones32", [P, P], FP32)
    cols = {n: small(n + "_c", [P, 4], FP32) for n in ("bn_g", "bn_b", "bl", "g1", "be1", "b2", "c1bias", "c2bias")}
    b1_sb = small("b1_c", [P, HT], FP32)
    bn_st = small("bn_st", [P, FT, NCH, 6], FP32)
    bn_mv = small("bn_mv", [P, FT, 2], FP32)
    bn_sc = small("bn_sc", [P, FT], FP32)
    bn_bi = small("bn_bi", [P, FT], FP32)
    ln_st = small("ln_st", [P, 6], FP32)
    ln_mv = small("ln_mv", [P, 2, 2], FP32)
    ln_v, ln_r, ln_u = (small(n, [P, 2], FP32) for n in ("ln_v", "ln_r", "ln_u"))
    bn_v, bn_u = (small(n, [P, FT], FP32) for n in ("bn_v", "bn_u"))
    deg = small("deg", [P, NT], FP32)
    dinv = small("dinv", [P, NT], FP32)
    dpos = small("dpos", [P, NT], FP32)
    deg_v, deg_u = (small(n, [P, NT], FP32) for n in ("deg_v", "deg_u"))

    pb = [nc.alloc_psum_tensor(f"bank{i}", [P, 512], FP32) for i in range(8)]
    RANK_BANK, T1_BANK, T2_BANK = 4, 6, 7

    S = {n: nc.alloc_semaphore(n) for n in (
        "ld_edges ld_w0 ld_x ld_self ld_par ld_recs ld_l1 ld_l2 ld_c1 ld_c2 hl_loaded init_rec init_attr "
        "inverse_ready root_ready iota_ready ident_ready tri_ready pads_ready mats_ready dve pool act "
        "key_oh_ready rank_mm ranked slots_ready rec_sent attr_sent0 attr_sent1 stage_ld0 stage_ld1 "
        "zc_ready ortho_full ortho_free squares_ready norm_ready s_scaled oh_ready oh_used adj_evac "
        "agg_step agg_full agg_copied dense_full dense_copied bn_ready z_ready y_ready t1_full t1_free normed t2_full "
        "t2_done split_done deg_full deg_done at_high at_split at_used at_oh_ready e2_done diag_ready diag_full diag_done "
        "h_full h_ready y_step at_in0 at_in1").split()}
    s_xin = [nc.alloc_semaphore(f"xin_{q}") for q in range(TPC)]
    s_xout = [nc.alloc_semaphore(f"xout_{q}") for q in range(TPC)]

    def tile_no(layer, ch, q=0):
        return layer * NT + ch * TPC + q

    def ccols(ch):
        return bass.ds(ch * CW, CW)

    ROOT_NORM, ROOT_NORM2, ROOT_BN, ROOT_DEG = 0, 1, (2, 20), 19
    ROOT_LN = (3, 21, 37, 53, 69)
    LOADS = {0: 0, 1: 1, 2: 2, 4: 3}
    attr_rows = attr_table.rearrange("(p s) r -> p (s r)", p=P)

    with nc.allow_non_contiguous_dma("parameters by column"), nc.Block() as block:

        @block.sync
        def _(sp):
            sp.dma_start(src_i[:], src.rearrange("(p c) -> p c", p=P)).then_inc(S["ld_edges"], 16)
            sp.dma_start(dst_i[:], dst.rearrange("(p c) -> p c", p=P)).then_inc(S["ld_edges"], 16)
            sp.dma_start(w_e[:], edge_weight.rearrange("(p c) -> p c", p=P)).then_inc(S["ld_edges"], 16)
            sp.dma_start(w0_sb[:], w0.rearrange("(i p) d -> p i d", p=P)).then_inc(S["ld_w0"], 16)
            sp.wait_ge(S["pads_ready"], 3)
            sp.dma_start(rec_table.rearrange("(p s) r -> p (s r)", p=P),
                         pad[:].rearrange("p s r -> p (s r)")).then_inc(S["init_rec"], 16)
            sp.dma_start(x0[:], x.rearrange("(t p) d -> p t d", p=P)).then_inc(S["ld_x"], 16)
            sp.dma_start(self_sb[:], self_w.rearrange("(i p) d -> p i d", p=P)).then_inc(S["ld_self"], 16)
            for name, vec in (("bn_g", bn_g), ("bn_b", bn_b), ("bl", bl), ("g1", g1), ("be1", be1),
                              ("b2", b2), ("c1bias", c1bias), ("c2bias", c2bias)):
                sp.dma_start(cols[name][:], vec.rearrange("(f p) -> p f", p=P)).then_inc(S["ld_par"], 16)
            sp.dma_start(b1_sb[:], b1.rearrange("(f p) -> p f", p=P)).then_inc(S["ld_par"], 16)
            for i in range(ZERO_DMAS):
                sp.dma_start(attr_rows[:, i * ZERO_COLS:(i + 1) * ZERO_COLS], zeros[:]).then_inc(S["init_attr"], 16)

            sp.wait_ge(S["init_attr"], 16 * ZERO_DMAS)
            sp.wait_ge(S["rec_sent"], 16 * EDGE_TILES)
            sp.dma_start(recs[:].rearrange("p s r -> p (s r)"),
                         rec_table.rearrange("(p s) r -> p (s r)", p=P)).then_inc(S["ld_recs"], 16)

            def load_x(layer, source, ch, so_far):
                for q in range(TPC):
                    sp.wait_ge(s_xout[q], 16 * (so_far * NCH + 1) + 16 * ch)
                for q in range(TPC):
                    t = tile_no(layer, ch if layer < 4 else 0, q)
                    sp.wait_ge(S["t2_full"], t + 1)
                    sp.wait_ge(S["split_done"], t + 1)
                    sp.dma_start(xr[:, q, :], source[bass.ds((ch * TPC + q) * P, P), :]).then_inc(s_xin[q], 16)

            def store_x(layer, to, ch):
                for q in range(TPC):
                    sp.wait_ge(S["normed"], tile_no(layer, ch, q) + 1)
                    sp.dma_start(to[bass.ds((ch * TPC + q) * P, P), :], xr[:, q, :]).then_inc(s_xout[q], 16)

            def stored(so_far):
                for q in range(TPC):
                    sp.wait_ge(s_xout[q], 16 * (so_far * NCH + 1))

            sp.sem_inc(S["t2_full"], TPC)
            sp.sem_inc(S["split_done"], TPC)
            sp.sem_inc(S["at_split"], 2)
            for q in range(TPC):
                sp.sem_inc(s_xout[q], 16)
            sp.wait_ge(S["oh_ready"], STEPS * GROUPS)
            with sp.Fori(0, NCH) as ch:
                load_x(0, x, ch, 0)
                store_x(0, x_after[0], ch)
            stored(1)
            sp.dma_start(wl_sb[:], wl.rearrange("(i p) d -> p i d", p=P)).then_inc(S["ld_l1"], 16)
            sp.dma_start(wr_sb[:], wr.rearrange("(i p) d -> p i d", p=P)).then_inc(S["ld_l1"], 16)
            for u in range(2):
                sp.wait_ge(S[f"attr_sent{u}"], 16 * LOT * ((LOTS + 1 - u) // 2))
            with sp.Fori(0, STEPS // 2) as i:
                for u in range(2):
                    sp.wait_ge(S["at_split"], i * 2 + u + 1)
                    sp.dma_start(at_in[:, u, :, :].rearrange("p s r -> p (s r)"),
                                 attr_rows[:, bass.ds((i * 2 + u) * (ST * EDGE_IN), ST * EDGE_IN)]
                                 ).then_inc(S[f"at_in{u}"], 16)
            with sp.Fori(0, NCH) as ch:
                load_x(1, x_after[0], ch, 1)
                store_x(1, x_after[1], ch)
            stored(2)
            sp.dma_start(w1_sb[:], w1[0:D, :].rearrange("(i p) d -> p i d", p=P)).then_inc(S["ld_l2"], 16)
            for half in range(2):
                sp.dma_start(w1e_sb[half * EDGE_IN:(half + 1) * EDGE_IN, :], w1[D:D + EDGE_IN, :]).then_inc(S["ld_l2"], 16)
            sp.dma_start(w2_sb[:], w2.rearrange("(i p) d -> p i d", p=P)).then_inc(S["ld_l2"], 16)
            with sp.Fori(0, NCH) as ch:
                load_x(2, x_after[1], ch, 2)
                store_x(2, x_after[2], ch)
            stored(3)
            for i, w in enumerate((c1a, c1b)):
                sp.dma_start(c1_sb[:, i, :, :], w.rearrange("(i p) d -> p i d", p=P)).then_inc(S["ld_c1"], 16)
            for tile, vec in ((lng_sb, ln_g), (lnb_sb, ln_b)):
                sp.dma_start(tile[:], vec.rearrange("(a d) -> a d", a=1).to_broadcast([P, D])).then_inc(S["ld_c1"], 16)
            for i, w in enumerate((c2a, c2b)):
                sp.dma_start(c2_sb[:, i, :, :], w.rearrange("(i p) d -> p i d", p=P)).then_inc(S["ld_c2"], 16)
            with sp.Fori(0, NCH) as ch:
                for q in range(TPC):
                    sp.wait_ge(S["split_done"], tile_no(3, ch, q) + 1 + TPC)
                    sp.dma_start(h_parts[bass.ds(ch * TPC + q, 1), :, :, :].rearrange("a p b d -> (a p) b d"),
                                 hl[:, q, :, :]).then_inc(s_xout[q], 16)
            for q in range(TPC):
                sp.wait_ge(s_xout[q], 16 * (4 * NCH + 1))
            sp.wait_ge(S["agg_full"], 2 * NCH)
            for i, tile in enumerate((x_hi, x_lo)):
                sp.dma_start(tile[:], h_parts[:, :, i, :].rearrange("t p d -> p t d")).then_inc(S["hl_loaded"], 16)
            with sp.Fori(0, NCH) as ch:
                load_x(4, x_after[2], ch, 4)
                store_x(4, out, ch)
            stored(5)

        @block.gpsimd
        def _(pool):
            chain = Chain(pool, S["pool"])
            nc.gpsimd.memset(zeros[:], 0.0).then_inc(S["pads_ready"], 1)
            nc.gpsimd.memset(pad[:], 0.0).then_inc(S["pads_ready"], 1)
            pool.wait_ge(S["pads_ready"], 2)
            nc.gpsimd.memset(pad[:, :, 0:2], -1.0).then_inc(S["pads_ready"], 1)
            nc.gpsimd.iota(iota[:], pattern=[[1, KEYS]], base=0, channel_multiplier=0,
                           allow_small_or_imprecise_dtypes=True).then_inc(S["iota_ready"], 1)
            chain.link(nc.gpsimd.memset(tri[:], 1.0))
            nc.gpsimd.affine_select(out=no_tri[:], in_=tri[:], compare_op=ALU.is_ge, fill=0.0, base=0,
                                    pattern=[[-1, P]], channel_multiplier=1).then_inc(S["tri_ready"], 1)
            pool.wait_ge(S["tri_ready"], 1)
            nc.gpsimd.affine_select(out=tri[:], in_=tri[:], compare_op=ALU.is_gt, fill=0.0, base=0,
                                    pattern=[[1, P]], channel_multiplier=-1).then_inc(S["tri_ready"], 1)
            chain.link(nc.gpsimd.memset(ident[:], 0.0))
            nc.gpsimd.affine_select(out=ident[:], in_=ident[:], compare_op=ALU.not_equal, fill=1.0, base=0,
                                    pattern=[[-1, P]], channel_multiplier=1).then_inc(S["ident_ready"], 1)
            nc.gpsimd.memset(ones16[:], 1.0).then_inc(S["ident_ready"], 1)
            nc.gpsimd.memset(ones32[:], 1.0).then_inc(S["ident_ready"], 1)

            pool.wait_ge(S["init_rec"], 16)
            for c in range(EDGE_TILES):
                if c % LOT == 0:
                    pool.wait_ge(S["slots_ready"], c // LOT + 1)
                pool.indirect_dma_start(out=rec_table, out_offset=bass.IndirectOffsetOnAxis(ap=slot[:, c:c + 1], axis=0),
                                        in_=rec[:, c, :], in_offset=None).then_inc(S["rec_sent"], 16)
            pool.wait_ge(S["init_attr"], 16 * ZERO_DMAS)
            attr_in = edge_attr.rearrange("(p c) r -> p c r", p=P)
            for lot in range(LOTS):
                u = lot % 2
                if lot >= 2:
                    pool.wait_ge(S[f"attr_sent{u}"], 16 * LOT * (lot // 2))
                pool.dma_start(stage[:, u, :, :], attr_in[:, lot * LOT:(lot + 1) * LOT, :]).then_inc(S[f"stage_ld{u}"], 16)
                pool.wait_ge(S[f"stage_ld{u}"], 16 * (lot // 2 + 1))
                for j in range(LOT):
                    c = lot * LOT + j
                    pool.indirect_dma_start(
                        out=attr_table, out_offset=bass.IndirectOffsetOnAxis(ap=slot[:, c:c + 1], axis=0),
                        in_=stage[:, u, j, :], in_offset=None).then_inc(S[f"attr_sent{u}"], 16)

            with pool.Fori(0, STEPS // 2) as i:
                for u in range(2):
                    pool.wait_ge(S["at_high"], i * 2 + u + 1)
                    nc.gpsimd.tensor_tensor(at_parts[:, u, :, 1, :], at_in[:, u, :, :], at_parts[:, u, :, 0, :],
                                            ALU.subtract).then_inc(S["at_split"], 1)

        @block.scalar
        def _(act):
            act.wait_ge(S["ident_ready"], 3)
            for m, v in ((eps_i, EPS), (mhalf_i, -0.5), (threehalf_i, 1.5)):
                nc.scalar.activation(m[:], ident[:], ACT.Copy, scale=v).then_inc(S["mats_ready"], 1)
            done = [0]

            def evac(to, scale=1.0, shape=None):
                n = done[0]
                bank = pb[n % 4][:] if shape is None else pb[n % 4][:].rearrange("p (a b) -> p a b", a=shape)
                act.wait_ge(S["ortho_full"], n + 1)
                done[0] += 1
                nc.scalar.activation(to, bank, ACT.Copy, scale=scale).then_inc(S["ortho_free"], 1)

            def evac_x0(t):
                evac(featT[:, :, t * P:(t + 1) * P], shape=FT)

            for i in range(4):
                evac(zcT[:, :, i * P:(i + 1) * P], shape=4)
            for i in range(4):
                evac(s_n[:, i, :])
                act.wait_ge(S["ortho_free"], done[0])
                nc.scalar.activation(sq_junk[:], s_n[:, i, :], ACT.Square, accum_out=sq_sum[:, i:i + 1]
                                     ).then_inc(S["squares_ready"], 1)
                act.wait_ge(S["squares_ready"], i + 1)
            done[0] += 1

            def root(no, to, inverse):
                act.wait_ge(S["inverse_ready"], no + 1)
                nc.scalar.activation(to, inverse, ACT.Sqrt).then_inc(S["root_ready"], 1)

            root(ROOT_NORM, s_rn[:], s_u[:])
            root(ROOT_NORM2, s_rrn[:], s_rn[:])
            act.wait_ge(S["norm_ready"], 1)
            for i in range(4):
                nc.scalar.activation(s_n[:, i, :], s_n[:, i, :], ACT.Copy, scale=s_rn[:]).then_inc(S["s_scaled"], 1)
            for i in range(4):
                evac(b_ping[:, i, :])
            b = [b_ping, b_pong]
            for it in range(4):
                for i in range(4):
                    evac(b_sq[:, i, :])
                for i in range(2):
                    evac_x0(4 * it + i)
                for i in range(4):
                    evac(b_s[:, i, :], scale=-0.5)
                for i in range(2):
                    evac_x0(4 * it + 2 + i)
                for i in range(4):
                    evac(b[1][:, i, :])
                b.reverse()
            for i in range(4):
                evac(t_sb[:, i, :], scale=s_rrn[:])

            act.sem_inc(S["adj_evac"], 2)
            act.sem_inc(S["agg_step"], AW_RING)
            act.sem_inc(S["dense_copied"], 4)
            act.sem_inc(S["y_step"], 4)
            act.sem_inc(S["h_ready"], 2)
            with act.Fori(0, NCH) as ch:
                for t in range(NT):
                    act.wait_ge(S["oh_used"], ch * (NT * GROUPS) + (t + 1) * GROUPS + OH_RING)
                    act.wait_ge(S["agg_step"], ch * NT + t + 1)
                    nc.scalar.activation(adj[:, t, ccols(ch)], pb[4 + 2 * (t % 2)][:], ACT.Copy)
                    nc.scalar.activation(aw[:, t % AW_RING, :], pb[5 + 2 * (t % 2)][:], ACT.Copy).then_inc(S["adj_evac"], 1)
                act.wait_ge(S["agg_step"], ch * NT + NT + AW_RING)
                for f in range(FT):
                    nc.scalar.activation(aggT[:, f, :], pb[f][:], ACT.Copy).then_inc(S["agg_copied"], 1)
                act.wait_ge(S["dense_full"], ch * FT + FT)
                for f in range(FT):
                    nc.scalar.activation(featT[:, f, ccols(ch)], pb[4 + f][:], ACT.Copy).then_inc(S["dense_copied"], 1)

            def features_to_ybuf(layer, ch, func, ready):
                act.wait_ge(S["t1_full"], tile_no(layer, ch) + TPC)
                for f in range(FT):
                    last = nc.scalar.activation(ybuf[:, f, :], featT[:, f, ccols(ch)], func,
                                                scale=bn_sc[:, f:f + 1], bias=bn_bi[:, f:f + 1])
                last.then_inc(S[ready], 1)

            def transposed_back(layer, ch):
                for q in range(TPC + 1):
                    if q < TPC:
                        root(ch * TPC + ROOT_LN[layer] + q, ln_r[:, q % 2:q % 2 + 1], ln_u[:, q % 2:q % 2 + 1])
                    if q == 0 or layer == 4:
                        continue
                    q -= 1
                    act.wait_ge(S["t2_full"], tile_no(layer, ch, q) + 1 + TPC)
                    nc.scalar.activation(featT[:, :, bass.ds((ch * TPC + q) * P, P)],
                                         pb[T2_BANK][:].rearrange("p (a b) -> p a b", a=FT),
                                         ACT.Copy).then_inc(S["t2_done"], 1)

            act.sem_inc(S["t1_full"], TPC)
            act.sem_inc(S["t2_done"], 1)
            root(ROOT_BN[0], bn_sc[:], bn_u[:])
            act.wait_ge(S["bn_ready"], 1)
            with act.Fori(0, NCH) as ch:
                features_to_ybuf(0, ch, ACT.Relu, "y_ready")
                transposed_back(0, ch)

            root(ROOT_DEG, dinv[:], deg_u[:])
            act.sem_inc(S["at_used"], 2)
            with act.Fori(0, NCH) as ch:
                for t in range(NT):
                    act.wait_ge(S[f"at_in{t % 2}"], ch * (16 * NT // 2) + 16 * (t // 2 + 1))
                    act.wait_ge(S["at_used"], ch * NT + t + 1)
                    nc.scalar.activation(at_parts[:, t % 2, :, 0, :], at_in[:, t % 2, :, :], ACT.Copy).then_inc(S["at_high"], 1)
                act.wait_ge(S["dense_full"], ch * FT + NCH * FT + FT)
                for f in range(FT):
                    nc.scalar.activation(featT[:, f, ccols(ch)], pb[4 + f][:], ACT.Identity,
                                         bias=cols["bl"][:, f:f + 1]).then_inc(S["dense_copied"], 1)
            root(ROOT_BN[1], bn_sc[:], bn_u[:])
            act.wait_ge(S["bn_ready"], 2)
            with act.Fori(0, NCH) as ch:
                features_to_ybuf(1, ch, ACT.Identity, "z_ready")
                transposed_back(1, ch)

            with act.Fori(0, NCH) as ch:
                for i in range(HT):
                    act.wait_ge(S["h_full"], ch * HT + i + 1)
                    act.wait_ge(S["y_step"], ch * HT + i + 1)
                    nc.scalar.activation(h_ring[:, i % 4, :], pb[4 + i % 2][:], ACT.Relu,
                                         bias=b1_sb[:, i:i + 1]).then_inc(S["h_ready"], 1)
                act.wait_ge(S["y_step"], ch * HT + HT + 4)
                act.wait_ge(S["t1_full"], tile_no(2, ch) + TPC)
                for f in range(FT):
                    last = nc.scalar.activation(ybuf[:, f, :], pb[f][:], ACT.Identity, bias=cols["b2"][:, f:f + 1])
                last.then_inc(S["y_ready"], 1)
                transposed_back(2, ch)

            for layer, bias in ((3, "c1bias"), (4, "c2bias")):
                with act.Fori(0, NCH) as ch:
                    act.wait_ge(S["t1_full"], tile_no(layer, ch) + TPC)
                    for f in range(FT):
                        act.wait_ge(S["dense_full"], (layer - 1) * NCH * FT + ch * FT + f + 1)
                        last = nc.scalar.activation(ybuf[:, f, :], pb[4 + f % 2][:], ACT.Identity,
                                                    bias=cols[bias][:, f:f + 1]).then_inc(S["dense_copied"], 1)
                    act.wait_ge(S["dense_copied"], (layer - 1) * NCH * FT + ch * FT + FT + 4)
                    act.sem_inc(S["y_ready"], 1)
                    transposed_back(layer, ch)

        @block.vector
        def _(dve):
            chain = Chain(dve, S["dve"])
            V = nc.vector

            def invert(no, v, u):
                chain.link(V.reciprocal(u, v))
                dve.sem_inc(S["inverse_ready"], 1)

            def inverse_root(no, v, u, r):
                dve.wait_ge(S["root_ready"], no + 1)
                chain.link(V.tensor_tensor(u, r, r, ALU.mult))
                chain.link(V.tensor_tensor(u, u, v, ALU.mult))
                chain.link(V.tensor_scalar(u, u, -0.5, 1.5, ALU.mult, ALU.add))
                chain.link(V.tensor_tensor(r, r, u, ALU.mult))

            dve.wait_ge(S["ld_w0"], 16)
            dve.wait_ge(S["ident_ready"], 3)
            chain.link(V.tensor_scalar(w0_sb[:], w0_sb[:], 0.5, None, ALU.mult))
            for i in range(4):
                block_i = w0_sb[:, i, i * P:(i + 1) * P]
                chain.link(V.scalar_tensor_tensor(block_i, ident[:], 0.5, block_i, ALU.mult, ALU.add))
            chain.link(V.tensor_reduce(z_sum[:], w0_sb[:], AX.X, ALU.add))
            chain.link(V.tensor_scalar(z_sum[:], z_sum[:], 1.0 / D, None, ALU.mult))
            for i in range(4):
                V.tensor_scalar(zc[:, i, :], w0_sb[:, i, :], z_sum[:, i:i + 1], None, ALU.subtract
                                ).then_inc(S["zc_ready"], 1)

            dve.wait_ge(S["ld_edges"], 48)
            chain.mark(V.tensor_scalar(sb_i[:], src_i[:], 7, None, ALU.logical_shift_right))
            chain.link(V.tensor_scalar(db_i[:], dst_i[:], 7, None, ALU.logical_shift_right))
            chain.mark(V.tensor_scalar(sbl_i[:], sb_i[:], TPC - 1, None, ALU.bitwise_and))
            chain.mark(V.tensor_scalar(dbl_i[:], db_i[:], TPC - 1, None, ALU.bitwise_and))
            chain.mark(V.tensor_scalar(src_i[:], src_i[:], P - 1, None, ALU.bitwise_and))
            chain.link(V.tensor_scalar(dst_i[:], dst_i[:], P - 1, None, ALU.bitwise_and))
            chain.mark(V.tensor_copy(rec[:, :, 0], src_i[:]))
            chain.mark(V.tensor_copy(rec[:, :, 1], dst_i[:]))
            chain.mark(V.scalar_tensor_tensor(key[:], db_i[:], float(NT), sb_i[:], ALU.mult, ALU.add))
            chain.link(V.tensor_scalar(base[:], dbl_i[:], 2.0 - ST * NT / TPC, None, ALU.mult))
            chain.link(V.scalar_tensor_tensor(base[:], db_i[:], ST * NT / TPC, base[:], ALU.mult, ALU.add))
            chain.link(V.scalar_tensor_tensor(base[:], sb_i[:], float(ST), base[:], ALU.mult, ALU.add))
            chain.mark(V.tensor_tensor(top[:], sbl_i[:], dbl_i[:], ALU.is_equal))
            chain.link(V.tensor_scalar(third[:], dbl_i[:], -2.0, float(2 * TPC - 1 - P * SLOT_TILES), ALU.mult, ALU.add))
            chain.link(V.tensor_scalar(top[:], top[:], float(P), float(2 * P - 1), ALU.mult, ALU.add))
            for k in range(3):
                chain.link(V.tensor_copy(rec[:, :, 2 + k], w_e[:]))
                if k < 2:
                    chain.link(V.tensor_tensor(w_e[:], w_e[:], rec[:, :, 2 + k], ALU.subtract))
            chain.mark(V.memset(rec[:, :, 5], 0.0))
            chain.link(V.memset(key_oh[:], 0.0))

            dve.wait_ge(S["iota_ready"], 1)
            dve.sem_inc(S["ranked"], 2)
            top2 = top[:].rearrange("p (c two) -> p c two", two=2)
            rank2 = rank[:].rearrange("p (c two) -> p c two", two=2)

            def rank_lots(first, count):
                with chain.loop(count, 7) as i:
                    c0 = i * LOT + first * LOT

                    def extract(j):
                        dve.wait_ge(S["rank_mm"], c0 + j + 1)
                        V.tensor_tensor_reduce(out=ranked_junk[:, j % 2, :], in0=pb[RANK_BANK + j % 2][:, 0:KEYS],
                                               in1=key_oh[:, j % OH_RING, :], scale=1.0, scalar=0.0,
                                               op0=ALU.mult, op1=ALU.add, accum_out=rank[:, j:j + 1]
                                               ).then_inc(S["ranked"], 1)

                    for j in range(LOT):
                        V.tensor_scalar(key_oh[:, j % OH_RING, :], iota[:], key[:, bass.ds(c0 + j, 1)], None,
                                        ALU.is_equal).then_inc(S["key_oh_ready"], 1)
                        if j >= 1:
                            extract(j - 1)
                    extract(LOT - 1)
                    dve.wait_ge(S["ranked"], c0 + LOT + 2)
                    lot = bass.ds(c0, LOT)
                    chain.link(V.tensor_tensor(rank2[:, :, 1], top2[:, bass.ds(i * (LOT // 2) + first * (LOT // 2), LOT // 2), 1],
                                               rank2[:, :, 1], ALU.subtract))
                    chain.mark(V.tensor_scalar(past1[:], rank[:], float(P), float(1 - P * SLOT_TILES), ALU.is_ge, ALU.mult))
                    chain.mark(V.scalar_tensor_tensor(past2[:], rank[:], float(2 * P), third[:, lot], ALU.is_ge, ALU.mult))
                    chain.link(V.scalar_tensor_tensor(row[:], rank[:], float(SLOT_TILES), base[:, lot], ALU.mult, ALU.add))
                    chain.link(V.tensor_tensor(row[:], row[:], past1[:], ALU.add))
                    chain.link(V.tensor_tensor(row[:], row[:], past2[:], ALU.add))
                    chain.link(V.tensor_scalar(slot[:, lot], row[:], 0.0, float(P * SLOT_TILES - 1), ALU.max, ALU.min))
                    dve.sem_inc(S["slots_ready"], 1)

            rank_lots(0, NORM_AFTER_LOTS)
            dve.wait_ge(S["ortho_full"], 9)
            chain.link(V.tensor_reduce(s_tot[:], pb[0][:, 0:4], AX.X, ALU.add))
            dve.sem_inc(S["ortho_free"], 1)
            invert(ROOT_NORM, s_tot[:], s_u[:])
            inverse_root(ROOT_NORM, s_tot[:], s_u[:], s_rn[:])
            chain.link(V.tensor_tensor(s_tot[:], s_tot[:], s_rn[:], ALU.mult))
            dve.sem_inc(S["inverse_ready"], 1)
            inverse_root(ROOT_NORM2, s_tot[:], s_u[:], s_rrn[:])
            dve.sem_inc(S["norm_ready"], 1)
            rank_lots(NORM_AFTER_LOTS, LOTS - NORM_AFTER_LOTS)

            dve.wait_ge(S["ld_recs"], 16)
            chain.link(V.tensor_copy(dst_keep[:], recs[:, :, 1]))
            dve.sem_inc(S["oh_used"], OH_RING)
            with dve.Fori(0, NCH) as ch:
                for g in range(NT * GROUPS):
                    dve.wait_ge(S["oh_used"], ch * (NT * GROUPS) + g + 1)
                    for i in range(GROUP):
                        s = bass.ds(ch * (NT * ST) + g * GROUP + i, 1)
                        V.tensor_scalar(oh[:, g % OH_RING, i, 0, :], iota[:, 0:P], recs[:, s, 0], None, ALU.is_equal)
                        V.tensor_scalar(oh[:, g % OH_RING, i, 1, :], iota[:, 0:P], recs[:, s, 1], None, ALU.is_equal)
                        for k in range(3):
                            last = V.tensor_scalar(oh[:, g % OH_RING, i, 2 + k, :], iota[:, 0:P], recs[:, s, 1],
                                                   recs[:, s, 2 + k], ALU.is_equal, ALU.mult)
                    last.then_inc(S["oh_ready"], 1)

            def batch_norm(no, gamma, beta, copied):
                dve.wait_ge(S["dense_copied"], copied)
                for f in range(FT):
                    for ch in range(NCH):
                        chain.mark(V.bn_stats(bn_st[:, f, ch, :], featT[:, f, ch * CW:(ch + 1) * CW]))
                chain.settle()
                for f in range(FT):
                    chain.link(V.bn_aggr(bn_mv[:, f, :], bn_st[:, f, :, :]))
                chain.link(V.tensor_scalar(bn_v[:], bn_mv[:, :, 1], EPS, None, ALU.add))
                invert(no, bn_v[:], bn_u[:])
                inverse_root(no, bn_v[:], bn_u[:], bn_sc[:])
                chain.link(V.tensor_tensor(bn_sc[:], bn_sc[:], cols[gamma][:], ALU.mult))
                chain.link(V.scalar_tensor_tensor(bn_bi[:], bn_mv[:, :, 0], -1.0, bn_sc[:], ALU.mult, ALU.mult))
                chain.link(V.tensor_tensor(bn_bi[:], bn_bi[:], cols[beta][:], ALU.add))
                dve.sem_inc(S["bn_ready"], 1)

            def post(layer, ch):

                def residual(q):
                    t = tile_no(layer, ch, q)
                    x_q, z, u = xr[:, q, :], pb[T1_BANK][:], q % 2
                    dve.wait_ge(S["t1_full"], t + 1 + TPC)
                    if layer == 3:
                        dve.wait_ge(S["t2_full"], t + 1)
                        dve.wait_ge(s_xout[q], 16 * (3 * NCH + 1))
                        chain.link(V.tensor_copy(x_q, z))
                    else:
                        dve.wait_ge(s_xin[q], 16 * (LOADS[layer] * NCH + 1) + ch * 16)
                        if layer in (1, 2):
                            chain.link(V.scalar_tensor_tensor(x_q, x_q, 2.0, z, ALU.mult, ALU.add))
                        else:
                            chain.link(V.tensor_tensor(x_q, x_q, z, ALU.add))
                    chain.link(V.bn_stats(ln_st[:], x_q))
                    dve.sem_inc(S["t1_free"], 1)
                    chain.link(V.bn_aggr(ln_mv[:, u, :], ln_st[:]))
                    chain.link(V.tensor_scalar(ln_v[:, u:u + 1], ln_mv[:, u, 1:2], EPS, None, ALU.add))
                    invert(None, ln_v[:, u:u + 1], ln_u[:, u:u + 1])

                def normed(q):
                    nt = bass.ds(ch * TPC + q, 1)
                    x_q, u = xr[:, q, :], q % 2
                    inverse_root(ch * TPC + ROOT_LN[layer] + q, ln_v[:, u:u + 1], ln_u[:, u:u + 1], ln_r[:, u:u + 1])
                    chain.link(V.tensor_scalar(x_q, x_q, ln_mv[:, u, 0:1], ln_r[:, u:u + 1], ALU.subtract, ALU.mult))
                    if layer == 3:
                        chain.link(V.tensor_tensor(x_q, x_q, lng_sb[:], ALU.mult))
                        chain.link(V.tensor_tensor(x_q, x_q, lnb_sb[:], ALU.add))
                        chain.link(V.scalar_tensor_tensor(x_q, x_q, SLOPE, x_q, ALU.mult, ALU.max))
                    dve.sem_inc(S["normed"], 1)
                    if layer in (0, 2):
                        hi, lo = (part[:, nt, :].rearrange("p a d -> p (a d)") for part in (x_hi, x_lo))
                    elif layer == 3:
                        hi, lo = hl[:, q, 0, :], hl[:, q, 1, :]
                        dve.wait_ge(s_xout[q], 16 * (3 * NCH + 1) + ch * 16)
                    if layer == 0:
                        chain.link(V.tensor_copy(hi, x_q))
                        chain.link(V.tensor_tensor(lo, x_q, hi, ALU.subtract))
                    elif layer in (2, 3):
                        chain.link(V.tensor_scalar(hi, x_q, dinv[:, nt], None, ALU.mult))
                        chain.link(V.scalar_tensor_tensor(lo, x_q, dinv[:, nt], hi, ALU.mult, ALU.subtract))
                    dve.sem_inc(S["split_done"], 1)

                if layer == 1:
                    dve.wait_ge(S["z_ready"], ch + 1)
                    for f in range(FT):
                        last = V.scalar_tensor_tensor(ybuf[:, f, :], ybuf[:, f, :], SLOPE, ybuf[:, f, :], ALU.mult, ALU.max)
                    last.then_inc(S["y_ready"], 1)
                for q in range(TPC):
                    residual(q)
                    if q >= 1:
                        normed(q - 1)
                normed(TPC - 1)

            dve.sem_inc(S["t1_free"], 1)
            dve.wait_ge(S["ld_par"], 16 * 9)
            batch_norm(ROOT_BN[0], "bn_g", "bn_b", 4 + NCH * FT)
            with chain.loop(NCH, 12 * TPC) as ch:
                post(0, ch)

            for ch in range(NCH):
                dve.wait_ge(S["deg_full"], ch + 1)
                chain.link(V.tensor_scalar(colscale[:, ch * CW:(ch + 1) * CW], pb[ch][:], 1.0, None, ALU.max))
                dve.sem_inc(S["deg_done"], 1)
                chain.link(V.reciprocal(colscale[:, ch * CW:(ch + 1) * CW], colscale[:, ch * CW:(ch + 1) * CW]))
            for t in range(NT):
                chain.link(V.tensor_reduce(deg[:, t:t + 1], adj[:, t, :], AX.X, ALU.add))
            chain.mark(V.tensor_scalar(dpos[:], deg[:], 0.0, None, ALU.is_gt))
            chain.link(V.tensor_scalar(deg_v[:], deg[:], 1.0, None, ALU.max))
            invert(ROOT_DEG, deg_v[:], deg_u[:])
            inverse_root(ROOT_DEG, deg_v[:], deg_u[:], dinv[:])
            chain.link(V.tensor_tensor(dinv[:], dinv[:], dpos[:], ALU.mult))

            def aggregated(agg_no, dense_no, ch):
                dve.wait_ge(S["agg_full"], ch + agg_no + 1)
                dve.wait_ge(S["dense_full"], ch * FT + dense_no)
                for f in range(FT):
                    V.tensor_tensor(aggT[:, f, :], pb[f][:], colscale[:, ccols(ch)], ALU.mult).then_inc(S["agg_copied"], 1)

            with dve.Fori(0, NCH) as ch:
                aggregated(0, NCH * FT, ch)
                for t in range(NT):
                    dve.wait_ge(S["at_used"], ch * NT + t + 1)
                    for i in range(ST):
                        last = V.tensor_scalar(at_oh[:, t % 2, i, :], iota[:, 0:P],
                                               dst_keep[:, bass.ds(ch * (NT * ST) + t * ST + i, 1)], None, ALU.is_equal)
                    last.then_inc(S["at_oh_ready"], 1)
                dve.wait_ge(S["at_used"], ch * NT + NT + 2)
                V.tensor_tensor(e2T[:, ccols(ch)], pb[4][:], colscale[:, ccols(ch)], ALU.mult).then_inc(S["e2_done"], 1)
            dve.wait_ge(S["dense_full"], 2 * NCH * FT)
            dve.wait_ge(S["e2_done"], NCH)
            for t in range(NT):
                V.tensor_scalar(diag[:, t, :], ident[:], dinv[:, t:t + 1], -1.0, ALU.mult, ALU.mult
                                ).then_inc(S["diag_ready"], 1)
            batch_norm(ROOT_BN[1], "g1", "be1", 4 + 2 * NCH * FT)
            dve.wait_ge(S["diag_full"], 1)
            for ch in range(NCH):
                V.tensor_copy(colscale[:, ch * CW:(ch + 1) * CW], pb[ch][:]).then_inc(S["diag_done"], 1)
            with chain.loop(NCH, 10 * TPC) as ch:
                post(1, ch)
            with chain.loop(NCH, 12 * TPC) as ch:
                post(2, ch)
            dve.wait_ge(S["diag_done"], NCH)
            dve.wait_ge(S["ld_c1"], 16 * 4)
            with chain.loop(NCH, 15 * TPC) as ch:
                aggregated(NCH, 2 * NCH * FT, ch)
                post(3, ch)
            with chain.loop(NCH, 10 * TPC) as ch:
                aggregated(2 * NCH, 3 * NCH * FT, ch)
                post(4, ch)

        @block.tensor
        def _(pe):
            mm, tp = nc.tensor.matmul, nc.tensor.transpose
            pieces, ranks = [0], [0]
            PIECES = 4 + 4 + 1 + 4 + 4 * (12 + 4) + 4

            def ranks_up_to(limit):
                while ranks[0] < min(limit, EDGE_TILES):
                    c = ranks[0]
                    ranks[0] += 1
                    bank = pb[RANK_BANK + c % 2][:, 0:KEYS]
                    pe.wait_ge(S["key_oh_ready"], c + 1)
                    pe.wait_ge(S["ranked"], c + 1)
                    mm(bank, no_tri[:], key_oh[:, (c + 2) % OH_RING, :], start=(c < 2), stop=True, skip_group_check=True)
                    mm(bank, tri[:], key_oh[:, c % OH_RING, :], start=False, stop=True,
                       skip_group_check=True).then_inc(S["rank_mm"], 1)

            def piece(products, needs=0):
                n = pieces[0]
                pieces[0] += 1
                if max(n - 3, needs) > 0:
                    pe.wait_ge(S["ortho_free"], max(n - 3, needs))
                products(pb[n % 4]).then_inc(S["ortho_full"], 1)
                lots = EDGE_TILES * (n + 1) // (PIECES - 4)
                ranks_up_to(min(lots, NORM_AFTER_LOTS * LOT) if n <= 8 else lots)

            def transposes(blocks):
                def go(bank):
                    for k, b in enumerate(blocks):
                        last = tp(bank[:, k * P:(k + 1) * P], b, ident[:])
                    return last
                return go

            def product(lhs, rhs, i, extra=None):
                def go(bank):
                    if extra is not None:
                        mm(bank[:], extra[0][:], extra[1][:, i, :], start=True, stop=False)
                    for k in range(4):
                        last = mm(bank[:], lhs[:, k, i * P:(i + 1) * P], rhs[:, k, :],
                                  start=(k == 0 and extra is None), stop=(k == 3))
                    return last
                return go

            def x0_transposes(t):
                piece(transposes([x0[:, t, f * P:(f + 1) * P] for f in range(FT)]))

            pe.wait_ge(S["ident_ready"], 3)
            pe.wait_ge(S["mats_ready"], 3)
            pe.wait_ge(S["tri_ready"], 2)
            pe.wait_ge(S["zc_ready"], 4)
            for i in range(4):
                piece(transposes([zc[:, i, k * P:(k + 1) * P] for k in range(4)]))

            def gram(i):
                def go(bank):
                    product(zcT, zcT, i)(bank)
                    return mm(bank[:, i * P:(i + 1) * P], eps_i[:], ident[:], start=False, stop=True, skip_group_check=True)
                return go

            for i in range(4):
                piece(gram(i), needs=4)
            pe.wait_ge(S["squares_ready"], 4)
            piece(lambda bank: mm(bank[:, 0:4], ones32[:], sq_sum[:], start=True, stop=True), needs=8)
            ranks_up_to(NORM_AFTER_LOTS * LOT)
            pe.wait_ge(S["s_scaled"], 4)
            n = pieces[0]

            def first_b(i):
                def go(bank):
                    mm(bank[:], mhalf_i[:], s_n[:, i, :], start=True, stop=True)
                    return mm(bank[:, i * P:(i + 1) * P], threehalf_i[:], ident[:], start=False, stop=True, skip_group_check=True)
                return go

            for i in range(4):
                piece(first_b(i))
            pe.wait_ge(S["ld_x"], 16)
            b = [b_ping, b_pong]
            for it in range(4):
                n = pieces[0]
                for i in range(4):
                    piece(product(b[0], b[0], i), needs=n)
                for i in range(2):
                    x0_transposes(4 * it + i)
                for i in range(4):
                    piece(product(b[0], s_n, i))
                for i in range(2):
                    x0_transposes(4 * it + 2 + i)
                n = pieces[0]
                for i in range(4):
                    piece(product(b_sq, b_s, i, extra=(threehalf_i, b[0])), needs=n - 2)
                b.reverse()
            n = pieces[0]
            for i in range(4):
                piece(product(b[0], zc, i), needs=n)
            assert pieces[0] == PIECES
            ranks_up_to(EDGE_TILES)

            pe.wait_ge(S["ortho_free"], PIECES)
            pe.wait_ge(S["ld_self"], 16)

            def aggregate_x0(ch, t):
                pe.wait_ge(S["adj_evac"], ch * NT + t + 1 + 2)
                for f in range(FT):
                    last = mm(pb[f][:], x0[:, t, f * P:(f + 1) * P], aw[:, t % AW_RING, :], start=(t == 0), stop=(t == NT - 1))
                last.then_inc(S["agg_step"], 1)

            def dense(bank, pairs, f):
                n = 0
                for w, feat in pairs:
                    for k in range(FT):
                        last = mm(bank[:], w[:, k, f * P:(f + 1) * P], feat(k), start=(n == 0), stop=(n == 2 * FT - 1))
                        n += 1
                last.then_inc(S["dense_full"], 1)

            pe.wait_ge(S["ranked"], EDGE_TILES + 2)
            with pe.Fori(0, NCH) as ch:
                pe.wait_ge(S["dense_copied"], ch * FT + 4)
                for t in range(NT):
                    pe.wait_ge(S["adj_evac"], ch * NT + t + 1)
                    counts, weights = pb[4 + 2 * (t % 2)], pb[5 + 2 * (t % 2)]
                    for s in range(ST):
                        g = t * GROUPS + s // GROUP
                        if s % GROUP == 0:
                            pe.wait_ge(S["oh_ready"], ch * (NT * GROUPS) + g + 1)
                        rows = oh[:, g % OH_RING, s % GROUP, :, :]
                        block_cols = s // 2 if s < 2 * TPC else t % TPC
                        c = slice(block_cols * P, (block_cols + 1) * P)
                        mm(counts[:, c], rows[:, 0, :], rows[:, 1, :], start=(s == 0), stop=True, skip_group_check=True)
                        for k in range(3):
                            last = mm(weights[:, c], rows[:, 0, :], rows[:, 2 + k, :], start=(s == 0 and k == 0),
                                      stop=True, skip_group_check=True)
                        if s % GROUP == GROUP - 1:
                            last.then_inc(S["oh_used"], 1)
                    if t >= 1:
                        aggregate_x0(ch, t - 1)
                aggregate_x0(ch, NT - 1)
                pe.wait_ge(S["agg_copied"], ch * FT + FT)
                pe.wait_ge(S["adj_evac"], ch * NT + NT + 2)
                for f in range(FT):
                    dense(pb[4 + f], ((t_sb, lambda k: aggT[:, k, :]), (self_sb, lambda k: featT[:, k, ccols(ch)])), f)

            for ch in range(NCH):
                for t in range(NT):
                    last = mm(pb[ch][:], ones16[:], adj[:, t, ch * CW:(ch + 1) * CW], start=(t == 0), stop=(t == NT - 1))
                last.then_inc(S["deg_full"], 1)

            def post(layer, ch):
                pe.wait_ge(S["y_ready"], ch + layer * NCH + 1)

                def there(q):
                    pe.wait_ge(S["t1_free"], tile_no(layer, ch, q) + 1)
                    for f in range(FT):
                        last = tp(pb[T1_BANK][:, f * P:(f + 1) * P], ybuf[:, f, q * P:(q + 1) * P], ident[:])
                    last.then_inc(S["t1_full"], 1)

                def back(q):
                    pe.wait_ge(S["normed"], tile_no(layer, ch, q) + 1)
                    pe.wait_ge(S["t2_done"], tile_no(layer, ch, q) + 1)
                    for f in range(FT):
                        last = tp(pb[T2_BANK][:, f * P:(f + 1) * P], xr[:, q, f * P:(f + 1) * P], ident[:])
                    last.then_inc(S["t2_full"], 1)

                for q in range(TPC):
                    there(q)
                    if q >= 1 and layer < 4:
                        back(q - 1)
                if layer < 4:
                    back(TPC - 1)

            pe.wait_ge(S["dense_copied"], 4 + NCH * FT)
            with pe.Fori(0, NCH) as ch:
                post(0, ch)

            def aggregate(ch, copied):
                pe.wait_ge(S["agg_copied"], ch * FT + copied)
                for t in range(NT):
                    for f in range(FT):
                        mm(pb[f][:], x_hi[:, t, f * P:(f + 1) * P], adj[:, t, ccols(ch)], start=(t == 0), stop=False)
                        last = mm(pb[f][:], x_lo[:, t, f * P:(f + 1) * P], adj[:, t, ccols(ch)], start=False, stop=(t == NT - 1))
                last.then_inc(S["agg_full"], 1)

            pe.wait_ge(S["deg_done"], NCH)
            pe.wait_ge(S["split_done"], NT + TPC)
            pe.wait_ge(S["ld_l1"], 32)
            pe.wait_ge(S["t2_done"], NT + 1)
            with pe.Fori(0, NCH) as ch:
                aggregate(ch, NCH * FT)
                pe.wait_ge(S["dense_copied"], ch * FT + NCH * FT + 4)
                for t in range(NT):
                    pe.wait_ge(S["at_split"], ch * NT + t + 1 + 2)
                    pe.wait_ge(S["at_oh_ready"], ch * NT + t + 1)
                    for s in range(ST):
                        block_cols = s // 2 if s < 2 * TPC else t % TPC
                        last = mm(pb[4][:, block_cols * P:(block_cols + 1) * P],
                                  at_parts[:, t % 2, s, :, :].rearrange("p a b -> p (a b)"), at_oh[:, t % 2, s, :],
                                  start=(t == 0 and s == 0), stop=True, skip_group_check=True)
                    last.then_inc(S["at_used"], 1)
                pe.wait_ge(S["agg_copied"], ch * FT + NCH * FT + FT)
                pe.wait_ge(S["e2_done"], ch + 1)
                for f in range(FT):
                    dense(pb[4 + f], ((wl_sb, lambda k: aggT[:, k, :]), (wr_sb, lambda k: featT[:, k, ccols(ch)])), f)
            for ch in range(NCH):
                pe.wait_ge(S["diag_ready"], (ch + 1) * TPC)
                for q in range(TPC):
                    last = mm(pb[ch][:, q * P:(q + 1) * P], ones32[:], diag[:, ch * TPC + q, :],
                              start=True, stop=True, skip_group_check=True)
            last.then_inc(S["diag_full"], 1)
            pe.wait_ge(S["dense_copied"], 4 + 2 * NCH * FT)
            with pe.Fori(0, NCH) as ch:
                post(1, ch)

            pe.wait_ge(S["diag_done"], NCH)
            pe.wait_ge(S["ld_l2"], 16 * 4)
            pe.wait_ge(S["t2_done"], 2 * NT + 1)
            with pe.Fori(0, NCH) as ch:
                pe.wait_ge(S["y_ready"], ch + 2 * NCH)

                def hidden_to_out(i):
                    pe.wait_ge(S["h_ready"], ch * HT + i + 1 + 2)
                    for f in range(FT):
                        last = mm(pb[f][:], w2_sb[:, i, f * P:(f + 1) * P], h_ring[:, i % 4, :], start=(i == 0), stop=(i == HT - 1))
                    last.then_inc(S["y_step"], 1)

                for i in range(HT):
                    pe.wait_ge(S["h_ready"], ch * HT + i + 1)
                    for k in range(FT):
                        mm(pb[4 + i % 2][:], w1_sb[:, k, i * P:(i + 1) * P], featT[:, k, ccols(ch)], start=(k == 0), stop=False)
                    mm(pb[4 + i % 2][:], w1e_sb[:, i * P:(i + 1) * P], e2T[:, ccols(ch)], start=False, stop=True
                       ).then_inc(S["h_full"], 1)
                    if i >= 1:
                        hidden_to_out(i - 1)
                hidden_to_out(HT - 1)
                post(2, ch)

            pe.wait_ge(S["ld_c1"], 16 * 4)
            pe.wait_ge(S["ld_c2"], 16 * 2)
            pe.wait_ge(S["y_ready"], 3 * NCH)
            for layer, w in ((3, c1_sb), (4, c2_sb)):
                if layer == 3:
                    pe.wait_ge(S["split_done"], 3 * NT + TPC)
                else:
                    pe.wait_ge(S["hl_loaded"], 32)
                pe.wait_ge(S["t2_done"], layer * NT + 1)
                with pe.Fori(0, NCH) as ch:
                    aggregate(ch, (layer - 1) * NCH * FT)
                    pe.wait_ge(S["agg_copied"], ch * FT + (layer - 1) * NCH * FT + FT)
                    for f in range(FT):
                        pe.wait_ge(S["dense_copied"], ch * FT + (layer - 1) * NCH * FT + f + 3)
                        dense(pb[4 + f % 2], ((w[:, 0, :, :], lambda k: featT[:, k, ccols(ch)]),
                                              (w[:, 1, :, :], lambda k: aggT[:, k, :])), f)
                    post(layer, ch)


_INS = ['x', 'src', 'dst', 'edge_attr_64', 'edge_weight', 'L0_gnn_weight', 'L0_gnn_self_weight', 'L0_gnn_bn_gamma',
        'L0_gnn_bn_beta', 'L1_gnn_W_l', 'L1_gnn_b_l', 'L1_gnn_W_r', 'L1_gnn_gamma', 'L1_gnn_beta', 'L2_gnn_W1',
        'L2_gnn_b1', 'L2_gnn_W2', 'L2_gnn_b2', 'L3_gnn_W1_0', 'L3_gnn_W1_1', 'L3_gnn_b1', 'L3_gnn_gamma',
        'L3_gnn_beta', 'L3_gnn_W2_0', 'L3_gnn_W2_1', 'L3_gnn_b2']


def kernel(**inputs):
    import numpy as _np
    import concourse.bacc as _bacc
    from concourse import mybir as _mybir
    from concourse.bass_utils import run_bass_kernel_spmd as _run

    nc = _bacc.Bacc("TRN2", target_bir_lowering=False, num_devices=1)
    arrays, args = {}, []
    for name in _INS:
        a = _np.ascontiguousarray(inputs[name])
        arrays[f"in_{name}"] = a
        args.append(nc.dram_tensor(f"in_{name}", a.shape, _mybir.dt.from_np(a.dtype), kind="ExternalInput").ap())
    out = nc.dram_tensor("out_0", (N, D), FP32, kind="ExternalOutput").ap()
    gnn_kernel(nc, *args, out)
    r = _run(nc, [arrays], core_ids=[0])
    return r.results[0]["out_0"]
```

```python
from contextlib import contextmanager

import concourse.bass as bass
from concourse import mybir

FP32 = mybir.dt.float32
FP16 = mybir.dt.float16
BF16 = mybir.dt.bfloat16
I32 = mybir.dt.int32
U32 = mybir.dt.uint32
ALU = mybir.AluOpType
ACT = mybir.ActivationFunctionType
AX = mybir.AxisListType

P = 128
N, D, E = 2048, 512, 34816
HID, EDGE_IN = 1024, 64
NT = N // P
FT = D // P
HT = HID // P
CW = 512
NCH = N // CW
TPC = CW // P
EDGE_TILES = E // P
LOT = 16
LOTS = EDGE_TILES // LOT
KEYS = NT * NT
ST = 2 * TPC + 1
STEPS = NCH * NT
SLOT_TILES = STEPS * ST
GROUP = 3
GROUPS = ST // GROUP
OH_RING = 4
REC = 6
AW_RING = 4
HL_RING = 3
BACK_AT = 2
AT_RING = 4
ZERO_COLS = 2048
ZERO_DMAS = SLOT_TILES * EDGE_IN // ZERO_COLS
PART = 8
PARTS = EDGE_TILES // PART
NORM_AFTER_LOTS = 2
SYM = 4 + 3
NORM_PIECE = 4 + SYM
ORTHO_PIECES = NORM_PIECE + 1 + 4 + 4 * (3 * SYM + 4) + 4
RANKED_BY_PRODUCT = 260
EPS = 1e-5
SLOPE = 0.01


class Chain:

    def __init__(self, engine, sem):
        self.engine, self.sem, self.base, self.n = engine, sem, 0, 0

    def link(self, instruction):
        instruction.then_inc(self.sem, 1)
        self.n += 1
        self.engine.wait_ge(self.sem, self.base + self.n)

    def settle(self):
        self.engine.wait_ge(self.sem, self.base + self.n)

    @contextmanager
    def loop(self, times, per):
        base, n = self.base, self.n
        with self.engine.Fori(0, times) as i:
            self.base, self.n = base + n + i * per, 0
            yield i
            assert self.n == per, (self.n, per)
        self.base, self.n = base, n + times * per

    def mark(self, instruction):
        instruction.then_inc(self.sem, 1)
        self.n += 1


def gnn_kernel(nc, x, src, dst, edge_attr, edge_weight, w0, self_w, bn_g, bn_b, wl, bl, wr, g1, be1,
               w1, b1, w2, b2, c1a, c1b, c1bias, ln_g, ln_b, c2a, c2b, c2bias, out, dbg=()):
    rec_table = nc.dram_tensor("rec_table", (P * SLOT_TILES, REC), BF16, kind="Internal").ap()
    attr_table = nc.dram_tensor("attr_table", (P * SLOT_TILES, EDGE_IN), FP32, kind="Internal").ap()
    x_after = [nc.dram_tensor(f"x_after_{i}", (N, D), FP32, kind="ExternalOutput" if dbg else "Internal").ap() for i in range(3)]
    h_parts = nc.dram_tensor("h_parts", (NT, P, 2, D), FP16, kind="Internal").ap()

    all_counts = nc.dram_tensor("all_counts", (STEPS, P, CW), FP16, kind="Internal").ap()
    all_weights = nc.dram_tensor("all_weights", (STEPS, P, CW), FP32, kind="Internal").ap()
    all_attrs = nc.dram_tensor("all_attrs", (NCH, P, CW), FP32, kind="Internal").ap()

    KB = 1024
    at = [(nc.sbuf_base + 31) // 32 * 32]

    def region(kb):
        start = at[0]
        at[0] += int(kb * KB)
        assert at[0] <= nc.sbuf_top, at[0] - nc.sbuf_top
        return start

    def sb(name, shape, dt, offset):
        return nc.alloc_sbuf_tensor_at(name, shape, dt, offset=offset)

    r_feat, r_adj, r_node = region(32), region(64), region(32)
    r_wa, r_wb = region(20), region(16)
    r_agg, r_y, r_xr, r_e2, r_cs = region(8), region(8), region(8), region(8), region(8)

    def small(name, shape, dt):
        size = {FP32: 4, I32: 4, U32: 4, FP16: 2, BF16: 2}[dt]
        for n in shape[1:]:
            size *= n
        start = at[0]
        at[0] += (size + 31) // 32 * 32
        assert at[0] <= nc.sbuf_top, at[0] - nc.sbuf_top
        return sb(name, shape, dt, start)

    featT = sb("featT", [P, FT, N], FP32, r_feat)
    adj = sb("adj", [P, NT, N], FP16, r_adj)
    x0 = sb("x0", [P, NT, D], FP32, r_node)
    x_hi = sb("x_hi", [P, NT, D], FP16, r_node)
    x_lo = sb("x_lo", [P, NT, D], FP16, r_node + 16 * KB)
    aggT = sb("aggT", [P, FT, CW], FP32, r_agg)
    ybuf = sb("ybuf", [P, FT, CW], FP32, r_y)
    xr = sb("xr", [P, TPC, D], FP32, r_xr)
    colscale = sb("colscale", [P, N], FP32, r_cs)
    zc, zcT, s_n, b_ping, b_pong, b_sq, b_s, w0_sb = (
        sb(n, [P, 4, D], FP32, r_adj + 8 * KB * i)
        for i, n in enumerate(("zc", "zcT", "s_n", "b_ping", "b_pong", "b_sq", "b_s", "w0_sb")))
    col = EDGE_TILES * 4
    src_i, dst_i, sb_i, db_i, dbl_i, sbl_i = (
        sb(n, [P, EDGE_TILES], I32, r_wa + col * i)
        for i, n in enumerate(("src_i", "dst_i", "sb_i", "db_i", "dbl_i", "sbl_i")))
    key, base, top, third, w_e = (
        sb(n, [P, EDGE_TILES], FP32, r_wa + col * (6 + i))
        for i, n in enumerate(("key", "base", "top", "third", "w_e")))
    rec = sb("rec", [P, EDGE_TILES, REC], BF16, r_wa + col * 11)
    slot = sb("slot", [P, EDGE_TILES], U32, r_wa + 18560)
    tri, no_tri = (sb(n, [P, P], BF16, r_cs + 256 * i) for i, n in enumerate(("tri", "no_tri")))
    eps_i, mhalf_i, threehalf_i = (
        sb(n, [P, P], FP32, r_cs + 512 * (1 + i)) for i, n in enumerate(("eps_i", "mhalf_i", "threehalf_i")))
    ranked_junk = sb("ranked_junk", [P, 2, KEYS], BF16, r_cs + 2048)
    rank = sb("rank", [P, LOT], FP32, r_cs + 3072)
    past1 = sb("past1", [P, LOT], FP32, r_cs + 3072 + 64)
    past2 = sb("past2", [P, LOT], FP32, r_cs + 3072 + 128)
    row = sb("row", [P, LOT], FP32, r_cs + 3072 + 192)
    z_sum = sb("z_sum", [P, 4], FP32, r_cs + 3584)
    sq_sum = sb("sq_sum", [P, 4], FP32, r_cs + 3648)
    s_tot = sb("s_tot", [P, 1], FP32, r_cs + 3680)
    s_rn = sb("s_rn", [P, 1], FP32, r_cs + 3712)
    s_rrn = sb("s_rrn", [P, 1], FP32, r_cs + 3744)
    s_u = sb("s_u", [P, 1], FP32, r_cs + 3776)
    sq_junk = sb("sq_junk", [P, D], FP32, r_cs + 4096)
    key_oh = sb("key_oh", [P, OH_RING, KEYS], BF16, r_cs + 6144)
    block_sb, block_db = (sb(n, [P, KEYS], I32, r_cs + 4096 + KB * i) for i, n in enumerate(("block_sb", "block_db")))
    block_cap, block_edges = (sb(n, [P, KEYS], FP32, r_cs + 6144 + KB * i) for i, n in enumerate(("block_cap", "block_edges")))
    over_max = sb("over_max", [P, 1], FP32, r_cs + 3776 + 32)
    pad = sb("pad", [P, SLOT_TILES, REC], BF16, r_e2)
    zeros = sb("zeros", [P, ZERO_COLS], FP32, r_xr)
    at_general = [r_adj]

    def general(name, shape, dt, size):
        at_general[0] += size
        return sb(name, shape, dt, at_general[0] - size)

    g_src_oh = general("g_src_oh", [P, PART, P], FP32, 4 * KB)
    g_dst_oh = general("g_dst_oh", [P, PART, CW], FP32, 16 * KB)
    g_weight_oh = general("g_weight_oh", [P, PART, CW], FP32, 16 * KB)
    g_attr = general("g_attr", [P, PART, P], FP32, 4 * KB)
    g_iota = general("g_iota", [P, CW], FP32, 2 * KB)
    g_zero = general("g_zero", [P, CW], FP32, 2 * KB)
    g_weights = general("g_weights", [P, CW], FP32, 2 * KB)
    g_counts = general("g_counts", [P, CW], FP16, 1 * KB)
    g_src_i, g_dst_i, g_w, g_src, g_dst = (
        general(n, [P, EDGE_TILES], dt, col) for n, dt in
        (("g_src_i", I32), ("g_dst_i", I32), ("g_w", FP32), ("g_src", FP32), ("g_dst", FP32)))
    oh = sb("oh", [P, OH_RING, 5, P, GROUP], BF16, r_wa)
    fields = sb("fields", [P, 5, SLOT_TILES], BF16, r_cs)
    iota_group = sb("iota_group", [P, P, GROUP], BF16, r_cs + 6 * KB)
    recs = sb("recs", [P, SLOT_TILES, REC], BF16, r_xr)
    dst_keep = sb("dst_keep", [P, SLOT_TILES], BF16, r_wa + 17 * KB)
    aw = sb("aw", [P, AW_RING, CW], FP32, r_y)
    stage = sb("stage", [P, 2, LOT, EDGE_IN], FP32, r_e2)
    t_sb = sb("t_sb", [P, 4, D], FP32, r_wb)
    self_sb = sb("self_sb", [P, 4, D], FP32, r_wb + 8 * KB)
    wl_sb = sb("wl_sb", [P, 4, D], FP32, r_wa)
    wr_sb = sb("wr_sb", [P, 4, D], FP32, r_wb)
    at_oh = sb("at_oh", [P, 2, GROUPS, P, GROUP], FP16, r_wa + 8 * KB)
    iota_group16 = sb("iota_group16", [P, P, GROUP], FP16, r_wa + 19 * KB - 512)
    at_parts = sb("at_parts", [P, 2, ST, 2, EDGE_IN], FP16, r_wa + 8 * KB + 4608)
    at_in = sb("at_in", [P, AT_RING, ST, EDGE_IN], FP32, r_y)
    e2T = sb("e2T", [P, N], FP32, r_e2)
    diag = sb("diag", [P, NT, P], FP32, r_agg)
    w1_sb = sb("w1_sb", [P, 4, HID], FP32, r_wa)
    w1e_sb = sb("w1e_sb", [P, HID], FP32, r_wa + 16 * KB)
    w2_sb = sb("w2_sb", [P, HT, D], FP32, r_wb)
    h_ring = sb("h_ring", [P, 4, CW], FP32, r_agg)
    c1_sb = sb("c1_sb", [P, 2, 4, D], FP32, r_wa)
    lng_sb = sb("lng_sb", [P, D], FP32, r_wa + 16 * KB)
    lnb_sb = sb("lnb_sb", [P, D], FP32, r_wa + 18 * KB)
    c2_sb = sb("c2_sb", [P, 2, 4, D], FP32, r_wb)
    hl = sb("hl", [P, HL_RING, 2, D], FP16, r_e2)
    bias_rows = {2: sb("b2_row", [P, D], FP32, r_y), 3: sb("c1_row", [P, D], FP32, r_e2 + 6 * KB),
                 4: sb("c2_row", [P, D], FP32, r_wa + 16 * KB)}
    ident = small("ident", [P, P], FP32)
    iota = small("iota", [P, KEYS], BF16)
    ones16 = small("ones16", [P, P], FP16)
    ones32 = small("ones32", [P, P], FP32)
    cols = {n: small(n + "_c", [P, 4], FP32) for n in ("bn_g", "bn_b", "bl", "g1", "be1")}
    b1_sb = small("b1_c", [P, HT], FP32)
    bn_st = small("bn_st", [P, FT, NCH, 6], FP32)
    bn_mv = small("bn_mv", [P, FT, 2], FP32)
    bn_sc = small("bn_sc", [P, FT], FP32)
    bn_bi = small("bn_bi", [P, FT], FP32)
    ln_st = small("ln_st", [P, TPC, 6], FP32)
    ln_mv = small("ln_mv", [P, TPC, 2], FP32)
    ln_v, ln_r, ln_u = (small(n, [P, TPC], FP32) for n in ("ln_v", "ln_r", "ln_u"))
    bn_v, bn_u = (small(n, [P, FT], FP32) for n in ("bn_v", "bn_u"))
    overfull = small("overfull", [P, 1], I32)
    deg = small("deg", [P, NT], FP32)
    dinv = small("dinv", [P, NT], FP32)
    dpos = small("dpos", [P, NT], FP32)
    deg_v, deg_u = (small(n, [P, NT], FP32) for n in ("deg_v", "deg_u"))

    pb = [nc.alloc_psum_tensor(f"bank{i}", [P, 512], FP32) for i in range(8)]
    RANK_BANK = 4

    def y_bank(layer, q):
        return pb[{0: q, 1: q, 2: q, 3: TPC + q % 2, 4: TPC + q % 2}[layer]]

    def t2_bank(layer, q):
        return pb[TPC + q if layer < 2 else 7]

    def bank_free(layer, ch, q):
        return tile_no(layer, ch, q) + (1 if layer < 2 else TPC)

    S = {n: nc.alloc_semaphore(n) for n in (
        "ld_edges ld_w0 ld_x ld_self ld_par ld_recs ld_l1 ld_l2 ld_c1 ld_c2 ld_b2 ld_c2_row x_copied hl_loaded init_rec init_attr "
        "inverse_ready root_ready iota_ready ident_ready tri_ready pads_ready mats_ready dve pool act "
        "key_oh_ready rank_mm ranked slots_ready rec_sent attr_sent0 attr_sent1 stage_ld0 stage_ld1 "
        "zc_ready ortho_full ortho_free squares_ready places_ready norm_ready stats_ready s_scaled oh_ready oh_used adj_evac "
        "agg_step agg_full agg_copied dense_full dense_copied bn_ready z_ready y_ready t1_full t1_free normed t2_full "
        "t2_done split_done deg_full deg_done at_high at_split at_used at_oh_ready e2_done diag_ready diag_full diag_done "
        "h_full h_ready y_step at_in0 at_in1 at_in2 at_in3 totals_ready overfull_ready g_edges_ld g_consts_ready g_oh_ready g_used "
        "g_out g_stored g_attr_ld g_dve g_attrs_stored adj_final general_ld general_attrs_ld").split()}
    s_xin = [nc.alloc_semaphore(f"xin_{q}") for q in range(TPC)]
    s_xout = [nc.alloc_semaphore(f"xout_{q}") for q in range(TPC)]

    def tile_no(layer, ch, q=0):
        return layer * NT + ch * TPC + q

    def ccols(ch):
        return bass.ds(ch * CW, CW)

    ROOT_NORM, ROOT_NORM2, ROOT_BN, ROOT_DEG = 0, 1, (2, 8), 7
    ROOT_LN = (3, 9, 13, 17, 21)
    LOADS = {0: 0, 1: 1, 2: 2, 4: 3}
    attr_rows = attr_table.rearrange("(p s) r -> p (s r)", p=P)

    with nc.allow_non_contiguous_dma("parameters by column"), nc.Block() as block:

        @block.sync
        def _(sp):
            sp.dma_start(src_i[:], src.rearrange("(p c) -> p c", p=P)).then_inc(S["ld_edges"], 16)
            sp.dma_start(dst_i[:], dst.rearrange("(p c) -> p c", p=P)).then_inc(S["ld_edges"], 16)
            sp.dma_start(w_e[:], edge_weight.rearrange("(p c) -> p c", p=P)).then_inc(S["ld_edges"], 16)
            sp.dma_start(w0_sb[:], w0.rearrange("(i p) d -> p i d", p=P)).then_inc(S["ld_w0"], 16)
            sp.wait_ge(S["pads_ready"], 3)
            sp.dma_start(rec_table.rearrange("(p s) r -> p (s r)", p=P),
                         pad[:].rearrange("p s r -> p (s r)")).then_inc(S["init_rec"], 16)
            sp.dma_start(x0[:], x.rearrange("(t p) d -> p t d", p=P)).then_inc(S["ld_x"], 16)
            sp.dma_start(self_sb[:], self_w.rearrange("(i p) d -> p i d", p=P)).then_inc(S["ld_self"], 16)
            for name, vec in (("bn_g", bn_g), ("bn_b", bn_b), ("bl", bl), ("g1", g1), ("be1", be1)):
                sp.dma_start(cols[name][:], vec.rearrange("(f p) -> p f", p=P)).then_inc(S["ld_par"], 16)
            sp.dma_start(b1_sb[:], b1.rearrange("(f p) -> p f", p=P)).then_inc(S["ld_par"], 16)
            for i in range(ZERO_DMAS):
                sp.dma_start(attr_rows[:, i * ZERO_COLS:(i + 1) * ZERO_COLS], zeros[:]).then_inc(S["init_attr"], 16)

            sp.wait_ge(S["overfull_ready"], 1)
            overfull_sp = sp.value_load(overfull[0:1, 0:1], min_val=0, max_val=1)
            with sp.If(overfull_sp > 0):
                sp.wait_ge(S["ortho_free"], ORTHO_PIECES)
                for tile, vec in ((g_src_i, src), (g_dst_i, dst), (g_w, edge_weight)):
                    sp.dma_start(tile[:], vec.rearrange("(p c) -> p c", p=P)).then_inc(S["g_edges_ld"], 16)
                with sp.Fori(0, STEPS) as i:
                    sp.wait_ge(S["g_out"], i + 1 + 1)
                    for table, tile in ((all_counts, g_counts), (all_weights, g_weights)):
                        sp.dma_start(table[bass.ds(i, 1), :, :].rearrange("a p d -> (a p) d"), tile[:]
                                     ).then_inc(S["g_stored"], 16)
                sp.wait_ge(S["g_consts_ready"], 4)
                with sp.Fori(0, NCH) as ch:
                    with sp.Fori(0, PARTS) as part:
                        sp.wait_ge(S["g_used"], part + ch * PARTS + STEPS * PARTS + 1)
                        sp.dma_start(g_attr[:, :, 0:EDGE_IN], edge_attr.rearrange("(p c) r -> p c r", p=P)
                                     [:, bass.ds(part * PART, PART), :]).then_inc(S["g_attr_ld"], 16)
                    sp.wait_ge(S["g_out"], ch + STEPS + 1 + 1)
                    sp.dma_start(all_attrs[bass.ds(ch, 1), :, :].rearrange("a p d -> (a p) d"), g_weights[:]
                                 ).then_inc(S["g_attrs_stored"], 16)
                sp.wait_ge(S["g_stored"], 32 * (STEPS + 1))
                sp.wait_ge(S["g_attrs_stored"], 16 * (NCH + 1))

            sp.wait_ge(S["init_attr"], 16 * ZERO_DMAS)
            sp.wait_ge(S["rec_sent"], 16 * EDGE_TILES)
            sp.dma_start(recs[:].rearrange("p s r -> p (s r)"),
                         rec_table.rearrange("(p s) r -> p (s r)", p=P)).then_inc(S["ld_recs"], 16)

            def load_x(layer, source, ch, so_far):
                for q in range(TPC):
                    sp.wait_ge(s_xout[q], 16 * (so_far * NCH + 1) + 16 * ch)
                for q in range(TPC):
                    t = tile_no(layer, ch if layer < 4 else 0, q)
                    sp.wait_ge(S["t2_full"], t + 1)
                    sp.wait_ge(S["split_done"], t + 1)
                    sp.dma_start(xr[:, q, :], source[bass.ds((ch * TPC + q) * P, P), :]).then_inc(s_xin[q], 16)

            def store_x(layer, to, ch):
                for q in range(TPC):
                    sp.wait_ge(S["normed"], tile_no(layer, ch, q) + 1)
                    sp.dma_start(to[bass.ds((ch * TPC + q) * P, P), :], xr[:, q, :]).then_inc(s_xout[q], 16)

            def stored(so_far):
                for q in range(TPC):
                    sp.wait_ge(s_xout[q], 16 * (so_far * NCH + 1))

            sp.sem_inc(S["t2_full"], TPC)
            sp.sem_inc(S["split_done"], TPC)
            sp.sem_inc(S["at_split"], AT_RING)
            for q in range(TPC):
                sp.sem_inc(s_xout[q], 16)
            with sp.If(overfull_sp > 0):
                with sp.Fori(0, NCH) as ch:
                    for t in range(NT):
                        sp.wait_ge(S["adj_evac"], ch * NT + t + 1 + 2)
                        step = bass.ds(ch * NT + t, 1)
                        for table, tile in ((all_counts, adj[:, t, ccols(ch)]), (all_weights, aw[:, t % AW_RING, :])):
                            sp.dma_start(tile, table[step, :, :].rearrange("a p d -> (a p) d")).then_inc(S["general_ld"], 16)
                        sp.wait_ge(S["general_ld"], (32 * NT) * ch + 32 * (t + 1))
                        sp.sem_inc(S["adj_final"], 1)
            with sp.If(overfull_sp < 1):
                with sp.Fori(0, NCH) as ch:
                    for t in range(NT):
                        sp.wait_ge(S["adj_evac"], ch * NT + t + 1 + 2)
                        sp.sem_inc(S["adj_final"], 1)
            sp.wait_ge(S["oh_ready"], STEPS * GROUPS)
            with sp.Fori(0, NCH) as ch:
                load_x(0, x, ch, 0)
                store_x(0, x_after[0], ch)
            stored(1)
            sp.dma_start(wl_sb[:], wl.rearrange("(i p) d -> p i d", p=P)).then_inc(S["ld_l1"], 16)
            sp.dma_start(wr_sb[:], wr.rearrange("(i p) d -> p i d", p=P)).then_inc(S["ld_l1"], 16)
            for u in range(2):
                sp.wait_ge(S[f"attr_sent{u}"], 16 * LOT * ((LOTS + 1 - u) // 2))
            for name in ("t1_full", "t2_full", "split_done"):
                sp.wait_ge(S[name], NT + TPC)
            with sp.Fori(0, STEPS // AT_RING) as i:
                for u in range(AT_RING):
                    sp.wait_ge(S["at_split"], i * AT_RING + u + 1)
                    sp.dma_start(at_in[:, u, :, :].rearrange("p s r -> p (s r)"),
                                 attr_rows[:, bass.ds((i * AT_RING + u) * (ST * EDGE_IN), ST * EDGE_IN)]
                                 ).then_inc(S[f"at_in{u}"], 16)
            sp.wait_ge(S["at_split"], STEPS + AT_RING)
            with sp.If(overfull_sp > 0):
                sp.wait_ge(S["e2_done"], NCH)
                sp.dma_start(e2T[:].rearrange("p (a d) -> p a d", a=NCH), all_attrs.rearrange("a p d -> p a d")
                             ).then_inc(S["general_attrs_ld"], 16)
            sp.wait_ge(S["dense_full"], 2 * NCH * FT)
            sp.dma_start(w1_sb[:], w1[0:D, :].rearrange("(i p) d -> p i d", p=P)).then_inc(S["ld_l2"], 16)
            for half in range(2):
                sp.dma_start(w1e_sb[half * EDGE_IN:(half + 1) * EDGE_IN, :], w1[D:D + EDGE_IN, :]).then_inc(S["ld_l2"], 16)
            sp.dma_start(w2_sb[:], w2.rearrange("(i p) d -> p i d", p=P)).then_inc(S["ld_l2"], 16)
            with sp.Fori(0, NCH) as ch:
                load_x(1, x_after[0], ch, 1)
                store_x(1, x_after[1], ch)
            stored(2)
            sp.dma_start(bias_rows[2][:], b2.rearrange("(a d) -> a d", a=1).to_broadcast([P, D])).then_inc(S["ld_b2"], 16)
            with sp.Fori(0, NCH - 1) as ch:
                load_x(2, x_after[1], ch, 2)
                store_x(2, x_after[2], ch)
            load_x(2, x_after[1], NCH - 1, 2)
            sp.wait_ge(S["y_step"], NCH * HT + 4)
            for i, w in enumerate((c1a, c1b)):
                sp.dma_start(c1_sb[:, i, :, :], w.rearrange("(i p) d -> p i d", p=P)).then_inc(S["ld_c1"], 16)
            for tile, vec in ((lng_sb, ln_g), (lnb_sb, ln_b), (bias_rows[3], c1bias)):
                sp.dma_start(tile[:], vec.rearrange("(a d) -> a d", a=1).to_broadcast([P, D])).then_inc(S["ld_c1"], 16)
            for i, w in enumerate((c2a, c2b)):
                sp.dma_start(c2_sb[:, i, :, :], w.rearrange("(i p) d -> p i d", p=P)).then_inc(S["ld_c2"], 16)
            store_x(2, x_after[2], NCH - 1)
            stored(3)
            with sp.Fori(0, NCH - 1) as ch:
                for q in range(TPC):
                    sp.wait_ge(S["split_done"], tile_no(3, ch, q) + 1 + TPC)
                    sp.dma_start(h_parts[bass.ds(ch * TPC + q, 1), :, :, :].rearrange("a p b d -> (a p) b d"),
                                 hl[:, q % HL_RING, :, :]).then_inc(s_xout[q], 16)
            for q in range(TPC):
                sp.wait_ge(s_xout[q], 16 * (4 * NCH - 1 + 1))
            sp.wait_ge(S["agg_full"], 2 * NCH)
            for i, tile in enumerate((x_hi, x_lo)):
                sp.dma_start(tile[:, 0:NT - TPC, :], h_parts[0:NT - TPC, :, i, :].rearrange("t p d -> p t d")
                             ).then_inc(S["hl_loaded"], 16)
            sp.wait_ge(S["split_done"], 4 * NT + TPC)
            sp.dma_start(bias_rows[4][:], c2bias.rearrange("(a d) -> a d", a=1).to_broadcast([P, D])).then_inc(S["ld_c2_row"], 16)
            for q in range(TPC):
                sp.sem_inc(s_xout[q], 16)
            with sp.Fori(0, NCH) as ch:
                load_x(4, x_after[2], ch, 4)
                store_x(4, out, ch)
            stored(5)

        @block.gpsimd
        def _(pool):
            chain = Chain(pool, S["pool"])
            nc.gpsimd.memset(zeros[:], 0.0).then_inc(S["pads_ready"], 1)
            nc.gpsimd.memset(pad[:], 0.0).then_inc(S["pads_ready"], 1)
            pool.wait_ge(S["pads_ready"], 2)
            nc.gpsimd.memset(pad[:, :, 0:2], -1.0).then_inc(S["pads_ready"], 1)
            nc.gpsimd.iota(iota[:], pattern=[[1, KEYS]], base=0, channel_multiplier=0,
                           allow_small_or_imprecise_dtypes=True).then_inc(S["iota_ready"], 1)
            chain.link(nc.gpsimd.memset(tri[:], 1.0))
            nc.gpsimd.affine_select(out=no_tri[:], in_=tri[:], compare_op=ALU.is_ge, fill=0.0, base=0,
                                    pattern=[[-1, P]], channel_multiplier=1).then_inc(S["tri_ready"], 1)
            pool.wait_ge(S["tri_ready"], 1)
            nc.gpsimd.affine_select(out=tri[:], in_=tri[:], compare_op=ALU.is_gt, fill=0.0, base=0,
                                    pattern=[[1, P]], channel_multiplier=-1).then_inc(S["tri_ready"], 1)
            chain.link(nc.gpsimd.memset(ident[:], 0.0))
            nc.gpsimd.affine_select(out=ident[:], in_=ident[:], compare_op=ALU.not_equal, fill=1.0, base=0,
                                    pattern=[[-1, P]], channel_multiplier=1).then_inc(S["ident_ready"], 1)
            nc.gpsimd.memset(ones16[:], 1.0).then_inc(S["ident_ready"], 1)
            nc.gpsimd.memset(ones32[:], 1.0).then_inc(S["ident_ready"], 1)

            pool.wait_ge(S["init_rec"], 16)
            for c in range(EDGE_TILES):
                if c % LOT == 0:
                    pool.wait_ge(S["slots_ready"], c // LOT + 1)
                pool.indirect_dma_start(out=rec_table, out_offset=bass.IndirectOffsetOnAxis(ap=slot[:, c:c + 1], axis=0),
                                        in_=rec[:, c, :], in_offset=None).then_inc(S["rec_sent"], 16)
            pool.wait_ge(S["init_attr"], 16 * ZERO_DMAS)
            attr_in = edge_attr.rearrange("(p c) r -> p c r", p=P)
            for lot in range(LOTS):
                u = lot % 2
                if lot >= 2:
                    pool.wait_ge(S[f"attr_sent{u}"], 16 * LOT * (lot // 2))
                pool.dma_start(stage[:, u, :, :], attr_in[:, lot * LOT:(lot + 1) * LOT, :]).then_inc(S[f"stage_ld{u}"], 16)
                pool.wait_ge(S[f"stage_ld{u}"], 16 * (lot // 2 + 1))
                for j in range(LOT):
                    c = lot * LOT + j
                    pool.indirect_dma_start(
                        out=attr_table, out_offset=bass.IndirectOffsetOnAxis(ap=slot[:, c:c + 1], axis=0),
                        in_=stage[:, u, j, :], in_offset=None).then_inc(S[f"attr_sent{u}"], 16)

            with pool.Fori(0, STEPS // AT_RING) as i:
                for u in range(AT_RING):
                    pool.wait_ge(S["at_high"], i * AT_RING + u + 1)
                    nc.gpsimd.tensor_tensor(at_parts[:, u % 2, :, 1, :], at_in[:, u, :, :], at_parts[:, u % 2, :, 0, :],
                                            ALU.subtract).then_inc(S["at_split"], 1)

        @block.scalar
        def _(act):
            act.wait_ge(S["ident_ready"], 3)
            for m, v in ((eps_i, EPS), (mhalf_i, -0.5), (threehalf_i, 1.5)):
                nc.scalar.activation(m[:], ident[:], ACT.Copy, scale=v).then_inc(S["mats_ready"], 1)
            done = [0]

            def evac(to, scale=1.0, shape=None, cols=slice(0, D)):
                n = done[0]
                bank = pb[n % 4][:, cols] if shape is None else pb[n % 4][:].rearrange("p (a b) -> p a b", a=shape)
                act.wait_ge(S["ortho_full"], n + 1)
                done[0] += 1
                nc.scalar.activation(to, bank, ACT.Copy, scale=scale).then_inc(S["ortho_free"], 1)

            def evac_x0(t):
                evac(featT[:, :, t * P:(t + 1) * P], shape=FT)

            for i in range(4):
                evac(zcT[:, :, i * P:(i + 1) * P], shape=4)
            def evac_upper(to, scale=1.0):
                for i in range(4):
                    evac(to[:, i, i * P:], scale=scale, cols=slice(i * P, D))

            def evac_mirrored(to):
                for i in range(1, 4):
                    evac(to[:, i, 0:i * P], cols=slice(0, i * P))

            evac_upper(s_n)
            evac_mirrored(s_n)
            act.wait_ge(S["ortho_free"], done[0])
            for i in range(4):
                nc.scalar.activation(sq_junk[:], s_n[:, i, :], ACT.Square, accum_out=sq_sum[:, i:i + 1]
                                     ).then_inc(S["squares_ready"], 1)
                act.wait_ge(S["squares_ready"], i + 1)
            done[0] += 1

            def root(no, to, inverse):
                act.wait_ge(S["inverse_ready"], no + 1)
                nc.scalar.activation(to, inverse, ACT.Sqrt).then_inc(S["root_ready"], 1)

            root(ROOT_NORM, s_rn[:], s_u[:])
            root(ROOT_NORM2, s_rrn[:], s_rn[:])
            act.wait_ge(S["norm_ready"], 1)
            for i in range(4):
                nc.scalar.activation(s_n[:, i, :], s_n[:, i, :], ACT.Copy, scale=s_rn[:]).then_inc(S["s_scaled"], 1)
            for i in range(4):
                evac(b_ping[:, i, :])
            b = [b_ping, b_pong]
            for it in range(4):
                evac_upper(b_sq)
                evac_upper(b_s, scale=-0.5)
                evac_mirrored(b_sq)
                evac_x0(4 * it)
                evac_x0(4 * it + 1)
                evac_mirrored(b_s)
                evac_x0(4 * it + 2)
                evac_upper(b[1])
                evac_x0(4 * it + 3)
                evac_mirrored(b[1])
                b.reverse()
            for i in range(4):
                evac(t_sb[:, i, :], scale=s_rrn[:])

            act.sem_inc(S["adj_evac"], 2)
            act.sem_inc(S["agg_step"], AW_RING)
            act.sem_inc(S["dense_copied"], 4)
            act.sem_inc(S["y_step"], 4)
            act.sem_inc(S["h_ready"], 2)
            with act.Fori(0, NCH) as ch:
                for t in range(NT):
                    act.wait_ge(S["oh_used"], ch * (NT * GROUPS) + (t + 1) * GROUPS + OH_RING)
                    act.wait_ge(S["agg_step"], ch * NT + t + 1)
                    nc.scalar.activation(adj[:, t, ccols(ch)], pb[4 + 2 * (t % 2)][:], ACT.Copy)
                    nc.scalar.activation(aw[:, t % AW_RING, :], pb[5 + 2 * (t % 2)][:], ACT.Copy).then_inc(S["adj_evac"], 1)
                act.wait_ge(S["agg_step"], ch * NT + NT + AW_RING)
                for f in range(FT):
                    nc.scalar.activation(aggT[:, f, :], pb[f][:], ACT.Copy).then_inc(S["agg_copied"], 1)
                act.wait_ge(S["dense_full"], ch * FT + FT)
                for f in range(FT):
                    nc.scalar.activation(featT[:, f, ccols(ch)], pb[4 + f][:], ACT.Copy).then_inc(S["dense_copied"], 1)

            def features_to_ybuf(layer, ch, func, ready):
                act.wait_ge(S["t1_full"], tile_no(layer, ch) + TPC)
                for f in range(FT):
                    last = nc.scalar.activation(ybuf[:, f, :], featT[:, f, ccols(ch)], func,
                                                scale=bn_sc[:, f:f + 1], bias=bn_bi[:, f:f + 1])
                last.then_inc(S[ready], 1)

            def ln_root(layer, ch):
                root(ch + ROOT_LN[layer], ln_r[:], ln_u[:])

            def transposed_back(layer, ch, q):
                act.wait_ge(S["t2_full"], tile_no(layer, ch, q) + 1 + TPC)
                nc.scalar.activation(featT[:, :, bass.ds((ch * TPC + q) * P, P)],
                                     t2_bank(layer, q)[:].rearrange("p (a b) -> p a b", a=FT),
                                     ACT.Copy).then_inc(S["t2_done"], 1)

            def post(layer, ch):
                ln_root(layer, ch)
                for q in range(TPC):
                    transposed_back(layer, ch, q)

            act.sem_inc(S["t1_full"], TPC)
            act.sem_inc(S["t2_done"], TPC)
            root(ROOT_BN[0], bn_sc[:], bn_u[:])
            act.wait_ge(S["bn_ready"], 1)
            features_to_ybuf(0, 0, ACT.Relu, "y_ready")
            with act.Fori(0, NCH - 1) as ch:
                features_to_ybuf(0, ch + 1, ACT.Relu, "y_ready")
                post(0, ch)
            post(0, NCH - 1)

            act.sem_inc(S["at_used"], 2)
            with act.Fori(0, NCH) as ch:
                for t in range(NT):
                    act.wait_ge(S[f"at_in{t % AT_RING}"], ch * (16 * NT // AT_RING) + 16 * (t // AT_RING + 1))
                    act.wait_ge(S["at_used"], ch * NT + t + 1)
                    nc.scalar.activation(at_parts[:, t % 2, :, 0, :], at_in[:, t % AT_RING, :, :], ACT.Copy).then_inc(S["at_high"], 1)
                act.wait_ge(S["dense_full"], ch * FT + NCH * FT + FT)
                for f in range(FT):
                    nc.scalar.activation(featT[:, f, ccols(ch)], pb[4 + (f + 1) % FT][:], ACT.Identity,
                                         bias=cols["bl"][:, f:f + 1]).then_inc(S["dense_copied"], 1)
            root(ROOT_DEG, dinv[:], deg_u[:])
            root(ROOT_BN[1], bn_sc[:], bn_u[:])
            act.wait_ge(S["bn_ready"], 2)
            features_to_ybuf(1, 0, ACT.Identity, "z_ready")
            with act.Fori(0, NCH - 1) as ch:
                features_to_ybuf(1, ch + 1, ACT.Identity, "z_ready")
                post(1, ch)
            post(1, NCH - 1)

            def layer2(ch, last_ch):
                for i in range(HT):
                    act.wait_ge(S["h_full"], ch * HT + i + 1)
                    act.wait_ge(S["y_step"], ch * HT + i + 1)
                    nc.scalar.activation(h_ring[:, i % 4, :], pb[4 + i % 2][:], ACT.Relu,
                                         bias=b1_sb[:, i:i + 1]).then_inc(S["h_ready"], 1)
                    if last_ch is not None:
                        if i == BACK_AT - 1:
                            ln_root(2, last_ch)
                        if BACK_AT <= i < BACK_AT + TPC:
                            transposed_back(2, last_ch, i - BACK_AT)

            layer2(0, None)
            with act.Fori(0, NCH - 1) as last_ch:
                layer2(last_ch + 1, last_ch)
            post(2, NCH - 1)

            for layer in (3, 4):
                act.wait_ge(S["t2_done"], layer * NT + TPC)
                with act.Fori(0, NCH) as ch:
                    act.wait_ge(S["dense_full"], (layer - 1) * NCH * FT + ch * FT)
                    for f in range(FT):
                        nc.scalar.activation(ybuf[:, f, :], featT[:, f, ccols(ch)], ACT.Copy).then_inc(S["x_copied"], 1)
                    if layer == 3:
                        post(3, ch)
                    else:
                        ln_root(4, ch)

        @block.vector
        def _(dve):
            chain = Chain(dve, S["dve"])
            V = nc.vector

            def invert(no, v, u):
                chain.link(V.reciprocal(u, v))
                dve.sem_inc(S["inverse_ready"], 1)

            def inverse_root(no, v, u, r):
                dve.wait_ge(S["root_ready"], no + 1)
                chain.link(V.tensor_tensor(u, r, r, ALU.mult))
                chain.link(V.tensor_tensor(u, u, v, ALU.mult))
                chain.link(V.tensor_scalar(u, u, -0.5, 1.5, ALU.mult, ALU.add))
                chain.link(V.tensor_tensor(r, r, u, ALU.mult))

            dve.wait_ge(S["ld_edges"], 48)
            chain.mark(V.tensor_scalar(sb_i[:], src_i[:], 7, None, ALU.logical_shift_right))
            chain.link(V.tensor_scalar(db_i[:], dst_i[:], 7, None, ALU.logical_shift_right))
            chain.mark(V.tensor_scalar(sbl_i[:], sb_i[:], TPC - 1, None, ALU.bitwise_and))
            chain.mark(V.tensor_scalar(dbl_i[:], db_i[:], TPC - 1, None, ALU.bitwise_and))
            chain.mark(V.tensor_scalar(src_i[:], src_i[:], P - 1, None, ALU.bitwise_and))
            chain.link(V.tensor_scalar(dst_i[:], dst_i[:], P - 1, None, ALU.bitwise_and))
            chain.mark(V.tensor_copy(rec[:, :, 0], src_i[:]))
            chain.mark(V.tensor_copy(rec[:, :, 1], dst_i[:]))
            chain.mark(V.scalar_tensor_tensor(key[:], db_i[:], float(NT), sb_i[:], ALU.mult, ALU.add))
            chain.link(V.tensor_scalar(base[:], dbl_i[:], 2.0 - ST * NT / TPC, None, ALU.mult))
            chain.link(V.scalar_tensor_tensor(base[:], db_i[:], ST * NT / TPC, base[:], ALU.mult, ALU.add))
            chain.link(V.scalar_tensor_tensor(base[:], sb_i[:], float(ST), base[:], ALU.mult, ALU.add))
            chain.mark(V.tensor_tensor(top[:], sbl_i[:], dbl_i[:], ALU.is_equal))
            chain.link(V.tensor_scalar(third[:], dbl_i[:], -2.0, float(2 * TPC - 1 - P * SLOT_TILES), ALU.mult, ALU.add))
            chain.link(V.tensor_scalar(top[:], top[:], float(P), float(2 * P - 1), ALU.mult, ALU.add))
            for k in range(3):
                chain.link(V.tensor_copy(rec[:, :, 2 + k], w_e[:]))
                if k < 2:
                    chain.link(V.tensor_tensor(w_e[:], w_e[:], rec[:, :, 2 + k], ALU.subtract))
            chain.mark(V.memset(rec[:, :, 5], 0.0))
            chain.link(V.memset(key_oh[:], 0.0))

            dve.wait_ge(S["iota_ready"], 1)
            dve.sem_inc(S["ranked"], 2)
            top2 = top[:].rearrange("p (c two) -> p c two", two=2)
            rank2 = rank[:].rearrange("p (c two) -> p c two", two=2)

            def rank_lots(first, count):
                with chain.loop(count, 7) as i:
                    c0 = i * LOT + first * LOT

                    def extract(j):
                        dve.wait_ge(S["rank_mm"], c0 + j + 1)
                        V.tensor_tensor_reduce(out=ranked_junk[:, j % 2, :], in0=pb[RANK_BANK + j % 2][:, 0:KEYS],
                                               in1=key_oh[:, j % OH_RING, :], scale=1.0, scalar=0.0,
                                               op0=ALU.mult, op1=ALU.add, accum_out=rank[:, j:j + 1]
                                               ).then_inc(S["ranked"], 1)

                    for j in range(LOT):
                        V.tensor_scalar(key_oh[:, j % OH_RING, :], iota[:], key[:, bass.ds(c0 + j, 1)], None,
                                        ALU.is_equal).then_inc(S["key_oh_ready"], 1)
                        if j >= 1:
                            extract(j - 1)
                    extract(LOT - 1)
                    dve.wait_ge(S["ranked"], c0 + LOT + 2)
                    lot = bass.ds(c0, LOT)
                    chain.link(V.tensor_tensor(rank2[:, :, 1], top2[:, bass.ds(i * (LOT // 2) + first * (LOT // 2), LOT // 2), 1],
                                               rank2[:, :, 1], ALU.subtract))
                    chain.mark(V.tensor_scalar(past1[:], rank[:], float(P), float(1 - P * SLOT_TILES), ALU.is_ge, ALU.mult))
                    chain.mark(V.scalar_tensor_tensor(past2[:], rank[:], float(2 * P), third[:, lot], ALU.is_ge, ALU.mult))
                    chain.link(V.scalar_tensor_tensor(row[:], rank[:], float(SLOT_TILES), base[:, lot], ALU.mult, ALU.add))
                    chain.link(V.tensor_tensor(row[:], row[:], past1[:], ALU.add))
                    chain.link(V.tensor_tensor(row[:], row[:], past2[:], ALU.add))
                    chain.link(V.tensor_scalar(slot[:, lot], row[:], 0.0, float(P * SLOT_TILES - 1), ALU.max, ALU.min))
                    dve.sem_inc(S["slots_ready"], 1)

            rank_lots(0, 1)
            dve.wait_ge(S["ld_w0"], 16)
            dve.wait_ge(S["ident_ready"], 3)
            chain.link(V.tensor_scalar(w0_sb[:], w0_sb[:], 0.5, None, ALU.mult))
            for i in range(4):
                block_i = w0_sb[:, i, i * P:(i + 1) * P]
                chain.link(V.scalar_tensor_tensor(block_i, ident[:], 0.5, block_i, ALU.mult, ALU.add))
            chain.link(V.tensor_reduce(z_sum[:], w0_sb[:], AX.X, ALU.add))
            chain.link(V.tensor_scalar(z_sum[:], z_sum[:], 1.0 / D, None, ALU.mult))
            for i in range(4):
                V.tensor_scalar(zc[:, i, :], w0_sb[:, i, :], z_sum[:, i:i + 1], None, ALU.subtract
                                ).then_inc(S["zc_ready"], 1)
            rank_lots(1, NORM_AFTER_LOTS - 1)
            dve.wait_ge(S["ortho_full"], NORM_PIECE + 1)
            chain.link(V.tensor_reduce(s_tot[:], pb[NORM_PIECE % 4][:, 0:4], AX.X, ALU.add))
            dve.sem_inc(S["ortho_free"], 1)
            invert(ROOT_NORM, s_tot[:], s_u[:])
            inverse_root(ROOT_NORM, s_tot[:], s_u[:], s_rn[:])
            chain.link(V.tensor_tensor(s_tot[:], s_tot[:], s_rn[:], ALU.mult))
            dve.sem_inc(S["inverse_ready"], 1)
            inverse_root(ROOT_NORM2, s_tot[:], s_u[:], s_rrn[:])
            dve.sem_inc(S["norm_ready"], 1)
            rank_lots(NORM_AFTER_LOTS, LOTS - NORM_AFTER_LOTS)

            dve.wait_ge(S["totals_ready"], 1)
            chain.link(V.tensor_copy(block_edges[:], pb[RANK_BANK][:, 0:KEYS]))
            chain.link(V.tensor_tensor(block_edges[:], block_edges[:], pb[RANK_BANK + 1][:, 0:KEYS], ALU.add))
            chain.link(V.tensor_copy(block_db[:], iota[:]))
            chain.mark(V.tensor_scalar(block_sb[:], block_db[:], TPC - 1, None, ALU.bitwise_and))
            chain.link(V.tensor_scalar(block_db[:], block_db[:], NT.bit_length() - 1, None, ALU.logical_shift_right))
            chain.link(V.tensor_scalar(block_db[:], block_db[:], TPC - 1, None, ALU.bitwise_and))
            chain.link(V.tensor_tensor(block_cap[:], block_sb[:], block_db[:], ALU.is_equal))
            chain.link(V.tensor_scalar(block_cap[:], block_cap[:], float(P), float(2 * P), ALU.mult, ALU.add))
            chain.link(V.tensor_tensor(block_cap[:], block_edges[:], block_cap[:], ALU.is_gt))
            chain.link(V.tensor_reduce(over_max[:], block_cap[:], AX.X, ALU.max))
            chain.link(V.tensor_copy(overfull[:], over_max[:]))
            dve.sem_inc(S["overfull_ready"], 1)
            overfull_dve = dve.value_load(overfull[0:1, 0:1], min_val=0, max_val=1)

            with dve.If(overfull_dve > 0):
                general = Chain(dve, S["g_dve"])
                dve.wait_ge(S["ortho_free"], ORTHO_PIECES)
                V.memset(g_zero[:], 0.0).then_inc(S["g_consts_ready"], 1)
                V.memset(g_attr[:], 0.0).then_inc(S["g_consts_ready"], 1)
                V.tensor_copy(g_iota[:, 0:KEYS], iota[:]).then_inc(S["g_consts_ready"], 1)
                V.tensor_scalar(g_iota[:, KEYS:2 * KEYS], iota[:], float(KEYS), None, ALU.add).then_inc(S["g_consts_ready"], 1)
                dve.wait_ge(S["g_consts_ready"], 4)
                dve.wait_ge(S["g_edges_ld"], 48)
                for name, free in (("g_used", 1), ("g_out", 1), ("g_stored", 32), ("g_attrs_stored", 16)):
                    dve.sem_inc(S[name], free)
                general.link(V.tensor_copy(g_src[:], g_src_i[:]))
                general.link(V.tensor_copy(g_dst[:], g_dst_i[:]))
                with general.loop(NCH, 2 + NT) as ch:
                    with general.loop(NT, 1) as t:
                        with dve.Fori(0, PARTS) as part:
                            dve.wait_ge(S["g_used"], part + t * PARTS + ch * (NT * PARTS) + 1)
                            for j in range(PART):
                                c = bass.ds(part * PART + j, 1)
                                V.tensor_scalar(g_src_oh[:, j, :], g_iota[:, 0:P], g_src[:, c], None, ALU.is_equal)
                                V.tensor_scalar(g_dst_oh[:, j, :], g_iota[:], g_dst[:, c], None, ALU.is_equal)
                                last = V.tensor_scalar(g_weight_oh[:, j, :], g_iota[:], g_dst[:, c], g_w[:, c],
                                                       ALU.is_equal, ALU.mult)
                            last.then_inc(S["g_oh_ready"], 1)
                        dve.wait_ge(S["g_used"], t * PARTS + ch * (NT * PARTS) + PARTS + 1)
                        dve.wait_ge(S["g_stored"], 32 * t + (32 * NT) * ch + 32)
                        V.tensor_copy(g_counts[:], pb[0][:])
                        V.tensor_copy(g_weights[:], pb[1][:]).then_inc(S["g_out"], 1)
                        general.link(V.tensor_scalar(g_src[:], g_src[:], float(-P), None, ALU.add))
                    general.link(V.tensor_scalar(g_src[:], g_src[:], float(N), None, ALU.add))
                    general.link(V.tensor_scalar(g_dst[:], g_dst[:], float(-CW), None, ALU.add))
                general.link(V.tensor_scalar(g_dst[:], g_dst[:], float(N), None, ALU.add))
                dve.wait_ge(S["g_stored"], 32 * (STEPS + 1))
                with general.loop(NCH, 1) as ch:
                    with dve.Fori(0, PARTS) as part:
                        dve.wait_ge(S["g_used"], part + ch * PARTS + STEPS * PARTS + 1)
                        for j in range(PART):
                            last = V.tensor_scalar(g_dst_oh[:, j, :], g_iota[:], g_dst[:, bass.ds(part * PART + j, 1)],
                                                   None, ALU.is_equal)
                        last.then_inc(S["g_oh_ready"], 1)
                    dve.wait_ge(S["g_used"], ch * PARTS + (STEPS + 1) * PARTS + 1)
                    dve.wait_ge(S["g_attrs_stored"], 16 * ch + 16)
                    V.tensor_copy(g_weights[:], pb[2][:]).then_inc(S["g_out"], 1)
                    general.link(V.tensor_scalar(g_dst[:], g_dst[:], float(-CW), None, ALU.add))
                dve.wait_ge(S["g_attrs_stored"], 16 * (NCH + 1))

            dve.wait_ge(S["ld_recs"], 16)
            dve.wait_ge(S["ortho_free"], ORTHO_PIECES)
            chain.mark(V.tensor_copy(dst_keep[:], recs[:, :, 1]))
            for i in range(5):
                chain.mark(V.tensor_copy(fields[:, i, :], recs[:, :, i]))
            chain.mark(V.tensor_copy(iota_group[:], iota[:, 0:P].rearrange("p (a d) -> p a d", d=1).to_broadcast([P, P, GROUP])))
            chain.settle()
            dve.sem_inc(S["oh_used"], OH_RING)
            with dve.Fori(0, NCH) as ch:
                for g in range(NT * GROUPS):
                    dve.wait_ge(S["oh_used"], ch * (NT * GROUPS) + g + 1)
                    rows = oh[:, g % OH_RING, :, :, :]
                    group = bass.ds(ch * (NT * ST) + g * GROUP, GROUP)

                    def spread(first, count):
                        return fields[:, first:first + count, group].rearrange("p a (b d) -> p a b d", b=1).to_broadcast(
                            [P, count, P, GROUP])

                    V.tensor_tensor(rows[:, 0:2, :, :], iota_group[:].rearrange("p (a b) d -> p a b d", a=1).to_broadcast(
                        [P, 2, P, GROUP]), spread(0, 2), ALU.is_equal).then_inc(S["places_ready"], 1)
                    dve.wait_ge(S["places_ready"], ch * (NT * GROUPS) + g + 1)
                    V.tensor_tensor(rows[:, 2:5, :, :], rows[:, 1:2, :, :].to_broadcast([P, 3, P, GROUP]), spread(2, 3),
                                    ALU.mult).then_inc(S["oh_ready"], 1)

            def batch_norm(no, gamma, beta, copied):
                for ch in range(NCH):
                    dve.wait_ge(S["dense_copied"], copied - (NCH - 1 - ch) * FT)
                    for f in range(FT):
                        chain.mark(V.bn_stats(bn_st[:, f, ch, :], featT[:, f, ch * CW:(ch + 1) * CW]))
                chain.settle()
                for f in range(FT):
                    chain.link(V.bn_aggr(bn_mv[:, f, :], bn_st[:, f, :, :]))
                chain.link(V.tensor_scalar(bn_v[:], bn_mv[:, :, 1], EPS, None, ALU.add))
                invert(no, bn_v[:], bn_u[:])
                inverse_root(no, bn_v[:], bn_u[:], bn_sc[:])
                chain.link(V.tensor_tensor(bn_sc[:], bn_sc[:], cols[gamma][:], ALU.mult))
                chain.link(V.scalar_tensor_tensor(bn_bi[:], bn_mv[:, :, 0], -1.0, bn_sc[:], ALU.mult, ALU.mult))
                chain.link(V.tensor_tensor(bn_bi[:], bn_bi[:], cols[beta][:], ALU.add))
                dve.sem_inc(S["bn_ready"], 1)

            def leaky(ch):
                dve.wait_ge(S["z_ready"], ch + 1)
                for f in range(FT):
                    last = V.scalar_tensor_tensor(ybuf[:, f, :], ybuf[:, f, :], SLOPE, ybuf[:, f, :], ALU.mult, ALU.max)
                last.then_inc(S["y_ready"], 1)

            def post(layer, ch, next_ch=None):

                def residual(q):
                    t = tile_no(layer, ch, q)
                    x_q, z = xr[:, q, :], y_bank(layer, q)[:]
                    if layer < 2:
                        dve.wait_ge(S["t1_full"], t + 1 + TPC)
                        dve.wait_ge(s_xin[q], 16 * (LOADS[layer] * NCH + 1) + ch * 16)
                    elif layer == 2:
                        dve.wait_ge(S["y_step"], ch * HT + HT + 4)
                    else:
                        dve.wait_ge(S["dense_full"], ch * FT + (layer - 1) * NCH * FT + q + 1)
                    if layer == 3:
                        dve.wait_ge(S["t2_full"], t + 1)
                        dve.wait_ge(s_xout[q], 16 * (3 * NCH + 1))
                        chain.link(V.tensor_tensor(x_q, z, bias_rows[3][:], ALU.add))
                    elif layer == 1:
                        chain.link(V.scalar_tensor_tensor(x_q, x_q, 2.0, z, ALU.mult, ALU.add))
                    else:
                        chain.link(V.tensor_tensor(x_q, x_q, z, ALU.add))
                    dve.sem_inc(S["t1_free"], 1)
                    chain.mark(V.bn_stats(ln_st[:, q, :], x_q))

                def normed(q):
                    x_q = xr[:, q, :]
                    chain.mark(V.tensor_scalar(x_q, x_q, ln_mv[:, q, 0:1], ln_r[:, q:q + 1], ALU.subtract, ALU.mult))
                    if layer == 3:
                        chain.settle()
                        chain.link(V.tensor_tensor(x_q, x_q, lng_sb[:], ALU.mult))
                        chain.link(V.tensor_tensor(x_q, x_q, lnb_sb[:], ALU.add))
                        chain.mark(V.scalar_tensor_tensor(x_q, x_q, SLOPE, x_q, ALU.mult, ALU.max))
                    chain.settle()
                    dve.sem_inc(S["normed"], 1)

                def split(q):
                    nt = bass.ds(ch * TPC + q, 1)
                    x_q = xr[:, q, :]
                    direct = layer == 3 and isinstance(ch, int)
                    if layer in (0, 2) or direct:
                        hi, lo = (part[:, nt, :].rearrange("p a d -> p (a d)") for part in (x_hi, x_lo))
                    elif layer == 3:
                        hi, lo = hl[:, q % HL_RING, 0, :], hl[:, q % HL_RING, 1, :]
                        dve.wait_ge(s_xout[q], 16 * (3 * NCH + 1) + ch * 16)
                        if q < TPC - HL_RING:
                            dve.wait_ge(s_xout[q + HL_RING], 16 * (3 * NCH + 1) + ch * 16)
                        if q >= HL_RING:
                            dve.wait_ge(s_xout[q - HL_RING], 16 * (3 * NCH + 2) + ch * 16)
                    if direct and q == 0:
                        dve.wait_ge(S["agg_full"], 2 * NCH)
                    if layer == 0:
                        chain.link(V.tensor_copy(hi, x_q))
                        chain.link(V.tensor_tensor(lo, x_q, hi, ALU.subtract))
                    elif layer in (2, 3):
                        chain.link(V.tensor_scalar(hi, x_q, dinv[:, nt], None, ALU.mult))
                        chain.link(V.scalar_tensor_tensor(lo, x_q, dinv[:, nt], hi, ALU.mult, ALU.subtract))
                    dve.sem_inc(S["split_done"], 1)

                if layer in (2, 4):
                    for q in range(TPC):
                        x_q = xr[:, q, :]
                        dve.wait_ge(s_xin[q], 16 * (LOADS[layer] * NCH + 1) + ch * 16)
                        chain.mark(V.scalar_tensor_tensor(x_q, x_q, 2.0 if layer == 2 else 1.0, bias_rows[layer][:],
                                                          ALU.mult, ALU.add))
                    chain.settle()
                for q in range(TPC):
                    residual(q)
                chain.settle()
                dve.sem_inc(S["stats_ready"], 1)
                for q in range(TPC):
                    chain.mark(V.bn_aggr(ln_mv[:, q, :], ln_st[:, q, :]))
                chain.settle()
                chain.link(V.tensor_scalar(ln_v[:], ln_mv[:, :, 1], EPS, None, ALU.add))
                invert(None, ln_v[:], ln_u[:])
                inverse_root(ch + ROOT_LN[layer], ln_v[:], ln_u[:], ln_r[:])
                for q in range(TPC):
                    normed(q)
                if layer == 1 and next_ch is not None:
                    leaky(next_ch)
                for q in range(TPC):
                    split(q)

            LINKS = {0: 5, 1: 3, 2: 6, 3: 8, 4: 4}
            dve.sem_inc(S["t1_free"], TPC)
            dve.wait_ge(S["ld_par"], 16 * 6)
            batch_norm(ROOT_BN[0], "bn_g", "bn_b", 4 + NCH * FT)
            with chain.loop(NCH, (LINKS[0] + 1) * TPC + 6) as ch:
                post(0, ch)

            for ch in range(NCH):
                dve.wait_ge(S["deg_full"], ch + 1)
                chain.link(V.tensor_scalar(colscale[:, ch * CW:(ch + 1) * CW], pb[TPC + ch][:], 1.0, None, ALU.max))
                dve.sem_inc(S["deg_done"], 1)
                chain.link(V.reciprocal(colscale[:, ch * CW:(ch + 1) * CW], colscale[:, ch * CW:(ch + 1) * CW]))
            def aggregated(agg_no, dense_no, ch):
                dve.wait_ge(S["agg_full"], ch + agg_no + 1)
                dve.wait_ge(S["dense_full"], ch * FT + dense_no)
                for f in range(FT):
                    V.tensor_tensor(aggT[:, f, :], pb[f][:], colscale[:, ccols(ch)], ALU.mult).then_inc(S["agg_copied"], 1)

            for u in range(2):
                dve.wait_ge(S[f"attr_sent{u}"], 16 * LOT * ((LOTS + 1 - u) // 2))
            chain.link(V.tensor_copy(iota_group16[:], iota[:, 0:P].rearrange("p (a d) -> p a d", d=1).to_broadcast([P, P, GROUP])))
            with chain.loop(NCH, TPC) as ch:
                for t in range(NT):
                    dve.wait_ge(S["at_used"], ch * NT + t + 1)
                    places = dst_keep[:, bass.ds(ch * (NT * ST) + t * ST, ST)].rearrange("p (a b d) -> p a b d", a=GROUPS, b=1)
                    V.tensor_tensor(at_oh[:, t % 2, :, :, :], iota_group16[:].rearrange("p (a b) d -> p a b d", a=1).to_broadcast(
                        [P, GROUPS, P, GROUP]), places.to_broadcast([P, GROUPS, P, GROUP]), ALU.is_equal
                        ).then_inc(S["at_oh_ready"], 1)
                for q in range(TPC):
                    nt = bass.ds(ch * TPC + q, 1)
                    chain.mark(V.tensor_reduce(deg[:, nt], adj[:, nt, :], AX.X, ALU.add))
                aggregated(0, NCH * FT, ch)
                dve.wait_ge(S["at_used"], ch * NT + NT + 2)
                V.tensor_tensor(e2T[:, ccols(ch)], pb[4][:], colscale[:, ccols(ch)], ALU.mult).then_inc(S["e2_done"], 1)
            chain.settle()
            chain.mark(V.tensor_scalar(dpos[:], deg[:], 0.0, None, ALU.is_gt))
            chain.link(V.tensor_scalar(deg_v[:], deg[:], 1.0, None, ALU.max))
            invert(ROOT_DEG, deg_v[:], deg_u[:])
            inverse_root(ROOT_DEG, deg_v[:], deg_u[:], dinv[:])
            chain.link(V.tensor_tensor(dinv[:], dinv[:], dpos[:], ALU.mult))
            dve.wait_ge(S["dense_full"], 2 * NCH * FT)
            dve.wait_ge(S["e2_done"], NCH)
            with dve.If(overfull_dve > 0):
                dve.wait_ge(S["general_attrs_ld"], 16)
                V.tensor_tensor(e2T[:], e2T[:], colscale[:], ALU.mult).then_inc(S["g_dve"], 1)
            for t in range(NT):
                V.tensor_scalar(diag[:, t, :], ident[:], dinv[:, t:t + 1], -1.0, ALU.mult, ALU.mult
                                ).then_inc(S["diag_ready"], 1)
            batch_norm(ROOT_BN[1], "g1", "be1", 4 + 2 * NCH * FT)
            dve.wait_ge(S["diag_full"], 1)
            for ch in range(NCH):
                V.tensor_copy(colscale[:, ch * CW:(ch + 1) * CW], pb[ch][:]).then_inc(S["diag_done"], 1)
            leaky(0)
            with chain.loop(NCH - 1, (LINKS[1] + 1) * TPC + 6) as ch:
                post(1, ch, ch + 1)
            post(1, NCH - 1)
            dve.wait_ge(S["ld_b2"], 16)
            with chain.loop(NCH, (LINKS[2] + 1) * TPC + 6) as ch:
                post(2, ch)
            dve.wait_ge(S["ld_c1"], 16 * 5)
            for layer, before in ((3, 1), (4, 2)):
                if layer == 4:
                    dve.wait_ge(S["ld_c2_row"], 16)
                with chain.loop(NCH - 1, (LINKS[layer] + 1) * TPC + 6) as ch:
                    aggregated(before * NCH, (before + 1) * NCH * FT, ch)
                    post(layer, ch)
                aggregated(before * NCH, (before + 1) * NCH * FT, NCH - 1)
                post(layer, NCH - 1)

        @block.tensor
        def _(pe):
            mm, tp = nc.tensor.matmul, nc.tensor.transpose
            pieces, ranks, slots = [0], [0], [0]

            def ranks_up_to(limit):
                while ranks[0] < min(limit, EDGE_TILES):
                    c = ranks[0]
                    ranks[0] += 1
                    bank = pb[RANK_BANK + c % 2][:, 0:KEYS]
                    pe.wait_ge(S["key_oh_ready"], c + 1)
                    pe.wait_ge(S["ranked"], c + 1)
                    mm(bank, no_tri[:], key_oh[:, (c + 2) % OH_RING, :], start=(c < 2), stop=True, skip_group_check=True)
                    mm(bank, tri[:], key_oh[:, c % OH_RING, :], start=False, stop=True,
                       skip_group_check=True).then_inc(S["rank_mm"], 1)

            def piece(products, needs=0):
                n = pieces[0]
                pieces[0] += 1
                if max(n - 3, needs) > 0:
                    pe.wait_ge(S["ortho_free"], max(n - 3, needs))
                products(pb[n % 4]).then_inc(S["ortho_full"], 1)

            def between():
                slots[0] += 1
                due = LOT + (EDGE_TILES - LOT) * slots[0] // RANKED_BY_PRODUCT
                ranks_up_to(min(due, NORM_AFTER_LOTS * LOT) if pieces[0] <= NORM_PIECE + 1 else due)

            def transposes(blocks):
                def go(bank):
                    for k, b in enumerate(blocks):
                        between()
                        last = tp(bank[:, k * P:(k + 1) * P], b, ident[:])
                    return last
                return go

            def product(lhs, rhs, i, extra=None, first=0):
                def go(bank):
                    if extra is not None:
                        mm(bank[:, first:], extra[0][:], extra[1][:, i, first:], start=True, stop=False)
                    for k in range(4):
                        between()
                        last = mm(bank[:, first:], lhs[:, k, i * P:(i + 1) * P], rhs[:, k, first:],
                                  start=(k == 0 and extra is None), stop=(k == 3))
                    return last
                return go

            def upper(lhs, rhs, needs=0, extra=None):
                for i in range(4):
                    piece(product(lhs, rhs, i, extra=extra, first=i * P), needs=needs)

            def mirror(m, first_piece):
                for i in range(1, 4):
                    piece(transposes([m[:, k, i * P:(i + 1) * P] for k in range(i)]), needs=first_piece + i)

            def x0_transposes(t):
                piece(transposes([x0[:, t, f * P:(f + 1) * P] for f in range(FT)]))

            pe.wait_ge(S["tri_ready"], 2)
            ranks_up_to(LOT)
            pe.wait_ge(S["ident_ready"], 3)
            pe.wait_ge(S["mats_ready"], 3)
            pe.wait_ge(S["zc_ready"], 4)
            for i in range(4):
                piece(transposes([zc[:, i, k * P:(k + 1) * P] for k in range(4)]))

            def gram(i):
                def go(bank):
                    product(zcT, zcT, i, first=i * P)(bank)
                    return mm(bank[:, i * P:(i + 1) * P], eps_i[:], ident[:], start=False, stop=True, skip_group_check=True)
                return go

            for i in range(4):
                piece(gram(i), needs=4)
            mirror(s_n, 4)
            pe.wait_ge(S["squares_ready"], 4)
            piece(lambda bank: mm(bank[:, 0:4], ones32[:], sq_sum[:], start=True, stop=True), needs=NORM_PIECE)
            ranks_up_to(NORM_AFTER_LOTS * LOT)
            pe.wait_ge(S["s_scaled"], 4)
            n = pieces[0]

            def first_b(i):
                def go(bank):
                    mm(bank[:], mhalf_i[:], s_n[:, i, :], start=True, stop=True)
                    return mm(bank[:, i * P:(i + 1) * P], threehalf_i[:], ident[:], start=False, stop=True, skip_group_check=True)
                return go

            for i in range(4):
                piece(first_b(i))
            pe.wait_ge(S["ld_x"], 16)
            b = [b_ping, b_pong]
            for it in range(4):
                n = pieces[0]
                upper(b[0], b[0], needs=n)
                upper(b[0], s_n)
                mirror(b_sq, n)
                x0_transposes(4 * it)
                x0_transposes(4 * it + 1)
                mirror(b_s, n + 4)
                n = pieces[0]
                x0_transposes(4 * it + 2)
                upper(b_sq, b_s, needs=n, extra=(threehalf_i, b[0]))
                x0_transposes(4 * it + 3)
                mirror(b[1], n + 1)
                b.reverse()
            n = pieces[0]
            for i in range(4):
                piece(product(b[0], zc, i), needs=n)
            assert pieces[0] == ORTHO_PIECES
            ranks_up_to(EDGE_TILES)

            pe.wait_ge(S["ranked"], EDGE_TILES + 2)
            for c in range(EDGE_TILES - 2, EDGE_TILES):
                last = mm(pb[RANK_BANK + c % 2][:, 0:KEYS], no_tri[:], key_oh[:, c % OH_RING, :], start=False, stop=True,
                          skip_group_check=True)
            last.then_inc(S["totals_ready"], 1)
            pe.wait_ge(S["overfull_ready"], 1)
            pe.wait_ge(S["ortho_free"], ORTHO_PIECES)

            overfull_pe = pe.value_load(overfull[0:1, 0:1], min_val=0, max_val=1)
            with pe.If(overfull_pe > 0):
                pe.wait_ge(S["g_consts_ready"], 4)
                with pe.Fori(0, STEPS) as i:
                    pe.wait_ge(S["g_out"], i + 1)
                    for bank in pb[0:2]:
                        mm(bank[:], g_zero[:, 0:P], g_zero[:], start=True, stop=True, skip_group_check=True)
                    with pe.Fori(0, PARTS) as part:
                        pe.wait_ge(S["g_oh_ready"], part + i * PARTS + 1)
                        for j in range(PART):
                            mm(pb[0][:], g_src_oh[:, j, :], g_dst_oh[:, j, :], start=False, stop=True, skip_group_check=True)
                            last = mm(pb[1][:], g_src_oh[:, j, :], g_weight_oh[:, j, :], start=False, stop=True,
                                      skip_group_check=True)
                        last.then_inc(S["g_used"], 1)
                with pe.Fori(0, NCH) as ch:
                    pe.wait_ge(S["g_out"], ch + STEPS + 1)
                    mm(pb[2][:], g_zero[:, 0:P], g_zero[:], start=True, stop=True, skip_group_check=True)
                    with pe.Fori(0, PARTS) as part:
                        pe.wait_ge(S["g_attr_ld"], 16 * part + (16 * PARTS) * ch + 16)
                        pe.wait_ge(S["g_oh_ready"], part + ch * PARTS + STEPS * PARTS + 1)
                        for j in range(PART):
                            last = mm(pb[2][:], g_attr[:, j, :], g_dst_oh[:, j, :], start=False, stop=True, skip_group_check=True)
                        last.then_inc(S["g_used"], 1)

            pe.wait_ge(S["ld_self"], 16)

            def aggregate_x0(ch, t):
                pe.wait_ge(S["adj_final"], ch * NT + t + 1)
                for f in range(FT):
                    last = mm(pb[f][:], x0[:, t, f * P:(f + 1) * P], aw[:, t % AW_RING, :], start=(t == 0), stop=(t == NT - 1))
                last.then_inc(S["agg_step"], 1)

            def dense(bank, pairs, f):
                n = 0
                for w, feat in pairs:
                    for k in range(FT):
                        last = mm(bank[:], w[:, k, f * P:(f + 1) * P], feat(k), start=(n == 0), stop=(n == 2 * FT - 1))
                        n += 1
                last.then_inc(S["dense_full"], 1)

            with pe.Fori(0, NCH) as ch:
                pe.wait_ge(S["dense_copied"], ch * FT + 4)
                for t in range(NT):
                    pe.wait_ge(S["adj_evac"], ch * NT + t + 1)
                    counts, weights = pb[4 + 2 * (t % 2)], pb[5 + 2 * (t % 2)]
                    for s in range(ST):
                        g = t * GROUPS + s // GROUP
                        if s % GROUP == 0:
                            pe.wait_ge(S["oh_ready"], ch * (NT * GROUPS) + g + 1)
                        rows = oh[:, g % OH_RING, :, :, s % GROUP]
                        block_cols = s // 2 if s < 2 * TPC else t % TPC
                        c = slice(block_cols * P, (block_cols + 1) * P)
                        mm(counts[:, c], rows[:, 0, :], rows[:, 1, :], start=(s == 0), stop=True, skip_group_check=True)
                        for k in range(3):
                            last = mm(weights[:, c], rows[:, 0, :], rows[:, 2 + k, :], start=(s == 0 and k == 0),
                                      stop=True, skip_group_check=True)
                        if s % GROUP == GROUP - 1:
                            last.then_inc(S["oh_used"], 1)
                    if t >= 1:
                        aggregate_x0(ch, t - 1)
                aggregate_x0(ch, NT - 1)
                pe.wait_ge(S["agg_copied"], ch * FT + FT)
                pe.wait_ge(S["adj_evac"], ch * NT + NT + 2)
                for f in range(FT):
                    dense(pb[4 + f], ((t_sb, lambda k: aggT[:, k, :]), (self_sb, lambda k: featT[:, k, ccols(ch)])), f)

            def there(layer, ch, q):
                if q == 0:
                    pe.wait_ge(S["y_ready"], ch + layer * NCH + 1)
                pe.wait_ge(S["t1_free"], bank_free(layer, ch, q))
                for f in range(FT):
                    last = tp(y_bank(layer, q)[:, f * P:(f + 1) * P], ybuf[:, f, q * P:(q + 1) * P], ident[:])
                last.then_inc(S["t1_full"], 1)

            def back(layer, ch, q):
                pe.wait_ge(S["normed"], tile_no(layer, ch, q) + 1)
                pe.wait_ge(S["t2_done"], bank_free(layer, ch, q))
                for f in range(FT):
                    last = tp(t2_bank(layer, q)[:, f * P:(f + 1) * P], xr[:, q, f * P:(f + 1) * P], ident[:])
                last.then_inc(S["t2_full"], 1)

            def posts(layer):
                for q in range(TPC):
                    there(layer, 0, q)
                with pe.Fori(0, NCH - 1) as ch:
                    for q in range(TPC):
                        back(layer, ch, q)
                    for q in range(TPC):
                        there(layer, ch + 1, q)
                for q in range(TPC):
                    back(layer, NCH - 1, q)

            pe.wait_ge(S["dense_copied"], 4 + NCH * FT)
            posts(0)
            pe.wait_ge(S["t2_done"], NT + TPC)
            for ch in range(NCH):
                for t in range(NT):
                    last = mm(pb[TPC + ch][:], ones16[:], adj[:, t, ch * CW:(ch + 1) * CW], start=(t == 0), stop=(t == NT - 1))
                last.then_inc(S["deg_full"], 1)

            def aggregate(ch, copied, between=()):
                pe.wait_ge(S["agg_copied"], ch * FT + copied)
                for t in range(NT):
                    for f in range(FT):
                        mm(pb[f][:], x_hi[:, t, f * P:(f + 1) * P], adj[:, t, ccols(ch)], start=(t == 0), stop=False)
                        last = mm(pb[f][:], x_lo[:, t, f * P:(f + 1) * P], adj[:, t, ccols(ch)], start=False, stop=(t == NT - 1))
                    if t in between:
                        between[t]()
                last.then_inc(S["agg_full"], 1)

            pe.wait_ge(S["deg_done"], NCH)
            pe.wait_ge(S["split_done"], NT + TPC)
            pe.wait_ge(S["ld_l1"], 32)
            with pe.Fori(0, NCH) as ch:
                pe.wait_ge(S["dense_copied"], ch * FT + NCH * FT + 4)

                def aggregate_attributes(t):
                    pe.wait_ge(S["at_split"], ch * NT + t + 1 + AT_RING)
                    pe.wait_ge(S["at_oh_ready"], ch * NT + t + 1)
                    for s in range(ST):
                        block_cols = s // 2 if s < 2 * TPC else t % TPC
                        last = mm(pb[4][:, block_cols * P:(block_cols + 1) * P],
                                  at_parts[:, t % 2, s, :, :].rearrange("p a b -> p (a b)"),
                                  at_oh[:, t % 2, s // GROUP, :, s % GROUP],
                                  start=(t == 0 and s == 0), stop=True, skip_group_check=True)
                    last.then_inc(S["at_used"], 1)

                aggregate(ch, NCH * FT, {t: (lambda t=t: aggregate_attributes(t)) for t in range(NT)})
                pe.wait_ge(S["agg_copied"], ch * FT + NCH * FT + FT)
                for f in range(FT):
                    if f == FT - 1:
                        pe.wait_ge(S["e2_done"], ch + 1)
                    dense(pb[4 + (f + 1) % FT], ((wl_sb, lambda k: aggT[:, k, :]), (wr_sb, lambda k: featT[:, k, ccols(ch)])), f)
            for ch in range(NCH):
                pe.wait_ge(S["diag_ready"], (ch + 1) * TPC)
                for q in range(TPC):
                    last = mm(pb[ch][:, q * P:(q + 1) * P], ones32[:], diag[:, ch * TPC + q, :],
                              start=True, stop=True, skip_group_check=True)
            last.then_inc(S["diag_full"], 1)
            pe.wait_ge(S["diag_done"], NCH)
            pe.wait_ge(S["dense_copied"], 4 + 2 * NCH * FT)
            posts(1)

            pe.wait_ge(S["ld_l2"], 16 * 4)
            pe.wait_ge(S["t2_done"], 2 * NT + TPC)

            def layer2(ch, last_ch):
                def hidden_to_out(i):
                    pe.wait_ge(S["h_ready"], ch * HT + i + 1 + 2)
                    if i == 0:
                        pe.wait_ge(S["t1_free"], tile_no(2, ch) + TPC)
                    for q in range(TPC):
                        last = mm(y_bank(2, q)[:], h_ring[:, i % 4, q * P:(q + 1) * P], w2_sb[:, i, :],
                                  start=(i == 0), stop=(i == HT - 1))
                    last.then_inc(S["y_step"], 1)

                for i in range(HT):
                    pe.wait_ge(S["h_ready"], ch * HT + i + 1)
                    for k in range(FT):
                        mm(pb[4 + i % 2][:], w1_sb[:, k, i * P:(i + 1) * P], featT[:, k, ccols(ch)], start=(k == 0), stop=False)
                    mm(pb[4 + i % 2][:], w1e_sb[:, i * P:(i + 1) * P], e2T[:, ccols(ch)], start=False, stop=True
                       ).then_inc(S["h_full"], 1)
                    if i >= 1:
                        hidden_to_out(i - 1)
                    if last_ch is not None and BACK_AT <= i < BACK_AT + TPC:
                        back(2, last_ch, i - BACK_AT)
                hidden_to_out(HT - 1)

            layer2(0, None)
            with pe.Fori(0, NCH - 1) as last_ch:
                layer2(last_ch + 1, last_ch)
            for q in range(TPC):
                back(2, NCH - 1, q)

            pe.wait_ge(S["ld_c1"], 16 * 5)
            pe.wait_ge(S["ld_c2"], 16 * 2)
            for layer, w in ((3, c1_sb), (4, c2_sb)):
                if layer == 3:
                    pe.wait_ge(S["split_done"], 3 * NT + TPC)
                else:
                    pe.wait_ge(S["hl_loaded"], 32)
                    pe.wait_ge(S["split_done"], 4 * NT + TPC)
                pe.wait_ge(S["t2_done"], layer * NT + TPC)

                def convolution(ch, last_ch):
                    between = {}
                    if layer == 3 and last_ch is not None:
                        for q in range(TPC):
                            between[8 + q] = lambda q=q: back(3, last_ch, q)
                    aggregate(ch, (layer - 1) * NCH * FT, between)
                    pe.wait_ge(S["x_copied"], ch * FT + (layer - 3) * NCH * FT + FT)
                    pe.wait_ge(S["agg_copied"], ch * FT + (layer - 1) * NCH * FT + FT)
                    for q in range(TPC):
                        pe.wait_ge(S["t1_free"], tile_no(layer, ch, q) - 1 + TPC)
                        nodes = slice(q * P, (q + 1) * P)
                        for k in range(FT):
                            mm(y_bank(layer, q)[:], ybuf[:, k, nodes], w[:, 0, k, :], start=(k == 0), stop=False)
                        for k in range(FT):
                            last = mm(y_bank(layer, q)[:], aggT[:, k, nodes], w[:, 1, k, :], start=False, stop=(k == FT - 1))
                        last.then_inc(S["dense_full"], 1)

                convolution(0, None)
                with pe.Fori(0, NCH - 1) as last_ch:
                    convolution(last_ch + 1, last_ch)
                if layer == 3:
                    for q in range(TPC):
                        back(3, NCH - 1, q)


_INS = ['x', 'src', 'dst', 'edge_attr_64', 'edge_weight', 'L0_gnn_weight', 'L0_gnn_self_weight', 'L0_gnn_bn_gamma',
        'L0_gnn_bn_beta', 'L1_gnn_W_l', 'L1_gnn_b_l', 'L1_gnn_W_r', 'L1_gnn_gamma', 'L1_gnn_beta', 'L2_gnn_W1',
        'L2_gnn_b1', 'L2_gnn_W2', 'L2_gnn_b2', 'L3_gnn_W1_0', 'L3_gnn_W1_1', 'L3_gnn_b1', 'L3_gnn_gamma',
        'L3_gnn_beta', 'L3_gnn_W2_0', 'L3_gnn_W2_1', 'L3_gnn_b2']


def kernel(**inputs):
    import numpy as _np
    import concourse.bacc as _bacc
    from concourse import mybir as _mybir
    from concourse.bass_utils import run_bass_kernel_spmd as _run

    nc = _bacc.Bacc("TRN2", target_bir_lowering=False, num_devices=1)
    arrays, args = {}, []
    for name in _INS:
        a = _np.ascontiguousarray(inputs[name])
        arrays[f"in_{name}"] = a
        args.append(nc.dram_tensor(f"in_{name}", a.shape, _mybir.dt.from_np(a.dtype), kind="ExternalInput").ap())
    out = nc.dram_tensor("out_0", (N, D), FP32, kind="ExternalOutput").ap()
    gnn_kernel(nc, *args, out)
    r = _run(nc, [arrays], core_ids=[0])
    return r.results[0]["out_0"]
```

```python
from contextlib import contextmanager

import concourse.bass as bass
from concourse import mybir

FP32 = mybir.dt.float32
FP16 = mybir.dt.float16
BF16 = mybir.dt.bfloat16
I32 = mybir.dt.int32
U32 = mybir.dt.uint32
ALU = mybir.AluOpType
ACT = mybir.ActivationFunctionType
AX = mybir.AxisListType

P = 128
N, D, E = 2048, 512, 34816
HID, EDGE_IN = 1024, 64
NT = N // P
FT = D // P
HT = HID // P
CW = 512
NCH = N // CW
TPC = CW // P
EDGE_TILES = E // P
LOT = 16
LOTS = EDGE_TILES // LOT
KEYS = NT * NT
ST = 2 * TPC + 1
STEPS = NCH * NT
SLOT_TILES = STEPS * ST
GROUP = 3
GROUPS = ST // GROUP
OH_RING = 4
REC = 4
AW_RING = 4
DIAG_RING = 3
HL_RING = 3
BACK_AT = 2
AT_RING = 4
ZERO_COLS = 2048
ZERO_DMAS = SLOT_TILES * EDGE_IN // ZERO_COLS
PART = 8
PARTS = EDGE_TILES // PART
NORM_AFTER_LOTS = 3
SPLIT_AFTER_LOTS = 8
SYM = 4 + 3
NORM_PIECE = 4 + SYM
ORTHO_PIECES = NORM_PIECE + 1 + 4 + 4 * (3 * SYM + 4) + 4
RANKED_BY_PRODUCT = 320
HALF_PIECES = NORM_PIECE + 1 + 4 + 2 * (3 * SYM + 4)
EPS = 1e-5
SLOPE = 0.01


class Chain:

    def __init__(self, engine, sem):
        self.engine, self.sem, self.base, self.n = engine, sem, 0, 0

    def link(self, instruction):
        instruction.then_inc(self.sem, 1)
        self.n += 1
        self.engine.wait_ge(self.sem, self.base + self.n)

    def settle(self):
        self.engine.wait_ge(self.sem, self.base + self.n)

    @contextmanager
    def loop(self, times, per):
        base, n = self.base, self.n
        with self.engine.Fori(0, times) as i:
            self.base, self.n = base + n + i * per, 0
            yield i
            assert self.n == per, (self.n, per)
        self.base, self.n = base, n + times * per

    def mark(self, instruction):
        instruction.then_inc(self.sem, 1)
        self.n += 1


def gnn_kernel(nc, x, src, dst, edge_attr, edge_weight, w0, self_w, bn_g, bn_b, wl, bl, wr, g1, be1,
               w1, b1, w2, b2, c1a, c1b, c1bias, ln_g, ln_b, c2a, c2b, c2bias, out, dbg=()):
    rec_table = nc.dram_tensor("rec_table", (P * SLOT_TILES, REC), FP16, kind="Internal").ap()
    attr_table = nc.dram_tensor("attr_table", (P * SLOT_TILES, EDGE_IN), FP32, kind="Internal").ap()
    x_after = [nc.dram_tensor(f"x_after_{i}", (N, D), FP32, kind="ExternalOutput" if dbg else "Internal").ap() for i in range(3)]
    h_parts = nc.dram_tensor("h_parts", (NT, P, 2, D), FP16, kind="Internal").ap()

    all_counts = nc.dram_tensor("all_counts", (STEPS, P, CW), FP16, kind="Internal").ap()
    all_weights = nc.dram_tensor("all_weights", (STEPS, P, 2, CW), FP16, kind="Internal").ap()
    all_attrs = nc.dram_tensor("all_attrs", (NCH, P, CW), FP32, kind="Internal").ap()

    KB = 1024
    at = [(nc.sbuf_base + 31) // 32 * 32]

    def region(kb):
        start = at[0]
        at[0] += int(kb * KB)
        assert at[0] <= nc.sbuf_top, at[0] - nc.sbuf_top
        return start

    def sb(name, shape, dt, offset):
        return nc.alloc_sbuf_tensor_at(name, shape, dt, offset=offset)

    r_feat, r_adj, r_node = region(32), region(64), region(32)
    r_wa, r_wb = region(20), region(16)
    r_agg, r_y, r_xr, r_e2, r_cs = region(8), region(8), region(8), region(8), region(8)

    def small(name, shape, dt):
        size = {FP32: 4, I32: 4, U32: 4, FP16: 2, BF16: 2}[dt]
        for n in shape[1:]:
            size *= n
        start = at[0]
        at[0] += (size + 31) // 32 * 32
        assert at[0] <= nc.sbuf_top, at[0] - nc.sbuf_top
        return sb(name, shape, dt, start)

    featT = sb("featT", [P, FT, N], FP32, r_feat)
    adj = sb("adj", [P, NT, N], FP16, r_adj)
    x_hi = sb("x_hi", [P, NT, D], FP16, r_node)
    x_lo = sb("x_lo", [P, NT, D], FP16, r_node + 16 * KB)
    x_stage = sb("x_stage", [P, NT // 2, D], FP32, r_agg)
    aggT = sb("aggT", [P, FT, CW], FP32, r_agg)
    ybuf = sb("ybuf", [P, FT, CW], FP32, r_y)
    xr = sb("xr", [P, TPC, D], FP32, r_xr)
    colscale = sb("colscale", [P, N], FP32, r_cs)
    zc, zcT, s_n, b_ping, b_pong, b_sq, b_s, w0_sb = (
        sb(n, [P, 4, D], FP32, r_adj + 8 * KB * i)
        for i, n in enumerate(("zc", "zcT", "s_n", "b_ping", "b_pong", "b_sq", "b_s", "w0_sb")))
    col = EDGE_TILES * 4
    src_i, dst_i, sb_i, db_i, dbl_i, sbl_i = (
        sb(n, [P, EDGE_TILES], I32, r_wa + col * i)
        for i, n in enumerate(("src_i", "dst_i", "sb_i", "db_i", "dbl_i", "sbl_i")))
    key, base, top, third, w_e = (
        sb(n, [P, EDGE_TILES], FP32, r_wa + col * (6 + i))
        for i, n in enumerate(("key", "base", "top", "third", "w_e")))
    rec = sb("rec", [P, EDGE_TILES, REC], FP16, r_wa + col * 11)
    slot = sb("slot", [P, EDGE_TILES], U32, r_wa + 18560)
    tri, no_tri = (sb(n, [P, P], BF16, r_cs + 256 * i) for i, n in enumerate(("tri", "no_tri")))
    eps_i, mhalf_i, threehalf_i = (
        sb(n, [P, P], FP32, r_cs + 512 * (1 + i)) for i, n in enumerate(("eps_i", "mhalf_i", "threehalf_i")))
    ranked_junk = sb("ranked_junk", [P, 2, KEYS], BF16, r_cs + 2048)
    rank = sb("rank", [P, LOT], FP32, r_cs + 3072)
    past1 = sb("past1", [P, LOT], FP32, r_cs + 3072 + 64)
    past2 = sb("past2", [P, LOT], FP32, r_cs + 3072 + 128)
    row = sb("row", [P, LOT], FP32, r_cs + 3072 + 192)
    z_sum = sb("z_sum", [P, 4], FP32, r_cs + 3584)
    sq_sum = sb("sq_sum", [P, 4], FP32, r_cs + 3648)
    s_tot = sb("s_tot", [P, 1], FP32, r_cs + 3680)
    s_rn = sb("s_rn", [P, 1], FP32, r_cs + 3712)
    s_u = sb("s_u", [P, 1], FP32, r_cs + 3776)
    sq_junk = sb("sq_junk", [P, D], FP32, r_cs + 4096)
    key_oh = sb("key_oh", [P, OH_RING, KEYS], BF16, r_cs + 6144)
    block_sb, block_db = (sb(n, [P, KEYS], I32, r_cs + 4096 + KB * i) for i, n in enumerate(("block_sb", "block_db")))
    block_cap, block_edges = (sb(n, [P, KEYS], FP32, r_cs + 6144 + KB * i) for i, n in enumerate(("block_cap", "block_edges")))
    over_max = sb("over_max", [P, 1], FP32, r_cs + 3776 + 32)
    pad = sb("pad", [P, SLOT_TILES, REC], FP16, r_e2)
    zeros = sb("zeros", [P, ZERO_COLS], FP32, r_xr)
    at_general = [r_adj]

    def general(name, shape, dt, size):
        at_general[0] += size
        return sb(name, shape, dt, at_general[0] - size)

    g_src_oh = general("g_src_oh", [P, PART, P], FP32, 4 * KB)
    g_dst_oh = general("g_dst_oh", [P, PART, CW], FP32, 16 * KB)
    g_weight_oh = general("g_weight_oh", [P, PART, CW], FP32, 16 * KB)
    g_attr = general("g_attr", [P, PART, P], FP32, 4 * KB)
    g_iota = general("g_iota", [P, CW], FP32, 2 * KB)
    g_zero = general("g_zero", [P, CW], FP32, 2 * KB)
    g_weights = general("g_weights", [P, 2, CW], FP16, 2 * KB)
    g_attr_sums = general("g_attr_sums", [P, CW], FP32, 2 * KB)
    g_counts = general("g_counts", [P, CW], FP16, 1 * KB)
    g_src_i, g_dst_i, g_w, g_src, g_dst = (
        general(n, [P, EDGE_TILES], dt, col) for n, dt in
        (("g_src_i", I32), ("g_dst_i", I32), ("g_w", FP32), ("g_src", FP32), ("g_dst", FP32)))
    oh = sb("oh", [P, OH_RING, REC, P, GROUP], FP16, r_wa)
    fields = sb("fields", [P, REC, SLOT_TILES], FP16, r_cs)
    iota_group = sb("iota_group", [P, P, GROUP], FP16, r_cs + 6 * KB)
    recs = sb("recs", [P, SLOT_TILES, REC], FP16, r_xr)
    dst_keep = sb("dst_keep", [P, SLOT_TILES], FP16, r_wa + 17 * KB)
    aw = sb("aw", [P, AW_RING, 2, CW], FP16, r_y)
    stage = sb("stage", [P, 2, LOT, EDGE_IN], FP32, r_e2)
    t_sb = sb("t_sb", [P, 4, D], FP32, r_wb)
    self_sb = sb("self_sb", [P, 4, D], FP32, r_wb + 8 * KB)
    x_post = sb("x_post", [P, TPC, D], FP32, r_wb + 8 * KB)
    wl_sb = sb("wl_sb", [P, 4, D], FP32, r_wa)
    wr_sb = sb("wr_sb", [P, 4, D], FP32, r_wb)
    at_oh = sb("at_oh", [P, 2, GROUPS, P, GROUP], FP16, r_wa + 8 * KB)
    iota_group16 = sb("iota_group16", [P, P, GROUP], FP16, r_wa + 19 * KB - 512)
    at_parts = sb("at_parts", [P, 2, ST, 2, EDGE_IN], FP16, r_wa + 8 * KB + 4608)
    at_in = sb("at_in", [P, AT_RING, ST, EDGE_IN], FP32, r_y)
    e2T = sb("e2T", [P, N], FP32, r_e2)
    diag = sb("diag", [P, DIAG_RING, TPC, P], FP32, r_y + 2 * KB)
    w1_sb = sb("w1_sb", [P, 4, HID], FP32, r_wa)
    w1e_sb = sb("w1e_sb", [P, HID], FP32, r_wa + 16 * KB)
    w2_sb = sb("w2_sb", [P, HT, D], FP32, r_wb)
    h_ring = sb("h_ring", [P, 4, CW], FP32, r_agg)
    c1_sb = sb("c1_sb", [P, 2, 4, D], FP32, r_wa)
    lng_sb = sb("lng_sb", [P, D], FP32, r_wa + 16 * KB)
    lnb_sb = sb("lnb_sb", [P, D], FP32, r_wa + 18 * KB)
    c2_sb = sb("c2_sb", [P, 2, 4, D], FP32, r_wb)
    hl = sb("hl", [P, HL_RING, 2, D], FP16, r_e2)
    bias_rows = {2: sb("b2_row", [P, D], FP32, r_y), 3: sb("c1_row", [P, D], FP32, r_e2 + 6 * KB),
                 4: sb("c2_row", [P, D], FP32, r_wa + 16 * KB)}
    ident = small("ident", [P, P], FP32)
    iota = small("iota", [P, KEYS], BF16)
    ones16 = small("ones16", [P, P], FP16)
    ones32 = small("ones32", [P, P], FP32)
    cols = {n: small(n + "_c", [P, 4], FP32) for n in ("bn_g", "bn_b", "bl", "g1", "be1")}
    b1_sb = small("b1_c", [P, HT], FP32)
    bn_st = small("bn_st", [P, FT, NCH, 6], FP32)
    bn_mv = small("bn_mv", [P, FT, 2], FP32)
    bn_sc = small("bn_sc", [P, FT], FP32)
    bn_bi = small("bn_bi", [P, FT], FP32)
    ln_st = small("ln_st", [P, TPC, 6], FP32)
    ln_mv = small("ln_mv", [P, TPC, 2], FP32)
    ln_v, ln_r, ln_u = (small(n, [P, TPC], FP32) for n in ("ln_v", "ln_r", "ln_u"))
    bn_v, bn_u = (small(n, [P, FT], FP32) for n in ("bn_v", "bn_u"))
    s_rrn = small("s_rrn", [P, 1], FP32)
    overfull = small("overfull", [P, 1], I32)
    deg = small("deg", [P, NT], FP32)
    dinv = small("dinv", [P, NT], FP32)
    dpos = small("dpos", [P, NT], FP32)
    deg_v, deg_u = (small(n, [P, NT], FP32) for n in ("deg_v", "deg_u"))

    pb = [nc.alloc_psum_tensor(f"bank{i}", [P, 512], FP32) for i in range(8)]
    RANK_BANK = 4

    def y_bank(layer, q):
        return pb[{0: q, 1: q, 2: q, 3: TPC + q % 2, 4: TPC + q % 2}[layer]]

    def t2_bank(layer, q):
        return pb[TPC + q if layer < 2 else 7]

    def bank_free(layer, ch, q):
        return tile_no(layer, ch, q) + (1 if layer < 2 else TPC)

    S = {n: nc.alloc_semaphore(n) for n in (
        "ld_edges ld_w0 ld_x ld_self ld_par ld_recs ld_l1 ld_l2 ld_c1 ld_c2 ld_b2 ld_c2_row normed_ahead x_copied x_high hl_loaded init_rec init_attr "
        "inverse_ready root_ready iota_ready ident_ready tri_ready pads_ready mats_ready dve pool "
        "key_oh_ready rank_mm ranked slots_ready rec_sent attr_sent0 attr_sent1 stage_ld0 stage_ld1 "
        "zc_ready ortho_full ortho_free squares_ready places_ready norm_ready stats_ready s_scaled oh_ready oh_used adj_evac aw_low x_split "
        "agg_step agg_full agg_copied dense_full dense_copied bn_ready z_ready y_ready t1_full t1_free normed t2_full "
        "t2_done split_done deg_full deg_done at_high at_split at_used at_oh_ready e2_done diag_ready diag_full diag_done "
        "h_full h_ready y_step at_in0 at_in1 at_in2 at_in3 totals_ready overfull_ready g_edges_ld g_consts_ready g_oh_ready g_used "
        "g_out g_stored g_attr_ld g_dve g_attrs_stored adj_final general_ld general_attrs_ld general_attrs_scaled e2_final").split()}
    s_xin = [nc.alloc_semaphore(f"xin_{q}") for q in range(TPC)]
    s_xout = [nc.alloc_semaphore(f"xout_{q}") for q in range(TPC)]

    def tile_no(layer, ch, q=0):
        return layer * NT + ch * TPC + q

    def ccols(ch):
        return bass.ds(ch * CW, CW)

    ROOT_NORM, ROOT_NORM2, ROOT_BN, ROOT_DEG = 0, 1, (2, 7), 12
    ROOT_LN = (3, 8, 13, 17, 21)
    LOADS = {0: 0, 1: 1, 2: 2, 4: 3}
    attr_rows = attr_table.rearrange("(p s) r -> p (s r)", p=P)

    with nc.allow_non_contiguous_dma("parameters by column"), nc.Block() as block:

        @block.sync
        def _(sp):
            sp.dma_start(src_i[:], src.rearrange("(p c) -> p c", p=P)).then_inc(S["ld_edges"], 16)
            sp.dma_start(dst_i[:], dst.rearrange("(p c) -> p c", p=P)).then_inc(S["ld_edges"], 16)
            sp.dma_start(w_e[:], edge_weight.rearrange("(p c) -> p c", p=P)).then_inc(S["ld_edges"], 16)
            sp.dma_start(w0_sb[:], w0.rearrange("(i p) d -> p i d", p=P)).then_inc(S["ld_w0"], 16)
            sp.wait_ge(S["pads_ready"], 3)
            sp.dma_start(rec_table.rearrange("(p s) r -> p (s r)", p=P),
                         pad[:].rearrange("p s r -> p (s r)")).then_inc(S["init_rec"], 16)
            x_halves = x.rearrange("(h t p) d -> h p t d", h=2, p=P)
            sp.dma_start(x_stage[:], x_halves[0]).then_inc(S["ld_x"], 16)
            sp.dma_start(self_sb[:], self_w.rearrange("(i p) d -> p i d", p=P)).then_inc(S["ld_self"], 16)
            for name, vec in (("bn_g", bn_g), ("bn_b", bn_b), ("bl", bl), ("g1", g1), ("be1", be1)):
                sp.dma_start(cols[name][:], vec.rearrange("(f p) -> p f", p=P)).then_inc(S["ld_par"], 16)
            sp.dma_start(b1_sb[:], b1.rearrange("(f p) -> p f", p=P)).then_inc(S["ld_par"], 16)
            for i in range(ZERO_DMAS):
                sp.dma_start(attr_rows[:, i * ZERO_COLS:(i + 1) * ZERO_COLS], zeros[:]).then_inc(S["init_attr"], 16)

            sp.wait_ge(S["ortho_full"], HALF_PIECES)
            sp.wait_ge(S["x_split"], 1)
            sp.dma_start(x_stage[:], x_halves[1]).then_inc(S["ld_x"], 16)

            sp.wait_ge(S["overfull_ready"], 1)
            overfull_sp = sp.value_load(overfull[0:1, 0:1], min_val=0, max_val=1)
            with sp.If(overfull_sp > 0):
                sp.wait_ge(S["ortho_free"], ORTHO_PIECES)
                for tile, vec in ((g_src_i, src), (g_dst_i, dst), (g_w, edge_weight)):
                    sp.dma_start(tile[:], vec.rearrange("(p c) -> p c", p=P)).then_inc(S["g_edges_ld"], 16)
                with sp.Fori(0, STEPS) as i:
                    sp.wait_ge(S["g_out"], i + 1 + 1)
                    sp.dma_start(all_counts[bass.ds(i, 1), :, :].rearrange("a p d -> (a p) d"), g_counts[:]
                                 ).then_inc(S["g_stored"], 16)
                    sp.dma_start(all_weights[bass.ds(i, 1), :, :, :].rearrange("a p b d -> (a p) b d"), g_weights[:]
                                 ).then_inc(S["g_stored"], 16)
                sp.wait_ge(S["g_consts_ready"], 4)
                with sp.Fori(0, NCH) as ch:
                    with sp.Fori(0, PARTS) as part:
                        sp.wait_ge(S["g_used"], part + ch * PARTS + STEPS * PARTS + 1)
                        sp.dma_start(g_attr[:, :, 0:EDGE_IN], edge_attr.rearrange("(p c) r -> p c r", p=P)
                                     [:, bass.ds(part * PART, PART), :]).then_inc(S["g_attr_ld"], 16)
                    sp.wait_ge(S["g_out"], ch + STEPS + 1 + 1)
                    sp.dma_start(all_attrs[bass.ds(ch, 1), :, :].rearrange("a p d -> (a p) d"), g_attr_sums[:]
                                 ).then_inc(S["g_attrs_stored"], 16)
                sp.wait_ge(S["g_stored"], 32 * (STEPS + 1))
                sp.wait_ge(S["g_attrs_stored"], 16 * (NCH + 1))

            sp.wait_ge(S["init_attr"], 16 * ZERO_DMAS)
            sp.wait_ge(S["rec_sent"], 16 * EDGE_TILES)
            sp.dma_start(recs[:].rearrange("p s r -> p (s r)"),
                         rec_table.rearrange("(p s) r -> p (s r)", p=P)).then_inc(S["ld_recs"], 16)

            def load_x(layer, source, ch, so_far):
                if layer >= 2:
                    for q in range(TPC):
                        sp.wait_ge(s_xout[q], 16 * (so_far * NCH + 1) + 16 * ch)
                for q in range(TPC):
                    t = tile_no(layer, ch if layer < 4 else 0, q)
                    if layer < 2:
                        sp.wait_ge(S["normed_ahead"], t + 1)
                    else:
                        sp.wait_ge(S["t2_full"], t + 1)
                        sp.wait_ge(S["split_done"], t + 1)
                    sp.dma_start((x_post if layer < 2 else xr)[:, q, :], source[bass.ds((ch * TPC + q) * P, P), :]
                                 ).then_inc(s_xin[q], 16)

            def store_x(layer, to, ch):
                for q in range(TPC):
                    sp.wait_ge(S["normed"], tile_no(layer, ch, q) + 1)
                    sp.dma_start(to[bass.ds((ch * TPC + q) * P, P), :], xr[:, q, :]).then_inc(s_xout[q], 16)

            def stored(so_far):
                for q in range(TPC):
                    sp.wait_ge(s_xout[q], 16 * (so_far * NCH + 1))

            sp.sem_inc(S["t2_full"], TPC)
            sp.sem_inc(S["normed_ahead"], TPC)
            sp.sem_inc(S["split_done"], TPC)
            sp.sem_inc(S["at_split"], AT_RING)
            for q in range(TPC):
                sp.sem_inc(s_xout[q], 16)
            with sp.If(overfull_sp > 0):
                with sp.Fori(0, NCH) as ch:
                    for t in range(NT):
                        sp.wait_ge(S["aw_low"], ch * NT + t + 1 + 2)
                        step = bass.ds(ch * NT + t, 1)
                        sp.dma_start(adj[:, t, ccols(ch)], all_counts[step, :, :].rearrange("a p d -> (a p) d")
                                     ).then_inc(S["general_ld"], 16)
                        sp.dma_start(aw[:, t % AW_RING, :, :], all_weights[step, :, :, :].rearrange("a p b d -> (a p) b d")
                                     ).then_inc(S["general_ld"], 16)
                        sp.wait_ge(S["general_ld"], (32 * NT) * ch + 32 * (t + 1))
                        sp.sem_inc(S["adj_final"], 1)
            with sp.If(overfull_sp < 1):
                with sp.Fori(0, NCH) as ch:
                    for t in range(NT):
                        sp.wait_ge(S["aw_low"], ch * NT + t + 1 + 2)
                        sp.sem_inc(S["adj_final"], 1)
            sp.wait_ge(S["dense_full"], NCH * FT)
            load_x(0, x, 0, 0)
            with sp.Fori(0, NCH - 1) as ch:
                load_x(0, x, ch + 1, 0)
                store_x(0, x_after[0], ch)
            store_x(0, x_after[0], NCH - 1)
            stored(1)
            sp.dma_start(wl_sb[:], wl.rearrange("(i p) d -> p i d", p=P)).then_inc(S["ld_l1"], 16)
            sp.dma_start(wr_sb[:], wr.rearrange("(i p) d -> p i d", p=P)).then_inc(S["ld_l1"], 16)
            for u in range(2):
                sp.wait_ge(S[f"attr_sent{u}"], 16 * LOT * ((LOTS + 1 - u) // 2))
            for name in ("t1_full", "t2_full", "split_done"):
                sp.wait_ge(S[name], NT + TPC)
            with sp.Fori(0, STEPS // AT_RING) as i:
                for u in range(AT_RING):
                    sp.wait_ge(S["at_split"], i * AT_RING + u + 1)
                    sp.dma_start(at_in[:, u, :, :].rearrange("p s r -> p (s r)"),
                                 attr_rows[:, bass.ds((i * AT_RING + u) * (ST * EDGE_IN), ST * EDGE_IN)]
                                 ).then_inc(S[f"at_in{u}"], 16)
            sp.wait_ge(S["at_split"], STEPS + AT_RING)
            with sp.If(overfull_sp > 0):
                sp.wait_ge(S["e2_done"], NCH)
                sp.dma_start(e2T[:].rearrange("p (a d) -> p a d", a=NCH), all_attrs.rearrange("a p d -> p a d")
                             ).then_inc(S["general_attrs_ld"], 16)
            sp.wait_ge(S["dense_full"], 2 * NCH * FT)
            sp.dma_start(w1_sb[:], w1[0:D, :].rearrange("(i p) d -> p i d", p=P)).then_inc(S["ld_l2"], 16)
            for half in range(2):
                sp.dma_start(w1e_sb[half * EDGE_IN:(half + 1) * EDGE_IN, :], w1[D:D + EDGE_IN, :]).then_inc(S["ld_l2"], 16)
            w2_rows = w2.rearrange("(i p) d -> p i d", p=P)
            sp.dma_start(w2_sb[:, 0:HT // 2, :], w2_rows[:, 0:HT // 2, :]).then_inc(S["ld_l2"], 16)
            load_x(1, x_after[0], 0, 1)
            with sp.Fori(0, NCH - 1) as ch:
                load_x(1, x_after[0], ch + 1, 1)
                store_x(1, x_after[1], ch)
            sp.wait_ge(S["normed_ahead"], 2 * NT + TPC)
            sp.dma_start(w2_sb[:, HT // 2:, :], w2_rows[:, HT // 2:, :]).then_inc(S["ld_l2"], 16)
            store_x(1, x_after[1], NCH - 1)
            stored(2)
            sp.dma_start(bias_rows[2][:], b2.rearrange("(a d) -> a d", a=1).to_broadcast([P, D])).then_inc(S["ld_b2"], 16)
            with sp.Fori(0, NCH - 1) as ch:
                load_x(2, x_after[1], ch, 2)
                store_x(2, x_after[2], ch)
            load_x(2, x_after[1], NCH - 1, 2)
            sp.wait_ge(S["y_step"], NCH * HT + 4)
            for i, w in enumerate((c1a, c1b)):
                sp.dma_start(c1_sb[:, i, :, :], w.rearrange("(i p) d -> p i d", p=P)).then_inc(S["ld_c1"], 16)
            for tile, vec in ((lng_sb, ln_g), (lnb_sb, ln_b), (bias_rows[3], c1bias)):
                sp.dma_start(tile[:], vec.rearrange("(a d) -> a d", a=1).to_broadcast([P, D])).then_inc(S["ld_c1"], 16)
            for i, w in enumerate((c2a, c2b)):
                sp.dma_start(c2_sb[:, i, :, :], w.rearrange("(i p) d -> p i d", p=P)).then_inc(S["ld_c2"], 16)
            store_x(2, x_after[2], NCH - 1)
            stored(3)
            with sp.Fori(0, NCH - 1) as ch:
                for q in range(TPC):
                    sp.wait_ge(S["split_done"], tile_no(3, ch, q) + 1 + TPC)
                    sp.dma_start(h_parts[bass.ds(ch * TPC + q, 1), :, :, :].rearrange("a p b d -> (a p) b d"),
                                 hl[:, q % HL_RING, :, :]).then_inc(s_xout[q], 16)
            for q in range(TPC):
                sp.wait_ge(s_xout[q], 16 * (4 * NCH - 1 + 1))
            sp.wait_ge(S["agg_full"], 2 * NCH)
            for i, tile in enumerate((x_hi, x_lo)):
                sp.dma_start(tile[:, 0:NT - TPC, :], h_parts[0:NT - TPC, :, i, :].rearrange("t p d -> p t d")
                             ).then_inc(S["hl_loaded"], 16)
            sp.wait_ge(S["split_done"], 4 * NT + TPC)
            sp.dma_start(bias_rows[4][:], c2bias.rearrange("(a d) -> a d", a=1).to_broadcast([P, D])).then_inc(S["ld_c2_row"], 16)
            for q in range(TPC):
                sp.sem_inc(s_xout[q], 16)
            with sp.Fori(0, NCH) as ch:
                load_x(4, x_after[2], ch, 4)
                store_x(4, out, ch)
            stored(5)

        @block.gpsimd
        def _(pool):
            chain = Chain(pool, S["pool"])
            nc.gpsimd.memset(zeros[:], 0.0).then_inc(S["pads_ready"], 1)
            nc.gpsimd.memset(pad[:], 0.0).then_inc(S["pads_ready"], 1)
            pool.wait_ge(S["pads_ready"], 2)
            nc.gpsimd.memset(pad[:, :, 0:2], -1.0).then_inc(S["pads_ready"], 1)
            nc.gpsimd.iota(iota[:], pattern=[[1, KEYS]], base=0, channel_multiplier=0,
                           allow_small_or_imprecise_dtypes=True).then_inc(S["iota_ready"], 1)
            chain.link(nc.gpsimd.memset(tri[:], 1.0))
            nc.gpsimd.affine_select(out=no_tri[:], in_=tri[:], compare_op=ALU.is_ge, fill=0.0, base=0,
                                    pattern=[[-1, P]], channel_multiplier=1).then_inc(S["tri_ready"], 1)
            pool.wait_ge(S["tri_ready"], 1)
            nc.gpsimd.affine_select(out=tri[:], in_=tri[:], compare_op=ALU.is_gt, fill=0.0, base=0,
                                    pattern=[[1, P]], channel_multiplier=-1).then_inc(S["tri_ready"], 1)
            chain.link(nc.gpsimd.memset(ident[:], 0.0))
            nc.gpsimd.affine_select(out=ident[:], in_=ident[:], compare_op=ALU.not_equal, fill=1.0, base=0,
                                    pattern=[[-1, P]], channel_multiplier=1).then_inc(S["ident_ready"], 1)
            nc.gpsimd.memset(ones16[:], 1.0).then_inc(S["ident_ready"], 1)
            nc.gpsimd.memset(ones32[:], 1.0).then_inc(S["ident_ready"], 1)

            pool.wait_ge(S["init_rec"], 16)
            for c in range(EDGE_TILES):
                if c % LOT == 0:
                    pool.wait_ge(S["slots_ready"], c // LOT + 1)
                pool.indirect_dma_start(out=rec_table, out_offset=bass.IndirectOffsetOnAxis(ap=slot[:, c:c + 1], axis=0),
                                        in_=rec[:, c, :], in_offset=None).then_inc(S["rec_sent"], 16)
            pool.wait_ge(S["init_attr"], 16 * ZERO_DMAS)
            attr_in = edge_attr.rearrange("(p c) r -> p c r", p=P)
            for lot in range(LOTS):
                u = lot % 2
                if lot >= 2:
                    pool.wait_ge(S[f"attr_sent{u}"], 16 * LOT * (lot // 2))
                pool.dma_start(stage[:, u, :, :], attr_in[:, lot * LOT:(lot + 1) * LOT, :]).then_inc(S[f"stage_ld{u}"], 16)
                pool.wait_ge(S[f"stage_ld{u}"], 16 * (lot // 2 + 1))
                for j in range(LOT):
                    c = lot * LOT + j
                    pool.indirect_dma_start(
                        out=attr_table, out_offset=bass.IndirectOffsetOnAxis(ap=slot[:, c:c + 1], axis=0),
                        in_=stage[:, u, j, :], in_offset=None).then_inc(S[f"attr_sent{u}"], 16)

            with pool.Fori(0, NCH) as ch:
                for q in range(TPC):
                    pool.wait_ge(S["x_high"], tile_no(0, ch, q) + 1)
                    hi, lo = (part[:, bass.ds(ch * TPC + q, 1), :].rearrange("p a d -> p (a d)") for part in (x_hi, x_lo))
                    nc.gpsimd.tensor_tensor(lo, xr[:, q, :], hi, ALU.subtract).then_inc(S["split_done"], 1)

            with pool.Fori(0, STEPS // AT_RING) as i:
                for u in range(AT_RING):
                    pool.wait_ge(S["at_high"], i * AT_RING + u + 1)
                    nc.gpsimd.tensor_tensor(at_parts[:, u % 2, :, 1, :], at_in[:, u, :, :], at_parts[:, u % 2, :, 0, :],
                                            ALU.subtract).then_inc(S["at_split"], 1)

        @block.scalar
        def _(act):
            act.wait_ge(S["ident_ready"], 3)
            for m, v in ((eps_i, EPS), (mhalf_i, -0.5), (threehalf_i, 1.5)):
                nc.scalar.activation(m[:], ident[:], ACT.Copy, scale=v).then_inc(S["mats_ready"], 1)
            done = [0]

            def evac(to, scale=1.0, shape=None, cols=slice(0, D)):
                n = done[0]
                bank = pb[n % 4][:, cols] if shape is None else pb[n % 4][:].rearrange("p (a b) -> p a b", a=shape)
                act.wait_ge(S["ortho_full"], n + 1)
                done[0] += 1
                nc.scalar.activation(to, bank, ACT.Copy, scale=scale).then_inc(S["ortho_free"], 1)

            def evac_x0(t):
                evac(featT[:, :, t * P:(t + 1) * P], shape=FT)

            for i in range(4):
                evac(zcT[:, :, i * P:(i + 1) * P], shape=4)
            def evac_upper(to, scale=1.0):
                for i in range(4):
                    evac(to[:, i, i * P:], scale=scale, cols=slice(i * P, D))

            def evac_mirrored(to):
                for i in range(1, 4):
                    evac(to[:, i, 0:i * P], cols=slice(0, i * P))

            evac_upper(s_n)
            evac_mirrored(s_n)
            act.wait_ge(S["ortho_free"], done[0])
            for i in range(4):
                nc.scalar.activation(sq_junk[:], s_n[:, i, :], ACT.Square, accum_out=sq_sum[:, i:i + 1]
                                     ).then_inc(S["squares_ready"], 1)
                act.wait_ge(S["squares_ready"], i + 1)
            done[0] += 1

            def root(no, to, inverse):
                act.wait_ge(S["inverse_ready"], no + 1)
                nc.scalar.activation(to, inverse, ACT.Sqrt).then_inc(S["root_ready"], 1)

            root(ROOT_NORM, s_rn[:], s_u[:])
            root(ROOT_NORM2, s_rrn[:], s_rn[:])
            act.wait_ge(S["norm_ready"], 1)
            for i in range(4):
                nc.scalar.activation(s_n[:, i, :], s_n[:, i, :], ACT.Copy, scale=s_rn[:]).then_inc(S["s_scaled"], 1)
            for i in range(4):
                evac(b_ping[:, i, :])
            b = [b_ping, b_pong]
            for it in range(4):
                evac_upper(b_sq)
                evac_upper(b_s, scale=-0.5)
                evac_mirrored(b_sq)
                evac_x0(4 * it)
                evac_x0(4 * it + 1)
                evac_mirrored(b_s)
                evac_x0(4 * it + 2)
                evac_upper(b[1])
                evac_x0(4 * it + 3)
                evac_mirrored(b[1])
                b.reverse()
            for i in range(4):
                evac(t_sb[:, i, :], scale=s_rrn[:])

            act.sem_inc(S["agg_step"], AW_RING)
            act.sem_inc(S["dense_copied"], 4)
            act.sem_inc(S["y_step"], 4)
            act.sem_inc(S["h_ready"], 2)
            with act.Fori(0, NCH) as ch:
                for t in range(NT):
                    act.wait_ge(S["oh_used"], ch * (NT * GROUPS) + (t + 1) * GROUPS + OH_RING)
                    act.wait_ge(S["agg_step"], ch * NT + t + 1)
                    nc.scalar.activation(adj[:, t, ccols(ch)], pb[4 + 2 * (t % 2)][:], ACT.Copy)
                    nc.scalar.activation(aw[:, t % AW_RING, 0, :], pb[5 + 2 * (t % 2)][:], ACT.Copy).then_inc(S["adj_evac"], 1)
                act.wait_ge(S["agg_step"], ch * NT + NT + AW_RING)
                for f in range(FT):
                    nc.scalar.activation(aggT[:, f, :], pb[f][:], ACT.Copy).then_inc(S["agg_copied"], 1)
                act.wait_ge(S["dense_full"], ch * FT + FT)
                for f in range(FT):
                    nc.scalar.activation(featT[:, f, ccols(ch)], pb[4 + f][:], ACT.Copy).then_inc(S["dense_copied"], 1)

            def features_to_ybuf(layer, ch, func, ready):
                act.wait_ge(S["t1_full"], tile_no(layer, ch) + TPC)
                for f in range(FT):
                    last = nc.scalar.activation(ybuf[:, f, :], featT[:, f, ccols(ch)], func,
                                                scale=bn_sc[:, f:f + 1], bias=bn_bi[:, f:f + 1])
                last.then_inc(S[ready], 1)

            def ln_root(layer, ch):
                root(ch + ROOT_LN[layer], ln_r[:], ln_u[:])

            def transposed_back(layer, ch, q):
                act.wait_ge(S["t2_full"], tile_no(layer, ch, q) + 1 + TPC)
                nc.scalar.activation(featT[:, :, bass.ds((ch * TPC + q) * P, P)],
                                     t2_bank(layer, q)[:].rearrange("p (a b) -> p a b", a=FT),
                                     ACT.Copy).then_inc(S["t2_done"], 1)

            def post(layer, ch):
                ln_root(layer, ch)
                for q in range(TPC):
                    if layer == 0:
                        act.wait_ge(S["normed"], tile_no(layer, ch, q) + 1)
                        nc.scalar.activation(x_hi[:, bass.ds(ch * TPC + q, 1), :].rearrange("p a d -> p (a d)"), xr[:, q, :],
                                             ACT.Copy).then_inc(S["x_high"], 1)
                    transposed_back(layer, ch, q)

            act.sem_inc(S["t1_full"], TPC)
            act.sem_inc(S["t2_done"], TPC)
            root(ROOT_BN[0], bn_sc[:], bn_u[:])
            act.wait_ge(S["bn_ready"], 1)
            features_to_ybuf(0, 0, ACT.Relu, "y_ready")
            with act.Fori(0, NCH - 1) as ch:
                features_to_ybuf(0, ch + 1, ACT.Relu, "y_ready")
                post(0, ch)
            post(0, NCH - 1)

            act.sem_inc(S["at_used"], 2)
            with act.Fori(0, NCH) as ch:
                for t in range(NT):
                    act.wait_ge(S[f"at_in{t % AT_RING}"], ch * (16 * NT // AT_RING) + 16 * (t // AT_RING + 1))
                    act.wait_ge(S["at_used"], ch * NT + t + 1)
                    nc.scalar.activation(at_parts[:, t % 2, :, 0, :], at_in[:, t % AT_RING, :, :], ACT.Copy).then_inc(S["at_high"], 1)
                act.wait_ge(S["dense_full"], ch * FT + NCH * FT + FT)
                for f in range(FT):
                    nc.scalar.activation(featT[:, f, ccols(ch)], pb[4 + (f + 1) % FT][:], ACT.Identity,
                                         bias=cols["bl"][:, f:f + 1]).then_inc(S["dense_copied"], 1)
            root(ROOT_BN[1], bn_sc[:], bn_u[:])
            act.wait_ge(S["bn_ready"], 2)
            features_to_ybuf(1, 0, ACT.Identity, "z_ready")
            with act.Fori(0, NCH - 1) as ch:
                features_to_ybuf(1, ch + 1, ACT.Identity, "z_ready")
                post(1, ch)
            post(1, NCH - 1)
            root(ROOT_DEG, dinv[:], deg_u[:])

            def layer2(ch, last_ch):
                for i in range(HT):
                    act.wait_ge(S["h_full"], ch * HT + i + 1)
                    act.wait_ge(S["y_step"], ch * HT + i + 1)
                    nc.scalar.activation(h_ring[:, i % 4, :], pb[4 + i % 2][:], ACT.Relu,
                                         bias=b1_sb[:, i:i + 1]).then_inc(S["h_ready"], 1)
                    if last_ch is not None:
                        if i == BACK_AT - 1:
                            ln_root(2, last_ch)
                        if BACK_AT <= i < BACK_AT + TPC:
                            transposed_back(2, last_ch, i - BACK_AT)

            layer2(0, None)
            with act.Fori(0, NCH - 1) as last_ch:
                layer2(last_ch + 1, last_ch)
            post(2, NCH - 1)

            for layer in (3, 4):
                act.wait_ge(S["t2_done"], layer * NT + TPC)
                with act.Fori(0, NCH) as ch:
                    act.wait_ge(S["dense_full"], (layer - 1) * NCH * FT + ch * FT)
                    for f in range(FT):
                        nc.scalar.activation(ybuf[:, f, :], featT[:, f, ccols(ch)], ACT.Copy).then_inc(S["x_copied"], 1)
                    if layer == 3:
                        post(3, ch)
                    else:
                        ln_root(4, ch)

        @block.vector
        def _(dve):
            chain = Chain(dve, S["dve"])
            V = nc.vector

            def invert(no, v, u):
                chain.link(V.reciprocal(u, v))
                dve.sem_inc(S["inverse_ready"], 1)

            def inverse_root(no, v, u, r):
                dve.wait_ge(S["root_ready"], no + 1)
                chain.link(V.tensor_tensor(u, r, r, ALU.mult))
                chain.link(V.tensor_tensor(u, u, v, ALU.mult))
                chain.link(V.tensor_scalar(u, u, -0.5, 1.5, ALU.mult, ALU.add))
                chain.link(V.tensor_tensor(r, r, u, ALU.mult))

            dve.wait_ge(S["ld_edges"], 48)
            chain.mark(V.tensor_scalar(sb_i[:], src_i[:], 7, None, ALU.logical_shift_right))
            chain.link(V.tensor_scalar(db_i[:], dst_i[:], 7, None, ALU.logical_shift_right))
            chain.mark(V.tensor_scalar(sbl_i[:], sb_i[:], TPC - 1, None, ALU.bitwise_and))
            chain.mark(V.tensor_scalar(dbl_i[:], db_i[:], TPC - 1, None, ALU.bitwise_and))
            chain.mark(V.tensor_scalar(src_i[:], src_i[:], P - 1, None, ALU.bitwise_and))
            chain.link(V.tensor_scalar(dst_i[:], dst_i[:], P - 1, None, ALU.bitwise_and))
            chain.mark(V.tensor_copy(rec[:, :, 0], src_i[:]))
            chain.mark(V.tensor_copy(rec[:, :, 1], dst_i[:]))
            chain.mark(V.scalar_tensor_tensor(key[:], db_i[:], float(NT), sb_i[:], ALU.mult, ALU.add))
            chain.link(V.tensor_scalar(base[:], dbl_i[:], 2.0 - ST * NT / TPC, None, ALU.mult))
            chain.link(V.scalar_tensor_tensor(base[:], db_i[:], ST * NT / TPC, base[:], ALU.mult, ALU.add))
            chain.link(V.scalar_tensor_tensor(base[:], sb_i[:], float(ST), base[:], ALU.mult, ALU.add))
            chain.mark(V.tensor_tensor(top[:], sbl_i[:], dbl_i[:], ALU.is_equal))
            chain.link(V.tensor_scalar(third[:], dbl_i[:], -2.0, float(2 * TPC - 1 - P * SLOT_TILES), ALU.mult, ALU.add))
            chain.link(V.tensor_scalar(top[:], top[:], float(P), float(2 * P - 1), ALU.mult, ALU.add))
            for k in range(2):
                chain.link(V.tensor_copy(rec[:, :, 2 + k], w_e[:]))
                if k < 1:
                    chain.link(V.tensor_tensor(w_e[:], w_e[:], rec[:, :, 2 + k], ALU.subtract))
            chain.link(V.memset(key_oh[:], 0.0))

            dve.wait_ge(S["iota_ready"], 1)
            dve.sem_inc(S["ranked"], 2)
            top2 = top[:].rearrange("p (c two) -> p c two", two=2)
            rank2 = rank[:].rearrange("p (c two) -> p c two", two=2)

            def block_row(c, j):
                V.tensor_scalar(key_oh[:, j % OH_RING, :], iota[:], key[:, bass.ds(c, 1)], None,
                                ALU.is_equal).then_inc(S["key_oh_ready"], 1)

            def rank_lots(first, count, more=True):
                with chain.loop(count, 7) as i:
                    c0 = i * LOT + first * LOT

                    def extract(j):
                        dve.wait_ge(S["rank_mm"], c0 + j + 1)
                        V.tensor_tensor_reduce(out=ranked_junk[:, j % 2, :], in0=pb[RANK_BANK + j % 2][:, 0:KEYS],
                                               in1=key_oh[:, j % OH_RING, :], scale=1.0, scalar=0.0,
                                               op0=ALU.mult, op1=ALU.add, accum_out=rank[:, j:j + 1]
                                               ).then_inc(S["ranked"], 1)

                    for j in range(2, LOT):
                        extract(j - 2)
                        block_row(c0 + j, j)
                    extract(LOT - 2)
                    extract(LOT - 1)
                    if more:
                        for j in range(2):
                            block_row(c0 + LOT + j, LOT + j)
                    dve.wait_ge(S["ranked"], c0 + LOT + 2)
                    lot = bass.ds(c0, LOT)
                    chain.link(V.tensor_tensor(rank2[:, :, 1], top2[:, bass.ds(i * (LOT // 2) + first * (LOT // 2), LOT // 2), 1],
                                               rank2[:, :, 1], ALU.subtract))
                    chain.mark(V.tensor_scalar(past1[:], rank[:], float(P), float(1 - P * SLOT_TILES), ALU.is_ge, ALU.mult))
                    chain.mark(V.scalar_tensor_tensor(past2[:], rank[:], float(2 * P), third[:, lot], ALU.is_ge, ALU.mult))
                    chain.link(V.scalar_tensor_tensor(row[:], rank[:], float(SLOT_TILES), base[:, lot], ALU.mult, ALU.add))
                    chain.link(V.tensor_tensor(row[:], row[:], past1[:], ALU.add))
                    chain.link(V.tensor_tensor(row[:], row[:], past2[:], ALU.add))
                    chain.link(V.tensor_scalar(slot[:, lot], row[:], 0.0, float(P * SLOT_TILES - 1), ALU.max, ALU.min))
                    dve.sem_inc(S["slots_ready"], 1)

            for j in range(2):
                block_row(j, j)
            rank_lots(0, 1)
            dve.wait_ge(S["ld_w0"], 16)
            dve.wait_ge(S["ident_ready"], 3)
            chain.link(V.tensor_scalar(w0_sb[:], w0_sb[:], 0.5, None, ALU.mult))
            for i in range(4):
                block_i = w0_sb[:, i, i * P:(i + 1) * P]
                chain.link(V.scalar_tensor_tensor(block_i, ident[:], 0.5, block_i, ALU.mult, ALU.add))
            chain.link(V.tensor_reduce(z_sum[:], w0_sb[:], AX.X, ALU.add))
            chain.link(V.tensor_scalar(z_sum[:], z_sum[:], 1.0 / D, None, ALU.mult))
            for i in range(4):
                V.tensor_scalar(zc[:, i, :], w0_sb[:, i, :], z_sum[:, i:i + 1], None, ALU.subtract
                                ).then_inc(S["zc_ready"], 1)
            rank_lots(1, NORM_AFTER_LOTS - 1)
            dve.wait_ge(S["ortho_full"], NORM_PIECE + 1)
            chain.link(V.tensor_reduce(s_tot[:], pb[NORM_PIECE % 4][:, 0:4], AX.X, ALU.add))
            dve.sem_inc(S["ortho_free"], 1)
            invert(ROOT_NORM, s_tot[:], s_u[:])
            inverse_root(ROOT_NORM, s_tot[:], s_u[:], s_rn[:])
            chain.link(V.tensor_tensor(s_tot[:], s_tot[:], s_rn[:], ALU.mult))
            dve.sem_inc(S["inverse_ready"], 1)
            inverse_root(ROOT_NORM2, s_tot[:], s_u[:], s_rrn[:])
            dve.sem_inc(S["norm_ready"], 1)
            def split_input(half):
                tiles = slice(half * (NT // 2), (half + 1) * (NT // 2))
                dve.wait_ge(S["ld_x"], 16 * (half + 1))
                chain.link(V.tensor_copy(x_hi[:, tiles, :], x_stage[:]))
                chain.link(V.tensor_tensor(x_lo[:, tiles, :], x_stage[:], x_hi[:, tiles, :], ALU.subtract))
                dve.sem_inc(S["x_split"], 1)

            rank_lots(NORM_AFTER_LOTS, SPLIT_AFTER_LOTS - NORM_AFTER_LOTS)
            split_input(0)
            rank_lots(SPLIT_AFTER_LOTS, LOTS - 1 - SPLIT_AFTER_LOTS)
            rank_lots(LOTS - 1, 1, more=False)

            dve.wait_ge(S["totals_ready"], 1)
            chain.link(V.tensor_copy(block_edges[:], pb[RANK_BANK][:, 0:KEYS]))
            chain.link(V.tensor_tensor(block_edges[:], block_edges[:], pb[RANK_BANK + 1][:, 0:KEYS], ALU.add))
            chain.link(V.tensor_copy(block_db[:], iota[:]))
            chain.mark(V.tensor_scalar(block_sb[:], block_db[:], TPC - 1, None, ALU.bitwise_and))
            chain.link(V.tensor_scalar(block_db[:], block_db[:], NT.bit_length() - 1, None, ALU.logical_shift_right))
            chain.link(V.tensor_scalar(block_db[:], block_db[:], TPC - 1, None, ALU.bitwise_and))
            chain.link(V.tensor_tensor(block_cap[:], block_sb[:], block_db[:], ALU.is_equal))
            chain.link(V.tensor_scalar(block_cap[:], block_cap[:], float(P), float(2 * P), ALU.mult, ALU.add))
            chain.link(V.tensor_tensor(block_cap[:], block_edges[:], block_cap[:], ALU.is_gt))
            chain.link(V.tensor_reduce(over_max[:], block_cap[:], AX.X, ALU.max))
            chain.link(V.tensor_copy(overfull[:], over_max[:]))
            dve.sem_inc(S["overfull_ready"], 1)
            overfull_dve = dve.value_load(overfull[0:1, 0:1], min_val=0, max_val=1)

            with dve.If(overfull_dve > 0):
                general = Chain(dve, S["g_dve"])
                dve.wait_ge(S["ortho_free"], ORTHO_PIECES)
                V.memset(g_zero[:], 0.0).then_inc(S["g_consts_ready"], 1)
                V.memset(g_attr[:], 0.0).then_inc(S["g_consts_ready"], 1)
                V.tensor_copy(g_iota[:, 0:KEYS], iota[:]).then_inc(S["g_consts_ready"], 1)
                V.tensor_scalar(g_iota[:, KEYS:2 * KEYS], iota[:], float(KEYS), None, ALU.add).then_inc(S["g_consts_ready"], 1)
                dve.wait_ge(S["g_consts_ready"], 4)
                dve.wait_ge(S["g_edges_ld"], 48)
                for name, free in (("g_used", 1), ("g_out", 1), ("g_stored", 32), ("g_attrs_stored", 16)):
                    dve.sem_inc(S[name], free)
                general.link(V.tensor_copy(g_src[:], g_src_i[:]))
                general.link(V.tensor_copy(g_dst[:], g_dst_i[:]))
                with general.loop(NCH, 2 + 2 * NT) as ch:
                    with general.loop(NT, 2) as t:
                        with dve.Fori(0, PARTS) as part:
                            dve.wait_ge(S["g_used"], part + t * PARTS + ch * (NT * PARTS) + 1)
                            for j in range(PART):
                                c = bass.ds(part * PART + j, 1)
                                V.tensor_scalar(g_src_oh[:, j, :], g_iota[:, 0:P], g_src[:, c], None, ALU.is_equal)
                                V.tensor_scalar(g_dst_oh[:, j, :], g_iota[:], g_dst[:, c], None, ALU.is_equal)
                                last = V.tensor_scalar(g_weight_oh[:, j, :], g_iota[:], g_dst[:, c], g_w[:, c],
                                                       ALU.is_equal, ALU.mult)
                            last.then_inc(S["g_oh_ready"], 1)
                        dve.wait_ge(S["g_used"], t * PARTS + ch * (NT * PARTS) + PARTS + 1)
                        dve.wait_ge(S["g_stored"], 32 * t + (32 * NT) * ch + 32)
                        V.tensor_copy(g_counts[:], pb[0][:])
                        general.link(V.tensor_copy(g_weights[:, 0, :], pb[1][:]))
                        V.tensor_tensor(g_weights[:, 1, :], pb[1][:], g_weights[:, 0, :], ALU.subtract).then_inc(S["g_out"], 1)
                        general.link(V.tensor_scalar(g_src[:], g_src[:], float(-P), None, ALU.add))
                    general.link(V.tensor_scalar(g_src[:], g_src[:], float(N), None, ALU.add))
                    general.link(V.tensor_scalar(g_dst[:], g_dst[:], float(-CW), None, ALU.add))
                general.link(V.tensor_scalar(g_dst[:], g_dst[:], float(N), None, ALU.add))
                dve.wait_ge(S["g_stored"], 32 * (STEPS + 1))
                with general.loop(NCH, 1) as ch:
                    with dve.Fori(0, PARTS) as part:
                        dve.wait_ge(S["g_used"], part + ch * PARTS + STEPS * PARTS + 1)
                        for j in range(PART):
                            last = V.tensor_scalar(g_dst_oh[:, j, :], g_iota[:], g_dst[:, bass.ds(part * PART + j, 1)],
                                                   None, ALU.is_equal)
                        last.then_inc(S["g_oh_ready"], 1)
                    dve.wait_ge(S["g_used"], ch * PARTS + (STEPS + 1) * PARTS + 1)
                    dve.wait_ge(S["g_attrs_stored"], 16 * ch + 16)
                    V.tensor_copy(g_attr_sums[:], pb[2][:]).then_inc(S["g_out"], 1)
                    general.link(V.tensor_scalar(g_dst[:], g_dst[:], float(-CW), None, ALU.add))
                dve.wait_ge(S["g_attrs_stored"], 16 * (NCH + 1))

            split_input(1)
            dve.wait_ge(S["ld_recs"], 16)
            dve.wait_ge(S["ortho_free"], ORTHO_PIECES - 4 - 3 - 1)
            chain.mark(V.tensor_copy(dst_keep[:], recs[:, :, 1]))
            for i in range(REC):
                chain.mark(V.tensor_copy(fields[:, i, :], recs[:, :, i]))
            chain.mark(V.tensor_copy(iota_group[:], iota[:, 0:P].rearrange("p (a d) -> p a d", d=1).to_broadcast([P, P, GROUP])))
            chain.settle()
            dve.sem_inc(S["oh_used"], OH_RING)
            dve.sem_inc(S["aw_low"], 2)

            def low_weights(ch, t):
                dve.wait_ge(S["adj_evac"], ch * NT + t + 1)
                V.tensor_tensor(aw[:, t % AW_RING, 1, :], pb[5 + 2 * (t % 2)][:], aw[:, t % AW_RING, 0, :],
                                ALU.subtract).then_inc(S["aw_low"], 1)

            with dve.Fori(0, NCH) as ch:
                for g in range(NT * GROUPS):
                    dve.wait_ge(S["oh_used"], ch * (NT * GROUPS) + g + 1)
                    rows = oh[:, g % OH_RING, :, :, :]
                    group = bass.ds(ch * (NT * ST) + g * GROUP, GROUP)

                    def spread(first, count):
                        return fields[:, first:first + count, group].rearrange("p a (b d) -> p a b d", b=1).to_broadcast(
                            [P, count, P, GROUP])

                    V.tensor_tensor(rows[:, 0:2, :, :], iota_group[:].rearrange("p (a b) d -> p a b d", a=1).to_broadcast(
                        [P, 2, P, GROUP]), spread(0, 2), ALU.is_equal).then_inc(S["places_ready"], 1)
                    dve.wait_ge(S["places_ready"], ch * (NT * GROUPS) + g + 1)
                    V.tensor_tensor(rows[:, 2:4, :, :], rows[:, 1:2, :, :].to_broadcast([P, 2, P, GROUP]), spread(2, 2),
                                    ALU.mult).then_inc(S["oh_ready"], 1)
                    if g % GROUPS == GROUPS - 1 and g >= GROUPS:
                        low_weights(ch, g // GROUPS - 1)
                low_weights(ch, NT - 1)

            def batch_norm(no, gamma, beta, copied):
                for ch in range(NCH):
                    dve.wait_ge(S["dense_copied"], copied - (NCH - 1 - ch) * FT)
                    for f in range(FT):
                        chain.mark(V.bn_stats(bn_st[:, f, ch, :], featT[:, f, ch * CW:(ch + 1) * CW]))
                chain.settle()
                for f in range(FT):
                    chain.mark(V.bn_aggr(bn_mv[:, f, :], bn_st[:, f, :, :]))
                chain.settle()
                chain.link(V.tensor_scalar(bn_v[:], bn_mv[:, :, 1], EPS, None, ALU.add))
                invert(no, bn_v[:], bn_u[:])
                inverse_root(no, bn_v[:], bn_u[:], bn_sc[:])
                chain.link(V.tensor_tensor(bn_sc[:], bn_sc[:], cols[gamma][:], ALU.mult))
                chain.link(V.scalar_tensor_tensor(bn_bi[:], bn_mv[:, :, 0], -1.0, bn_sc[:], ALU.mult, ALU.mult))
                chain.link(V.tensor_tensor(bn_bi[:], bn_bi[:], cols[beta][:], ALU.add))
                dve.sem_inc(S["bn_ready"], 1)

            def leaky(ch):
                dve.wait_ge(S["z_ready"], ch + 1)
                for f in range(FT):
                    last = V.scalar_tensor_tensor(ybuf[:, f, :], ybuf[:, f, :], SLOPE, ybuf[:, f, :], ALU.mult, ALU.max)
                last.then_inc(S["y_ready"], 1)

            def post(layer, ch, next_ch=None):

                def residual(q):
                    t = tile_no(layer, ch, q)
                    x_q, y_q = xr[:, q, :], y_bank(layer, q)[:]
                    if layer < 2:
                        x_q = x_post[:, q, :]
                        dve.wait_ge(S["t1_full"], t + 1 + TPC)
                        dve.wait_ge(s_xin[q], 16 * (LOADS[layer] * NCH + 1) + ch * 16)
                    elif layer == 2:
                        dve.wait_ge(S["y_step"], ch * HT + HT + 4)
                    else:
                        dve.wait_ge(S["dense_full"], ch * FT + (layer - 1) * NCH * FT + q + 1)
                    if layer == 3:
                        dve.wait_ge(S["t2_full"], t + 1)
                        dve.wait_ge(s_xout[q], 16 * (3 * NCH + 1))
                        chain.link(V.tensor_tensor(x_q, y_q, bias_rows[3][:], ALU.add))
                    elif layer == 1:
                        chain.link(V.scalar_tensor_tensor(x_q, x_q, 2.0, y_q, ALU.mult, ALU.add))
                    else:
                        chain.link(V.tensor_tensor(x_q, x_q, y_q, ALU.add))
                    dve.sem_inc(S["t1_free"], 1)
                    chain.mark(V.bn_stats(ln_st[:, q, :], x_q))

                def normed(q):
                    x_q = xr[:, q, :]
                    if layer < 2:
                        t = tile_no(layer, ch, q)
                        dve.wait_ge(S["t2_full"], t + 1)
                        dve.wait_ge(S["split_done"], t + 1)
                        dve.wait_ge(s_xout[q], 16 * (layer * NCH + 1) + 16 * ch)
                    chain.mark(V.tensor_scalar(x_q, x_post[:, q, :] if layer < 2 else x_q, ln_mv[:, q, 0:1],
                                               ln_r[:, q:q + 1], ALU.subtract, ALU.mult))
                    if layer == 3:
                        chain.settle()
                        chain.link(V.tensor_tensor(x_q, x_q, lng_sb[:], ALU.mult))
                        chain.link(V.tensor_tensor(x_q, x_q, lnb_sb[:], ALU.add))
                        chain.mark(V.scalar_tensor_tensor(x_q, x_q, SLOPE, x_q, ALU.mult, ALU.max))
                    chain.settle()
                    dve.sem_inc(S["normed"], 1)
                    if layer < 2:
                        dve.sem_inc(S["normed_ahead"], 1)

                def split(q):
                    nt = bass.ds(ch * TPC + q, 1)
                    x_q = xr[:, q, :]
                    direct = layer == 3 and isinstance(ch, int)
                    if layer == 2 or direct:
                        hi, lo = (part[:, nt, :].rearrange("p a d -> p (a d)") for part in (x_hi, x_lo))
                    elif layer == 3:
                        hi, lo = hl[:, q % HL_RING, 0, :], hl[:, q % HL_RING, 1, :]
                        dve.wait_ge(s_xout[q], 16 * (3 * NCH + 1) + ch * 16)
                        if q < TPC - HL_RING:
                            dve.wait_ge(s_xout[q + HL_RING], 16 * (3 * NCH + 1) + ch * 16)
                        if q >= HL_RING:
                            dve.wait_ge(s_xout[q - HL_RING], 16 * (3 * NCH + 2) + ch * 16)
                    if direct and q == 0:
                        dve.wait_ge(S["agg_full"], 2 * NCH)
                    if layer in (2, 3):
                        chain.link(V.tensor_scalar(hi, x_q, dinv[:, nt], None, ALU.mult))
                        chain.link(V.scalar_tensor_tensor(lo, x_q, dinv[:, nt], hi, ALU.mult, ALU.subtract))
                    dve.sem_inc(S["split_done"], 1)

                if layer in (2, 4):
                    for q in range(TPC):
                        x_q = xr[:, q, :]
                        dve.wait_ge(s_xin[q], 16 * (LOADS[layer] * NCH + 1) + ch * 16)
                        chain.mark(V.scalar_tensor_tensor(x_q, x_q, 2.0 if layer == 2 else 1.0, bias_rows[layer][:],
                                                          ALU.mult, ALU.add))
                    chain.settle()
                for q in range(TPC):
                    residual(q)
                chain.settle()
                dve.sem_inc(S["stats_ready"], 1)
                for q in range(TPC):
                    chain.mark(V.bn_aggr(ln_mv[:, q, :], ln_st[:, q, :]))
                chain.settle()
                chain.link(V.tensor_scalar(ln_v[:], ln_mv[:, :, 1], EPS, None, ALU.add))
                invert(None, ln_v[:], ln_u[:])
                inverse_root(ch + ROOT_LN[layer], ln_v[:], ln_u[:], ln_r[:])
                for q in range(TPC):
                    normed(q)
                if layer == 1 and next_ch is not None:
                    leaky(next_ch)
                if layer > 0:
                    for q in range(TPC):
                        split(q)

            LINKS = {0: 3, 1: 3, 2: 6, 3: 8, 4: 4}
            dve.sem_inc(S["t1_free"], TPC)
            dve.wait_ge(S["ld_par"], 16 * 6)
            batch_norm(ROOT_BN[0], "bn_g", "bn_b", 4 + NCH * FT)
            with chain.loop(NCH, (LINKS[0] + 1) * TPC + 6) as ch:
                post(0, ch)

            for ch in range(NCH):
                dve.wait_ge(S["deg_full"], ch + 1)
                chain.link(V.tensor_scalar(colscale[:, ch * CW:(ch + 1) * CW], pb[TPC + ch][:], 1.0, None, ALU.max))
                dve.sem_inc(S["deg_done"], 1)
            def aggregated(agg_no, dense_no, ch):
                dve.wait_ge(S["agg_full"], ch + agg_no + 1)
                dve.wait_ge(S["dense_full"], ch * FT + dense_no)
                for f in range(FT):
                    V.tensor_tensor(aggT[:, f, :], pb[f][:], colscale[:, ccols(ch)], ALU.mult).then_inc(S["agg_copied"], 1)

            for u in range(2):
                dve.wait_ge(S[f"attr_sent{u}"], 16 * LOT * ((LOTS + 1 - u) // 2))
            chain.link(V.tensor_copy(iota_group16[:], iota[:, 0:P].rearrange("p (a d) -> p a d", d=1).to_broadcast([P, P, GROUP])))
            with chain.loop(NCH, TPC + 1) as ch:
                for t in range(NT):
                    dve.wait_ge(S["at_used"], ch * NT + t + 1)
                    places = dst_keep[:, bass.ds(ch * (NT * ST) + t * ST, ST)].rearrange("p (a b d) -> p a b d", a=GROUPS, b=1)
                    V.tensor_tensor(at_oh[:, t % 2, :, :, :], iota_group16[:].rearrange("p (a b) d -> p a b d", a=1).to_broadcast(
                        [P, GROUPS, P, GROUP]), places.to_broadcast([P, GROUPS, P, GROUP]), ALU.is_equal
                        ).then_inc(S["at_oh_ready"], 1)
                chain.link(V.reciprocal(colscale[:, ccols(ch)], colscale[:, ccols(ch)]))
                aggregated(0, NCH * FT, ch)
                dve.wait_ge(S["at_used"], ch * NT + NT + 2)
                V.tensor_tensor(e2T[:, ccols(ch)], pb[4][:], colscale[:, ccols(ch)], ALU.mult).then_inc(S["e2_done"], 1)
                for q in range(TPC):
                    nt = bass.ds(ch * TPC + q, 1)
                    chain.mark(V.tensor_reduce(deg[:, nt], adj[:, nt, :], AX.X, ALU.add))
            chain.settle()
            batch_norm(ROOT_BN[1], "g1", "be1", 4 + 2 * NCH * FT)
            leaky(0)
            with chain.loop(NCH - 1, (LINKS[1] + 1) * TPC + 6) as ch:
                post(1, ch, ch + 1)
            post(1, NCH - 1)
            dve.wait_ge(S["e2_done"], NCH)
            with dve.If(overfull_dve > 0):
                dve.wait_ge(S["general_attrs_ld"], 16)
                V.tensor_tensor(e2T[:], e2T[:], colscale[:], ALU.mult).then_inc(S["general_attrs_scaled"], 1)
                dve.wait_ge(S["general_attrs_scaled"], 1)
            dve.sem_inc(S["e2_final"], 1)
            chain.mark(V.tensor_scalar(dpos[:], deg[:], 0.0, None, ALU.is_gt))
            chain.link(V.tensor_scalar(deg_v[:], deg[:], 1.0, None, ALU.max))
            invert(ROOT_DEG, deg_v[:], deg_u[:])
            inverse_root(ROOT_DEG, deg_v[:], deg_u[:], dinv[:])
            chain.link(V.tensor_tensor(dinv[:], dinv[:], dpos[:], ALU.mult))

            def diagonals(ch):
                if ch >= DIAG_RING:
                    dve.wait_ge(S["diag_full"], ch - DIAG_RING + 1)
                for q in range(TPC):
                    t = ch * TPC + q
                    last = V.tensor_scalar(diag[:, ch % DIAG_RING, q, :], ident[:], dinv[:, t:t + 1], -1.0, ALU.mult, ALU.mult)
                last.then_inc(S["diag_ready"], 1)

            for ch in range(DIAG_RING):
                diagonals(ch)
            for ch in range(NCH):
                dve.wait_ge(S["diag_full"], ch + 1)
                V.tensor_copy(colscale[:, ch * CW:(ch + 1) * CW], pb[6][:]).then_inc(S["diag_done"], 1)
                if ch + DIAG_RING < NCH:
                    diagonals(ch + DIAG_RING)
            dve.wait_ge(S["diag_done"], NCH)

            dve.wait_ge(S["ld_b2"], 16)
            with chain.loop(NCH, (LINKS[2] + 1) * TPC + 6) as ch:
                post(2, ch)
            dve.wait_ge(S["ld_c1"], 16 * 5)
            for layer, before in ((3, 1), (4, 2)):
                if layer == 4:
                    dve.wait_ge(S["ld_c2_row"], 16)
                with chain.loop(NCH - 1, (LINKS[layer] + 1) * TPC + 6) as ch:
                    aggregated(before * NCH, (before + 1) * NCH * FT, ch)
                    post(layer, ch)
                aggregated(before * NCH, (before + 1) * NCH * FT, NCH - 1)
                post(layer, NCH - 1)

        @block.tensor
        def _(pe):
            mm, tp = nc.tensor.matmul, nc.tensor.transpose
            pieces, ranks, slots = [0], [0], [0]

            def ranks_up_to(limit):
                while ranks[0] < min(limit, EDGE_TILES):
                    c = ranks[0]
                    ranks[0] += 1
                    bank = pb[RANK_BANK + c % 2][:, 0:KEYS]
                    pe.wait_ge(S["key_oh_ready"], c + 1)
                    pe.wait_ge(S["ranked"], c + 1)
                    mm(bank, no_tri[:], key_oh[:, (c + 2) % OH_RING, :], start=(c < 2), stop=True, skip_group_check=True)
                    mm(bank, tri[:], key_oh[:, c % OH_RING, :], start=False, stop=True,
                       skip_group_check=True).then_inc(S["rank_mm"], 1)

            def block_totals():
                pe.wait_ge(S["ranked"], EDGE_TILES + 2)
                for c in range(EDGE_TILES - 2, EDGE_TILES):
                    last = mm(pb[RANK_BANK + c % 2][:, 0:KEYS], no_tri[:], key_oh[:, c % OH_RING, :], start=False, stop=True,
                              skip_group_check=True)
                last.then_inc(S["totals_ready"], 1)

            def piece(products, needs=0):
                n = pieces[0]
                pieces[0] += 1
                if max(n - 3, needs) > 0:
                    pe.wait_ge(S["ortho_free"], max(n - 3, needs))
                products(pb[n % 4]).then_inc(S["ortho_full"], 1)

            def between():
                slots[0] += 1
                if slots[0] > RANKED_BY_PRODUCT:
                    return
                due = LOT + (EDGE_TILES - LOT) * slots[0] // RANKED_BY_PRODUCT
                ranks_up_to(min(due, NORM_AFTER_LOTS * LOT) if pieces[0] <= NORM_PIECE + 1 else due)
                if due == EDGE_TILES:
                    block_totals()

            def transposes(blocks):
                def go(bank):
                    for k, b in enumerate(blocks):
                        between()
                        last = tp(bank[:, k * P:(k + 1) * P], b, ident[:])
                    return last
                return go

            def product(lhs, rhs, i, extra=None, first=0):
                def go(bank):
                    if extra is not None:
                        mm(bank[:, first:], extra[0][:], extra[1][:, i, first:], start=True, stop=False)
                    for k in range(4):
                        between()
                        last = mm(bank[:, first:], lhs[:, k, i * P:(i + 1) * P], rhs[:, k, first:],
                                  start=(k == 0 and extra is None), stop=(k == 3))
                    return last
                return go

            def upper(lhs, rhs, needs=0, extra=None):
                for i in range(4):
                    piece(product(lhs, rhs, i, extra=extra, first=i * P), needs=needs)

            def mirror(m, first_piece):
                for i in range(1, 4):
                    piece(transposes([m[:, k, i * P:(i + 1) * P] for k in range(i)]), needs=first_piece + i)

            def x0_transposes(t):
                piece(transposes([x_stage[:, t % (NT // 2), f * P:(f + 1) * P] for f in range(FT)]))

            pe.wait_ge(S["tri_ready"], 2)
            ranks_up_to(LOT)
            pe.wait_ge(S["ident_ready"], 3)
            pe.wait_ge(S["mats_ready"], 3)
            pe.wait_ge(S["zc_ready"], 4)
            for i in range(4):
                piece(transposes([zc[:, i, k * P:(k + 1) * P] for k in range(4)]))

            def gram(i):
                def go(bank):
                    product(zcT, zcT, i, first=i * P)(bank)
                    return mm(bank[:, i * P:(i + 1) * P], eps_i[:], ident[:], start=False, stop=True, skip_group_check=True)
                return go

            for i in range(4):
                piece(gram(i), needs=4)
            mirror(s_n, 4)
            pe.wait_ge(S["squares_ready"], 4)
            piece(lambda bank: mm(bank[:, 0:4], ones32[:], sq_sum[:], start=True, stop=True), needs=NORM_PIECE)
            ranks_up_to(NORM_AFTER_LOTS * LOT)
            pe.wait_ge(S["s_scaled"], 4)
            n = pieces[0]

            def first_b(i):
                def go(bank):
                    mm(bank[:], mhalf_i[:], s_n[:, i, :], start=True, stop=True)
                    return mm(bank[:, i * P:(i + 1) * P], threehalf_i[:], ident[:], start=False, stop=True, skip_group_check=True)
                return go

            for i in range(4):
                piece(first_b(i))
            pe.wait_ge(S["ld_x"], 16)
            b = [b_ping, b_pong]
            for it in range(4):
                if it == 2:
                    assert pieces[0] == HALF_PIECES
                    pe.wait_ge(S["ld_x"], 32)
                n = pieces[0]
                upper(b[0], b[0], needs=n)
                upper(b[0], s_n)
                mirror(b_sq, n)
                x0_transposes(4 * it)
                x0_transposes(4 * it + 1)
                mirror(b_s, n + 4)
                n = pieces[0]
                x0_transposes(4 * it + 2)
                upper(b_sq, b_s, needs=n, extra=(threehalf_i, b[0]))
                x0_transposes(4 * it + 3)
                mirror(b[1], n + 1)
                b.reverse()
            n = pieces[0]
            for i in range(4):
                piece(product(b[0], zc, i), needs=n)
            assert pieces[0] == ORTHO_PIECES and ranks[0] == EDGE_TILES

            pe.wait_ge(S["overfull_ready"], 1)
            pe.wait_ge(S["ortho_free"], ORTHO_PIECES)

            overfull_pe = pe.value_load(overfull[0:1, 0:1], min_val=0, max_val=1)
            with pe.If(overfull_pe > 0):
                pe.wait_ge(S["g_consts_ready"], 4)
                with pe.Fori(0, STEPS) as i:
                    pe.wait_ge(S["g_out"], i + 1)
                    for bank in pb[0:2]:
                        mm(bank[:], g_zero[:, 0:P], g_zero[:], start=True, stop=True, skip_group_check=True)
                    with pe.Fori(0, PARTS) as part:
                        pe.wait_ge(S["g_oh_ready"], part + i * PARTS + 1)
                        for j in range(PART):
                            mm(pb[0][:], g_src_oh[:, j, :], g_dst_oh[:, j, :], start=False, stop=True, skip_group_check=True)
                            last = mm(pb[1][:], g_src_oh[:, j, :], g_weight_oh[:, j, :], start=False, stop=True,
                                      skip_group_check=True)
                        last.then_inc(S["g_used"], 1)
                with pe.Fori(0, NCH) as ch:
                    pe.wait_ge(S["g_out"], ch + STEPS + 1)
                    mm(pb[2][:], g_zero[:, 0:P], g_zero[:], start=True, stop=True, skip_group_check=True)
                    with pe.Fori(0, PARTS) as part:
                        pe.wait_ge(S["g_attr_ld"], 16 * part + (16 * PARTS) * ch + 16)
                        pe.wait_ge(S["g_oh_ready"], part + ch * PARTS + STEPS * PARTS + 1)
                        for j in range(PART):
                            last = mm(pb[2][:], g_attr[:, j, :], g_dst_oh[:, j, :], start=False, stop=True, skip_group_check=True)
                        last.then_inc(S["g_used"], 1)

            pe.wait_ge(S["ld_self"], 16)
            pe.wait_ge(S["x_split"], 2)

            def aggregate_x0(ch, t):
                pe.wait_ge(S["adj_final"], ch * NT + t + 1)
                for f in range(FT):
                    fs = slice(f * P, (f + 1) * P)
                    mm(pb[f][:], x_hi[:, t, fs], aw[:, t % AW_RING, 0, :], start=(t == 0), stop=False)
                    mm(pb[f][:], x_hi[:, t, fs], aw[:, t % AW_RING, 1, :], start=False, stop=False)
                    last = mm(pb[f][:], x_lo[:, t, fs], aw[:, t % AW_RING, 0, :], start=False, stop=(t == NT - 1))
                last.then_inc(S["agg_step"], 1)

            def dense(bank, pairs, f, copied):
                n = 0
                for w, feat in pairs:
                    if n == FT and f == 0:
                        pe.wait_ge(S["agg_copied"], copied)
                    for k in range(FT):
                        last = mm(bank[:], w[:, k, f * P:(f + 1) * P], feat(k), start=(n == 0), stop=(n == 2 * FT - 1))
                        n += 1
                last.then_inc(S["dense_full"], 1)

            with pe.Fori(0, NCH) as ch:
                pe.wait_ge(S["dense_copied"], ch * FT + 4)
                for t in range(NT):
                    pe.wait_ge(S["aw_low"], ch * NT + t + 1)
                    counts, weights = pb[4 + 2 * (t % 2)], pb[5 + 2 * (t % 2)]
                    for s in range(ST):
                        g = t * GROUPS + s // GROUP
                        if s % GROUP == 0:
                            pe.wait_ge(S["oh_ready"], ch * (NT * GROUPS) + g + 1)
                        rows = oh[:, g % OH_RING, :, :, s % GROUP]
                        block_cols = s // 2 if s < 2 * TPC else t % TPC
                        c = slice(block_cols * P, (block_cols + 1) * P)
                        mm(counts[:, c], rows[:, 0, :], rows[:, 1, :], start=(s == 0), stop=True, skip_group_check=True)
                        for k in range(2):
                            last = mm(weights[:, c], rows[:, 0, :], rows[:, 2 + k, :], start=(s == 0 and k == 0),
                                      stop=True, skip_group_check=True)
                        if s % GROUP == GROUP - 1:
                            last.then_inc(S["oh_used"], 1)
                    if t >= 1:
                        aggregate_x0(ch, t - 1)
                aggregate_x0(ch, NT - 1)
                pe.wait_ge(S["aw_low"], ch * NT + NT + 2)
                for f in range(FT):
                    dense(pb[4 + f], ((self_sb, lambda k: featT[:, k, ccols(ch)]), (t_sb, lambda k: aggT[:, k, :])), f,
                          ch * FT + FT)

            def there(layer, ch, q):
                if q == 0:
                    pe.wait_ge(S["y_ready"], ch + layer * NCH + 1)
                pe.wait_ge(S["t1_free"], bank_free(layer, ch, q))
                for f in range(FT):
                    last = tp(y_bank(layer, q)[:, f * P:(f + 1) * P], ybuf[:, f, q * P:(q + 1) * P], ident[:])
                last.then_inc(S["t1_full"], 1)

            def back(layer, ch, q):
                pe.wait_ge(S["normed"], tile_no(layer, ch, q) + 1)
                pe.wait_ge(S["t2_done"], bank_free(layer, ch, q))
                for f in range(FT):
                    last = tp(t2_bank(layer, q)[:, f * P:(f + 1) * P], xr[:, q, f * P:(f + 1) * P], ident[:])
                last.then_inc(S["t2_full"], 1)

            def posts(layer):
                for q in range(TPC):
                    there(layer, 0, q)
                with pe.Fori(0, NCH - 1) as ch:
                    for step in ((there, back) if layer == 0 else (back, there)):
                        for q in range(TPC):
                            step(layer, ch + 1 if step is there else ch, q)
                for q in range(TPC):
                    back(layer, NCH - 1, q)

            pe.wait_ge(S["dense_copied"], 4 + NCH * FT)
            posts(0)
            pe.wait_ge(S["t2_done"], NT + TPC)
            for ch in range(NCH):
                for t in range(NT):
                    last = mm(pb[TPC + ch][:], ones16[:], adj[:, t, ch * CW:(ch + 1) * CW], start=(t == 0), stop=(t == NT - 1))
                last.then_inc(S["deg_full"], 1)

            def aggregate(ch, copied, between=()):
                pe.wait_ge(S["agg_copied"], ch * FT + copied)
                for t in range(NT):
                    for f in range(FT):
                        mm(pb[f][:], x_hi[:, t, f * P:(f + 1) * P], adj[:, t, ccols(ch)], start=(t == 0), stop=False)
                        last = mm(pb[f][:], x_lo[:, t, f * P:(f + 1) * P], adj[:, t, ccols(ch)], start=False, stop=(t == NT - 1))
                    if t in between:
                        between[t]()
                last.then_inc(S["agg_full"], 1)

            pe.wait_ge(S["deg_done"], NCH)
            pe.wait_ge(S["split_done"], NT + TPC)
            pe.wait_ge(S["ld_l1"], 32)
            with pe.Fori(0, NCH) as ch:
                pe.wait_ge(S["dense_copied"], ch * FT + NCH * FT + 4)

                def aggregate_attributes(t):
                    pe.wait_ge(S["at_split"], ch * NT + t + 1 + AT_RING)
                    pe.wait_ge(S["at_oh_ready"], ch * NT + t + 1)
                    for s in range(ST):
                        block_cols = s // 2 if s < 2 * TPC else t % TPC
                        last = mm(pb[4][:, block_cols * P:(block_cols + 1) * P],
                                  at_parts[:, t % 2, s, :, :].rearrange("p a b -> p (a b)"),
                                  at_oh[:, t % 2, s // GROUP, :, s % GROUP],
                                  start=(t == 0 and s == 0), stop=True, skip_group_check=True)
                    last.then_inc(S["at_used"], 1)

                aggregate(ch, NCH * FT, {t: (lambda t=t: aggregate_attributes(t)) for t in range(NT)})
                for f in range(FT):
                    if f == FT - 1:
                        pe.wait_ge(S["e2_done"], ch + 1)
                    dense(pb[4 + (f + 1) % FT], ((wr_sb, lambda k: featT[:, k, ccols(ch)]), (wl_sb, lambda k: aggT[:, k, :])), f,
                          ch * FT + NCH * FT + FT)
            pe.wait_ge(S["dense_copied"], 4 + 2 * NCH * FT)
            posts(1)

            pe.wait_ge(S["ld_l2"], 16 * 5)
            pe.wait_ge(S["e2_final"], 1)
            pe.wait_ge(S["t2_done"], 2 * NT + TPC)

            def spread_diagonal(ch):
                pe.wait_ge(S["diag_ready"], ch + 1)
                if ch >= 1:
                    pe.wait_ge(S["diag_done"], ch)
                for q in range(TPC):
                    last = mm(pb[6][:, q * P:(q + 1) * P], ones32[:], diag[:, ch % DIAG_RING, q, :],
                              start=(q == 0), stop=True, skip_group_check=True)
                last.then_inc(S["diag_full"], 1)

            def layer2(ch, last_ch):
                def hidden_to_out(i):
                    pe.wait_ge(S["h_ready"], ch * HT + i + 1 + 2)
                    if i == 0:
                        pe.wait_ge(S["t1_free"], tile_no(2, ch) + TPC)
                    for q in range(TPC):
                        last = mm(y_bank(2, q)[:], h_ring[:, i % 4, q * P:(q + 1) * P], w2_sb[:, i, :],
                                  start=(i == 0), stop=(i == HT - 1))
                    last.then_inc(S["y_step"], 1)

                for i in range(HT):
                    pe.wait_ge(S["h_ready"], ch * HT + i + 1)
                    for k in range(FT):
                        mm(pb[4 + i % 2][:], w1_sb[:, k, i * P:(i + 1) * P], featT[:, k, ccols(ch)], start=(k == 0), stop=False)
                    mm(pb[4 + i % 2][:], w1e_sb[:, i * P:(i + 1) * P], e2T[:, ccols(ch)], start=False, stop=True
                       ).then_inc(S["h_full"], 1)
                    if i >= 1:
                        hidden_to_out(i - 1)
                    if last_ch is not None and BACK_AT <= i < BACK_AT + TPC:
                        back(2, last_ch, i - BACK_AT)
                    if last_ch is None and 1 <= i <= NCH:
                        spread_diagonal(i - 1)
                hidden_to_out(HT - 1)

            layer2(0, None)
            with pe.Fori(0, NCH - 1) as last_ch:
                layer2(last_ch + 1, last_ch)
            pe.wait_ge(S["t1_free"], 3 * NT + TPC)
            for layer, w in ((3, c1_sb), (4, c2_sb)):
                if layer == 4:
                    pe.wait_ge(S["hl_loaded"], 32)

                def last_tiles_back(q, layer=layer):
                    back(layer - 1, NCH - 1, q)
                    if q == TPC - 1:
                        pe.wait_ge(S["split_done"], layer * NT + TPC)

                def convolution(ch, last_ch):
                    between = {}
                    for q in range(TPC):
                        if last_ch is None:
                            between[NT - 2 * TPC + q] = lambda q=q: last_tiles_back(q)
                        elif layer == 3:
                            between[NT - 2 * TPC + q] = lambda q=q: back(3, last_ch, q)
                    aggregate(ch, (layer - 1) * NCH * FT, between)
                    if last_ch is None:
                        pe.wait_ge(*((S["ld_c1"], 16 * 5) if layer == 3 else (S["ld_c2"], 16 * 2)))
                    pe.wait_ge(S["x_copied"], ch * FT + (layer - 3) * NCH * FT + FT)
                    for q in range(TPC):
                        pe.wait_ge(S["t1_free"], tile_no(layer, ch, q) - 1 + TPC)
                        nodes = slice(q * P, (q + 1) * P)
                        for k in range(FT):
                            mm(y_bank(layer, q)[:], ybuf[:, k, nodes], w[:, 0, k, :], start=(k == 0), stop=False)
                        if q == 0:
                            pe.wait_ge(S["agg_copied"], ch * FT + (layer - 1) * NCH * FT + FT)
                        for k in range(FT):
                            last = mm(y_bank(layer, q)[:], aggT[:, k, nodes], w[:, 1, k, :], start=False, stop=(k == FT - 1))
                        last.then_inc(S["dense_full"], 1)

                convolution(0, None)
                with pe.Fori(0, NCH - 1) as last_ch:
                    convolution(last_ch + 1, last_ch)


_INS = ['x', 'src', 'dst', 'edge_attr_64', 'edge_weight', 'L0_gnn_weight', 'L0_gnn_self_weight', 'L0_gnn_bn_gamma',
        'L0_gnn_bn_beta', 'L1_gnn_W_l', 'L1_gnn_b_l', 'L1_gnn_W_r', 'L1_gnn_gamma', 'L1_gnn_beta', 'L2_gnn_W1',
        'L2_gnn_b1', 'L2_gnn_W2', 'L2_gnn_b2', 'L3_gnn_W1_0', 'L3_gnn_W1_1', 'L3_gnn_b1', 'L3_gnn_gamma',
        'L3_gnn_beta', 'L3_gnn_W2_0', 'L3_gnn_W2_1', 'L3_gnn_b2']


def kernel(**inputs):
    import numpy as _np
    import concourse.bacc as _bacc
    from concourse import mybir as _mybir
    from concourse.bass_utils import run_bass_kernel_spmd as _run

    nc = _bacc.Bacc("TRN2", target_bir_lowering=False, num_devices=1)
    arrays, args = {}, []
    for name in _INS:
        a = _np.ascontiguousarray(inputs[name])
        arrays[f"in_{name}"] = a
        args.append(nc.dram_tensor(f"in_{name}", a.shape, _mybir.dt.from_np(a.dtype), kind="ExternalInput").ap())
    out = nc.dram_tensor("out_0", (N, D), FP32, kind="ExternalOutput").ap()
    gnn_kernel(nc, *args, out)
    r = _run(nc, [arrays], core_ids=[0])
    return r.results[0]["out_0"]
```
